# Optimizing a Trainium2 kernel written in Bass

```python
import numpy as np
import jax
import jax.numpy as jnp

def _softmax(x, axis=-1):
    return jax.nn.softmax(x, axis=axis)

def _gelu(x):
    return jax.nn.gelu(x, approximate=True)

def _silu(x):
    return jax.nn.silu(x)

def _sigmoid(x):
    return jax.nn.sigmoid(x)

def _layernorm(x, axis=-1, eps=1e-05):
    m = jnp.mean(x, axis=axis, keepdims=True)
    v = jnp.var(x, axis=axis, keepdims=True)
    return (x - m) / jnp.sqrt(v + eps)

def _scatter_add(tgt, idx, src, axis=0):
    return tgt.at[idx].add(src)

def _segment_sum(src, seg, n):
    return jax.ops.segment_sum(src, seg, n)
kernel_name = 'mk_conv_attn_hybrid_d2_conv_nchw256_r4_36733f'

def setup_inputs(seed: int=0):
    np.random.seed(seed)
    _w = jnp.asarray

    def _rec_inputs():
        import jax
        import jax.numpy as jnp
        _gk = jax.random.key(seed)
        x = -0.000125 + 0.9999 * jax.random.normal(jax.random.fold_in(_gk, 1), (32, 64, 16, 16), jnp.float32)
        return x
    x = _rec_inputs()

    def _L0_conv_setup():
        import jax, jax.numpy as jnp
        from jax import lax
        import numpy as np
        K = 3
        PAD = 1
        STRIDE = 1
        key = jax.random.key(seed)
        ks = jax.random.split(key, 6)
        b, c, h, w = (32, 64, 16, 16)
        dim = 64
        x = jax.random.normal(ks[0], (b, c, h, w), dtype=jnp.float32)
        w1 = jax.random.normal(ks[1], (dim * K * K, dim), dtype=jnp.float32) * 0.02
        b1 = jax.random.normal(ks[2], (dim * K * K,), dtype=jnp.float32) * 0.02
        w2 = jax.random.normal(ks[3], (dim * K * K, dim), dtype=jnp.float32) * 0.02
        b2 = jax.random.normal(ks[4], (dim * K * K,), dtype=jnp.float32) * 0.02
        bias = jnp.zeros((dim,), dtype=jnp.float32)
        return {'x': x, 'w1': w1, 'b1': b1, 'w2': w2, 'b2': b2, 'bias': bias}
    _L0_conv_all = _L0_conv_setup()
    _L0_conv_in = {k: v for k, v in _L0_conv_all.items() if k in ('w1', 'b1', 'w2', 'b2', 'bias')}
    del _L0_conv_all

    def _L1_attn_setup():
        import jax, jax.numpy as jnp
        import numpy as np
        N_HASHES = 4
        N_BUCKETS = 8
        NUM_HEADS = 8
        LN_EPS = 1e-05

        def layer_norm(x, g, b):
            m = jnp.mean(x, axis=-1, keepdims=True)
            v = jnp.mean(jnp.square(x - m), axis=-1, keepdims=True)
            return (x - m) * jax.lax.rsqrt(v + LN_EPS) * g + b
        key = jax.random.key(seed)
        ks = jax.random.split(key, 8)
        B, N, C = (16, 2048, 64)
        dff = 4 * C
        w = 0.05
        return {'x': jax.random.normal(ks[0], (B, N, C), jnp.float32), 'rotations': jax.random.normal(ks[1], (1, C, N_HASHES, N_BUCKETS // 2), jnp.float32), 'norm1_g': jnp.ones((C,), jnp.float32), 'norm1_b': jnp.zeros((C,), jnp.float32), 'q_w': jax.random.normal(ks[2], (C, C), jnp.float32) * w, 'kv_w': jax.random.normal(ks[3], (C, 2 * C), jnp.float32) * w, 'norm2_g': jnp.ones((C,), jnp.float32), 'norm2_b': jnp.zeros((C,), jnp.float32), 'fc1_w': jax.random.normal(ks[4], (C, dff), jnp.float32) * w, 'fc1_b': jnp.zeros((dff,), jnp.float32), 'fc2_w': jax.random.normal(ks[5], (dff, C), jnp.float32) * w, 'fc2_b': jnp.zeros((C,), jnp.float32)}
    _L1_attn_all = _L1_attn_setup()
    _L1_attn_in = {k: v for k, v in _L1_attn_all.items() if k in ('rotations', 'norm1_g', 'norm1_b', 'q_w', 'kv_w', 'norm2_g', 'norm2_b', 'fc1_w', 'fc1_b', 'fc2_w', 'fc2_b')}
    del _L1_attn_all

    def _L1_ffn_setup():
        import jax, jax.numpy as jnp
        import numpy as np
        N_EXPERTS = 8
        TOP_K = 2
        key = jax.random.key(seed)
        ks = jax.random.split(key, 5)
        B, T, C, E, H = (8, 512, 64, 8, 682)
        scale = 1.0 / np.sqrt(C)
        return {'x': jax.random.normal(ks[0], (B, T, C), dtype=jnp.float32), 'router_w': jax.random.normal(ks[1], (E, C), dtype=jnp.float32) * scale, 'w1': jax.random.normal(ks[2], (E, H, C), dtype=jnp.float32) * scale, 'w2': jax.random.normal(ks[3], (E, C, H), dtype=jnp.float32) * (1.0 / np.sqrt(H)), 'w3': jax.random.normal(ks[4], (E, H, C), dtype=jnp.float32) * scale}
    _L1_ffn_all = _L1_ffn_setup()
    _L1_ffn_in = {k: v for k, v in _L1_ffn_all.items() if k in ('router_w', 'w1', 'w2', 'w3')}
    del _L1_ffn_all
    return {'x': x, 'L0_conv_w1': _L0_conv_in['w1'], 'L0_conv_b1': _L0_conv_in['b1'], 'L0_conv_w2': _L0_conv_in['w2'], 'L0_conv_b2': _L0_conv_in['b2'], 'L0_conv_bias': _L0_conv_in['bias'], 'L1_attn_rotations': _L1_attn_in['rotations'], 'L1_attn_norm1_g': _L1_attn_in['norm1_g'], 'L1_attn_norm1_b': _L1_attn_in['norm1_b'], 'L1_attn_q_w': _L1_attn_in['q_w'], 'L1_attn_kv_w': _L1_attn_in['kv_w'], 'L1_attn_norm2_g': _L1_attn_in['norm2_g'], 'L1_attn_norm2_b': _L1_attn_in['norm2_b'], 'L1_attn_fc1_w': _L1_attn_in['fc1_w'], 'L1_attn_fc1_b': _L1_attn_in['fc1_b'], 'L1_attn_fc2_w': _L1_attn_in['fc2_w'], 'L1_attn_fc2_b': _L1_attn_in['fc2_b'], 'L1_ffn_router_w': _L1_ffn_in['router_w'], 'L1_ffn_w1': _L1_ffn_in['w1'], 'L1_ffn_w2': _L1_ffn_in['w2'], 'L1_ffn_w3': _L1_ffn_in['w3']}

def reference(x, L0_conv_w1, L0_conv_b1, L0_conv_w2, L0_conv_b2, L0_conv_bias, L1_attn_rotations, L1_attn_norm1_g, L1_attn_norm1_b, L1_attn_q_w, L1_attn_kv_w, L1_attn_norm2_g, L1_attn_norm2_b, L1_attn_fc1_w, L1_attn_fc1_b, L1_attn_fc2_w, L1_attn_fc2_b, L1_ffn_router_w, L1_ffn_w1, L1_ffn_w2, L1_ffn_w3):
    import jax
    import jax.numpy as jnp

    def _L0_conv_ref(x, w1, b1, w2, b2, bias):
        import jax, jax.numpy as jnp
        from jax import lax
        import numpy as np
        K = 3
        PAD = 1
        STRIDE = 1
        b, c, h, w = x.shape
        avg = jnp.mean(x, axis=(2, 3))
        mx = jnp.max(x, axis=(2, 3))
        a = avg @ w1.T + b1
        m = mx @ w2.T + b2
        wt = (m - a).reshape(b * c, 1, K, K)
        wt = jax.nn.softmax(wt, axis=1)
        xr = x.reshape(1, b * c, h, w)
        y = lax.conv_general_dilated(xr, wt, window_strides=(STRIDE, STRIDE), padding=((PAD, PAD), (PAD, PAD)), feature_group_count=b * c, dimension_numbers=('NCHW', 'OIHW', 'NCHW'))
        y = y + jnp.tile(bias, b)[None, :, None, None]
        y = y.reshape(b, c, h, w)
        return y + x

    def _L1_attn_ref(x, rotations, norm1_g, norm1_b, q_w, kv_w, norm2_g, norm2_b, fc1_w, fc1_b, fc2_w, fc2_b):
        import jax, jax.numpy as jnp
        import numpy as np
        N_HASHES = 4
        N_BUCKETS = 8
        NUM_HEADS = 8
        LN_EPS = 1e-05

        def layer_norm(x, g, b):
            m = jnp.mean(x, axis=-1, keepdims=True)
            v = jnp.mean(jnp.square(x - m), axis=-1, keepdims=True)
            return (x - m) * jax.lax.rsqrt(v + LN_EPS) * g + b
        B, N, C = x.shape
        H = NUM_HEADS
        Dh = C // H
        scale = Dh ** (-0.5)
        x_ = layer_norm(x, norm1_g, norm1_b)
        q = (x_ @ q_w).reshape(B, N, H, Dh).transpose(0, 2, 1, 3)
        rotated = jnp.einsum('btf,fhi->bhti', x_, rotations[0])
        rotated = jnp.concatenate([rotated, -rotated], axis=-1)
        buckets = jnp.argmax(rotated, axis=-1)
        one_hot = jax.nn.one_hot(buckets, N_BUCKETS, dtype=x.dtype)
        sum_buckets = jnp.sum(one_hot, axis=2)
        pooled = jnp.einsum('bnf,bhni->bhif', x_, one_hot)
        pooled = pooled / (jax.lax.stop_gradient(sum_buckets)[..., None] + 1e-20)
        rp_x = pooled.reshape(B, N_HASHES * N_BUCKETS, C)
        sumb = jax.lax.stop_gradient(sum_buckets.reshape(B, N_HASHES * N_BUCKETS))
        M = N_HASHES * N_BUCKETS
        kv = (rp_x @ kv_w).reshape(B, M, 2, H, Dh).transpose(2, 0, 3, 1, 4)
        k, v = (kv[0], kv[1])
        attn = jnp.einsum('bhnd,bhmd->bhnm', q, k) * scale
        mask = (sumb >= 1)[:, None, None, :]
        attn = jnp.where(mask, attn, -jnp.finfo(attn.dtype).max)
        attn = jax.nn.softmax(attn, axis=-1)
        out = jnp.einsum('bhnm,bhmd->bnhd', attn, v).reshape(B, N, C)
        x = x + out
        y = layer_norm(x, norm2_g, norm2_b)
        h = jax.nn.gelu(y @ fc1_w + fc1_b, approximate=False)
        y = h @ fc2_w + fc2_b
        return x + y

    def _L1_ffn_ref(x, router_w, w1, w2, w3):
        import jax, jax.numpy as jnp
        import numpy as np
        N_EXPERTS = 8
        TOP_K = 2
        B, T, C = x.shape
        flat = x.reshape(-1, C)
        logits = flat @ router_w.T
        probs = jax.nn.softmax(logits, axis=-1)
        topk_probs, topk_idx = jax.lax.top_k(probs, TOP_K)
        topk_probs = topk_probs / (jnp.sum(topk_probs, axis=-1, keepdims=True) + 1e-09)
        onehot = jax.nn.one_hot(topk_idx, N_EXPERTS, dtype=flat.dtype)
        gates = jnp.einsum('nk,nke->ne', topk_probs, onehot)
        h1 = jnp.einsum('nc,ehc->neh', flat, w1)
        h3 = jnp.einsum('nc,ehc->neh', flat, w3)
        h = jax.nn.silu(h1) * h3
        y = jnp.einsum('neh,ech->nec', h, w2)
        out = jnp.einsum('ne,nec->nc', gates, y)
        return out.reshape(B, T, C)

    def _gn(v, G=32, eps=1e-05):
        B_, C_, H_, W_ = v.shape
        g = v.reshape(B_, G, C_ // G, H_, W_)
        m = jnp.mean(g, axis=(2, 3, 4), keepdims=True)
        s = jnp.var(g, axis=(2, 3, 4), keepdims=True)
        return ((g - m) / jnp.sqrt(s + eps)).reshape(v.shape)

    def _ln_c(v, eps=1e-06):
        m = jnp.mean(v, axis=1, keepdims=True)
        s = jnp.var(v, axis=1, keepdims=True)
        return (v - m) / jnp.sqrt(s + eps)

    def _ln_t(v, eps=1e-05):
        m = jnp.mean(v, axis=-1, keepdims=True)
        s = jnp.var(v, axis=-1, keepdims=True)
        return (v - m) / jnp.sqrt(s + eps)

    def _to_tokens(v):
        B_, C_, H_, W_ = v.shape
        return v.reshape(B_, C_, H_ * W_).transpose(0, 2, 1)

    def _from_tokens(t, like):
        B_, C_, H_, W_ = like.shape
        return t.transpose(0, 2, 1).reshape(B_, C_, H_, W_)
    x = x + _L0_conv_ref(_gn(x), L0_conv_w1, L0_conv_b1, L0_conv_w2, L0_conv_b2, L0_conv_bias)
    t = _to_tokens(x)
    t = t + _L1_attn_ref(_ln_t(t), L1_attn_rotations, L1_attn_norm1_g, L1_attn_norm1_b, L1_attn_q_w, L1_attn_kv_w, L1_attn_norm2_g, L1_attn_norm2_b, L1_attn_fc1_w, L1_attn_fc1_b, L1_attn_fc2_w, L1_attn_fc2_b)
    t = t + _L1_ffn_ref(_ln_t(t), L1_ffn_router_w, L1_ffn_w1, L1_ffn_w2, L1_ffn_w3)
    x = _from_tokens(t, x)
    return x

_drawn_inputs = setup_inputs


def setup_inputs(seed=0):
    import zlib

    import numpy as np

    out = dict(_drawn_inputs(seed))
    spreads = {'L0_conv_bias': (0.0, 0.294),
     'L1_attn_norm1_g': (1.0, 0.6),
     'L1_attn_norm1_b': (0.0, 0.719),
     'L1_attn_norm2_g': (1.0, 0.6),
     'L1_attn_norm2_b': (0.0, 0.8),
     'L1_attn_fc1_b': (0.0, 0.671),
     'L1_attn_fc2_b': (0.0, 0.366)}
    factors = {'L1_attn_rotations': 8.0, 'L1_attn_q_w': 8.0, 'L1_attn_kv_w': 3.658}
    for name, (base, spread) in spreads.items():
        noise = np.random.default_rng([zlib.crc32(name.encode()), seed]).standard_normal(out[name].shape)
        drawn = base * np.exp(spread * noise) if base else spread * noise
        out[name] = jnp.asarray(drawn.astype(out[name].dtype))
    for name, factor in factors.items():
        out[name] = (out[name] * factor).astype(out[name].dtype)
    return out
```

```python
from contextlib import ExitStack

import concourse.bass as bass
from concourse import mybir
from concourse.bass import ds

P = 128
B, C, HH, WW = 32, 64, 16, 16
N = HH * WW
T = B * N
GB = 4
NG = B // GB
GT = GB * N
NJ = GT // P
HASHES, BUCKETS = 4, 8
M = HASHES * BUCKETS
HEADS = 8
DH = C // HEADS
DFF = 4 * C
NE = 8
HID = 682
CF = 5
CR = HID - CF * P
CH = CF + 1
MT = 256
REG = T + MT
NT = (2 * T + NE * (MT - 1)) // MT
NS = NT + 1
ROW = C + 2
DUMP = 2 * T
XS = 2048.0
EPS = 1e-5
TINY = 1e-30
EXP_MASK = 0x7F800000
SCALE_EXP = 127 + 13 + 127
BACK_EXP = 13 + 11
MASKED = -1e30

ALU = mybir.AluOpType
ACT = mybir.ActivationFunctionType
F32 = mybir.dt.float32
F16 = mybir.dt.float16
U32 = mybir.dt.uint32
I32 = mybir.dt.int32
AX = mybir.AxisListType


def hybrid_block(nc, x, conv_bias, rotations, norm1_g, norm1_b, q_w, kv_w, norm2_g, norm2_b,
                 fc1_w, fc1_b, fc2_w, fc2_b, router_w, w1, w2, w3, out):
    with ExitStack() as ctx:
        def sb(name, shape, dt=F32):
            return ctx.enter_context(nc.sbuf_tensor(name, shape, dt))

        def sem(name):
            return ctx.enter_context(nc.semaphore(name))

        rows = nc.dram_tensor("expert_rows", (NE * REG + MT, ROW), F32).ap()
        results = nc.dram_tensor("expert_results", (DUMP, C), F32).ap()

        ident = sb("ident", [P, P])
        ident16 = sb("ident16", [P, P], F16)
        pair_mean = sb("pair_mean", [P, P])
        before = sb("before", [P, P])
        ones = sb("ones", [P, P])
        descend = sb("descend", [P, BUCKETS])
        head_of = sb("head_of", [C + 1, HEADS])
        v_mask = sb("v_mask", [P, 2, C])
        v_heads = sb("v_heads", [P, 2, HEADS])
        region = sb("region", [P, NE, NJ])
        scan_keep = sb("scan_keep", [P, NE, NJ + 1])
        c_mhalf = sb("c_mhalf", [P, NJ])
        c_64th = sb("c_64th", [P, NJ])
        c_eps = sb("c_eps", [P, NJ])
        c_group = sb("c_group", [P, 2, NJ])
        bias2 = sb("bias2", [P, 1])
        g1 = sb("g1", [C, 1])
        g2 = sb("g2", [C, 1])
        b2c = sb("b2c", [C, 1])
        fc1_bias0 = sb("fc1_bias0", [P, 2])
        fc1_bias = sb("fc1_bias", [P, 2])
        diag_g1 = sb("diag_g1", [C, C + 1])
        proj = sb("proj", [C, C + M + 2 * C])
        q_aug = sb("q_aug", [C + 1, C + 1])
        rot_aug = sb("rot_aug", [C + 1, M])
        k_aug = sb("k_aug", [C + 2, C + 1])
        v_aug = sb("v_aug", [C + 1, C])
        fc1_n = sb("fc1_n", [C, DFF])
        fc1_s = sb("fc1_s", [C, DFF])
        fc2_s = sb("fc2_s", [P, 2, C])
        fc2_row = sb("fc2_row", [1, NJ, C])
        router_n = sb("router_n", [NE, C])
        router_t = sb("router_t", [C, NE])
        wn = sb("wn", [P, 2, CH, C])
        w2n = sb("w2n", [C, CH * P])
        w_hi = sb("w_hi", [P, 2, CH, C], F16)
        w_lo = sb("w_lo", [P, 2, CH, C], F16)
        w13 = sb("w13", [P, NE, 2, CH, 2, P], F16)
        w2s = sb("w2s", [P, NE, CH, C])
        wmax = sb("wmax", [P, 2])
        wmax_all = sb("wmax_all", [P, 2])
        wexp = sb("wexp", [P, 2], U32)
        wscale = sb("wscale", [P, 2], U32)
        wback = sb("wback", [P, NE, 2], U32)
        xg = sb("xg", [P, 2, HH, WW])
        xpad = sb("xpad", [P, 2, HH + 2, WW + 2])
        hsum = sb("hsum", [P, 2, HH + 2, WW])
        xres = sb("xres", [P, 2, HH, WW])
        bst = sb("bst", [P, 2, 6])
        mv = sb("mv", [P, 2, 2])
        dmean = sb("dmean", [P, 2])
        dmean2 = sb("dmean2", [P, 2])
        chvar = sb("chvar", [P, 2])
        gmean = sb("gmean", [P, 2])
        gvar = sb("gvar", [P, 2])
        grstd = sb("grstd", [P, 2])
        tok = sb("tok", [P, NJ, C])
        ssum = sb("ssum", [P, NJ])
        cent = sb("cent", [P, NJ, C])
        sq = sb("sq", [P, NJ, C])
        ssq = sb("ssq", [P, NJ])
        vare = sb("vare", [P, NJ])
        r1 = sb("r1", [P, NJ])
        r1sq = sb("r1sq", [P, NJ])
        v64 = sb("v64", [P, NJ])
        uvar = sb("uvar", [P, NJ])
        uvare = sb("uvare", [P, NJ])
        r2 = sb("r2", [P, NJ])
        r12 = sb("r12", [P, NJ])
        u = sb("u", [P, NJ, C])
        n1 = sb("n1", [P, NJ, C + 1])
        res = sb("res", [P, 2, 2, NJ, C])
        n1t = res[0:C + 1, 0, :, :, :].rearrange("p k j c -> p (k j c)")
        qt = res[0:C + 1, 1, :, :, :].rearrange("p k j c -> p (k j c)")
        bmax = sb("bmax", [P, NJ * HASHES])
        beq = sb("beq", [P, NJ * HASHES, BUCKETS])
        bfirst = sb("bfirst", [P, NJ * HASHES])
        onehot = sb("onehot", [P, NJ * HASHES, BUCKETS])
        cnt = sb("cnt", [P, 1])
        rcnt = sb("rcnt", [P, 1])
        pooled = sb("pooled", [P, C + 2])
        pooled_t = sb("pooled_t", [C + 2, P])
        pooled_rep = sb("pooled_rep", [C + 1, GB, 4, M])
        kblk = sb("kblk", [C + 1, GB, HEADS, M])
        vblk = sb("vblk", [P, GB, 2, C + HEADS])
        smax = sb("smax", [P, 2, 2 * HEADS])
        ssub = sb("ssub", [P, 2, 2 * HEADS, M])
        prob = sb("prob", [P, 2, 4, P])
        prob_t = sb("prob_t", [P, 2, 4, P])
        rden = sb("rden", [P, 2, 4, HEADS])
        att = sb("att", [P, 2, 4, C])
        x2 = sb("x2", [P, NJ, C])
        x2t = sb("x2t", [P, NJ, C])
        n2 = sb("n2", [P, NJ, C])
        hbuf = sb("hbuf", [P, 2, CH, MT])
        hid = hbuf[:, :, :, :].rearrange("p b k n -> p (b k n)")[:, 0:2 * GT].rearrange("p (a n) -> p a n", a=2)
        t3 = sb("t3", [P, 2, NJ, C])
        og = sb("og", [P, 2, 2 * N])
        n2t = t3[0:C, :, :, :].rearrange("p b j c -> p (b j c)")
        wtok_t = og[0:C, :, :].rearrange("p b n -> p (b n)")
        t2 = sb("t2", [P, NJ, C])
        t2_all = sb("t2_all", [P, NG, NJ, C])
        wtok = sb("wtok", [P, NJ, C])
        lmax = sb("lmax", [P, NJ])
        lsub = sb("lsub", [P, NJ, NE])
        lexp = sb("lexp", [P, NJ, NE])
        lden = sb("lden", [P, NJ])
        lrec = sb("lrec", [P, NJ])
        pr = sb("pr", [P, NJ, NE])
        pk = sb("pk", [P, 2, NJ])
        peq = sb("peq", [P, NJ, NE])
        pfirst = sb("pfirst", [P, NJ])
        oh = sb("oh", [P, 2, NJ, NE])
        prest = sb("prest", [P, NJ, NE])
        gsum = sb("gsum", [P, NJ])
        grec = sb("grec", [P, NJ])
        picked = sb("picked", [P, NE, NJ + 1])
        passed = sb("passed", [P, NE, NJ + 1])
        posall = sb("posall", [P, NE, NJ])
        posk = sb("posk", [P, 2, NE, NJ])
        posf = sb("posf", [P, 2, NJ])
        pos = sb("pos", [P, 2, NJ], U32)
        srow = sb("srow", [P, 2, NJ, ROW])

        cnt8 = sb("cnt8", [1, NE])
        k_rows = sb("k_rows", [1, T // MT])
        over = sb("over", [1, NE, T // MT])
        tiles = sb("tiles", [1, NE])
        tiles_end = sb("tiles_end", [1, NE])
        adjust = sb("adjust", [1, NE])
        g_no = sb("g_no", [1, NS])
        g_row = sb("g_row", [1, NS])
        past = sb("past", [1, NS, NE])
        past_a = sb("past_a", [1, NS, NE])
        n_past = sb("n_past", [1, NS])
        a_past = sb("a_past", [1, NS])
        tile_expert = sb("tile_expert", [1, NS], U32)
        tile_row = sb("tile_row", [1, NS], U32)
        pad_row = sb("pad_row", [1, NE], U32)
        pad = sb("pad", [P, 2, ROW])
        xin = sb("xin", [P, 2, 2, ROW])
        xs = sb("xs", [P, 2, MT], F16)
        route = sb("route", [P, 2, 2, 2])
        dest = sb("dest", [P, 2, 2], U32)
        silu = sb("silu", [P, 2, 2 * MT])
        yout = sb("yout", [P, 2, 2, C])

        def ps(name, shape, dt=F32):
            return ctx.enter_context(nc.psum_tensor(name, shape, dt))

        bk0 = ps("bk0", [P, 512])
        bk12 = ps("bk12", [P, 2, 512])
        bk34 = ps("bk34", [P, 2, 512])
        bk56 = ps("bk56", [P, 2, 512])
        bk7 = ps("bk7", [P, 512])

        t_ps = bk0[:, :]
        k_ps = bk0[0:C + 1, 0:P]
        v_ps = bk0[:, 256:512].rearrange("p (b c) -> p b c", b=GB)
        y_ps = bk0[:, :].rearrange("p (j c) -> p j c", j=NJ)
        rot_ps = bk7[:, 0:256]
        pool_ps = bk7[:, 256:256 + C + 1]
        poolt_ps = bk7[0:C + 2, 384:512]
        gmean_ps = bk7[:, 0:2]
        gvar_ps = bk7[:, 8:10]
        l_ps = bk7[:, 0:NJ * NE].rearrange("p (j e) -> p j e", j=NJ)
        pos_ps = bk7[:, 128:128 + NE * NJ].rearrange("p (e j) -> p e j", e=NE)
        w13_q = w13[:, :, :, :, :, :].rearrange("p e t k a n -> p e (t k a) n")
        w_dst16 = [bk34[:, 0, :].bitcast(F16), bk34[:, 1, :].bitcast(F16), bk56[:, 0, :].bitcast(F16)]
        av_ps = [bk[:, 0:4 * (C + HEADS)].rearrange("p (j c) -> p j c", j=4) for bk in (bk0, bk7)]

        waited = sem("waited")
        small_loaded = sem("small_loaded")
        experts_loaded = sem("experts_loaded")
        w2_loaded = sem("w2_loaded")
        sched_ready = sem("sched_ready")
        counted = sem("counted")
        pads_written = sem("pads_written")
        xin_loaded = [sem(f"xin_loaded{b}") for b in range(2)]
        xt_turned = sem("xt_turned")
        xs_ready = sem("xs_ready")
        h1_ready = sem("h1_ready")
        h3_ready = sem("h3_ready")
        silu_ready = sem("silu_ready")
        h_ready = sem("h_ready")
        e_y_ready = sem("e_y_ready")
        route_ready = sem("route_ready")
        yout_ready = [sem(f"yout_ready{b}") for b in range(2)]
        y_scattered = [sem(f"y_scattered{b}") for b in range(2)]
        res_loaded = [sem(f"res_loaded{b}") for b in range(2)]
        t3_ready = sem("t3_ready")
        t3_sum = sem("t3_sum")
        sched_step = sem("sched_step")
        o_turned = [sem(f"o_turned{b}") for b in range(2)]
        og_ready = [sem(f"og_ready{b}") for b in range(2)]
        out_stored = [sem(f"out_stored{b}") for b in range(2)]
        consts_step = sem("consts_step")
        consts_ready = sem("consts_ready")
        pe_setup = sem("pe_setup")
        dve_setup = sem("dve_setup")
        w_max_ready = sem("w_max_ready")
        w_scale_ready = sem("w_scale_ready")
        w_max_all = sem("w_max_all")
        w_hi_ready = sem("w_hi_ready")
        w_parts_ready = sem("w_parts_ready")
        w_turned = sem("w_turned")
        w_stored_act = sem("w_stored_act")
        w_stored_dve = sem("w_stored_dve")
        x_loaded = sem("x_loaded")
        x_used = sem("x_used")
        dve_step = sem("dve_step")
        mean_ready = sem("mean_ready")
        gmean_ready = sem("gmean_ready")
        chvar_ready = sem("chvar_ready")
        gvar_done = sem("gvar_done")
        gvar_ready = sem("gvar_ready")
        grstd_ready = sem("grstd_ready")
        conv_ready = sem("conv_ready")
        t_ready = sem("t_ready")
        tok_ready = sem("tok_ready")
        cent_ready = sem("cent_ready")
        sq_ready = sem("sq_ready")
        vare_ready = sem("vare_ready")
        pool_step = sem("pool_step")
        r_ready = sem("r_ready")
        n_ready = sem("n_ready")
        nt_turned = sem("nt_turned")
        nt_act = sem("nt_act")
        nt_dve = sem("nt_dve")
        rot_ready = sem("rot_ready")
        q_ready = sem("q_ready")
        qt_ready = sem("qt_ready")
        onehot_ready = sem("onehot_ready")
        pool_ready = sem("pool_ready")
        pooled_ready = sem("pooled_ready")
        poolt_ready = sem("poolt_ready")
        pooledt_ready = sem("pooledt_ready")
        rep_ready = sem("rep_ready")
        kv_ready = sem("kv_ready")
        blk_ready = sem("blk_ready")
        s_ready = sem("s_ready")
        ssub_ready = sem("ssub_ready")
        prob_ready = sem("prob_ready")
        probt_turned = sem("probt_turned")
        probt_ready = sem("probt_ready")
        av_ready = sem("av_ready")
        x2t_ready = sem("x2t_ready")
        x2_ready = sem("x2_ready")
        fc1_ready = sem("fc1_ready")
        hid_ready = sem("hid_ready")
        y_ready = sem("y_ready")
        router_ready = sem("router_ready")
        lsub_ready = sem("lsub_ready")
        lexp_ready = sem("lexp_ready")
        picked_ready = sem("picked_ready")
        passed_ready = sem("passed_ready")
        pos_ready = sem("pos_ready")
        pos_counted = sem("pos_counted")
        wtok_ready = sem("wtok_ready")
        whi_ready = sem("whi_ready")
        dst_ready = sem("dst_ready")
        srow_ready = sem("srow_ready")
        srow2_ready = sem("srow2_ready")
        scattered = sem("scattered")

        x_rows = x.rearrange("b c h w -> (b c) (h w)")
        x_groups = x_rows.rearrange("(g s p) n -> g p s n", g=NG, s=2)

        block = ctx.enter_context(nc.Block())

        NSMALL = 18

        @block.sync
        def _(sp):
            flat = xg[:, :, :, :].rearrange("p s h w -> p s (h w)")
            sp.dma_start(bias2[0:C, :], conv_bias.rearrange("(c o) -> c o", o=1)).then_inc(small_loaded, 16)
            sp.dma_start(bias2[C:P, :], conv_bias.rearrange("(c o) -> c o", o=1)).then_inc(small_loaded, 16)
            sp.dma_start(g1[:, :], norm1_g.rearrange("(c o) -> c o", o=1)).then_inc(small_loaded, 16)
            sp.dma_start(diag_g1[:, C:C + 1], norm1_b.rearrange("(c o) -> c o", o=1)).then_inc(small_loaded, 16)
            sp.dma_start(g2[:, :], norm2_g.rearrange("(c o) -> c o", o=1)).then_inc(small_loaded, 16)
            sp.dma_start(b2c[:, :], norm2_b.rearrange("(c o) -> c o", o=1)).then_inc(small_loaded, 16)
            sp.dma_start(proj[:, 0:C], q_w).then_inc(small_loaded, 16)
            rot_dst = proj[:, C:C + M].rearrange("c (h n) -> c h n", h=HASHES)
            sp.dma_start(rot_dst[:, :, 0:BUCKETS // 2], rotations.rearrange("o c h n -> (o c) h n")).then_inc(small_loaded, 16)
            sp.dma_start(proj[:, C + M:], kv_w).then_inc(small_loaded, 16)
            sp.dma_start(fc1_n[:, :], fc1_w).then_inc(small_loaded, 16)
            for a in range(2):
                sp.dma_start(fc1_bias0[:, a:a + 1], fc1_b[a * P:(a + 1) * P].rearrange("(p o) -> p o", o=1))\
                    .then_inc(small_loaded, 16)
            sp.dma_start(fc2_s[:, :, :], fc2_w.rearrange("(a p) c -> p a c", a=2)).then_inc(small_loaded, 16)
            sp.dma_start(router_n[:, :], router_w).then_inc(small_loaded, 16)
            fc2_b_row = fc2_b.rearrange("(o c) -> o c", o=1)
            sp.dma_start(fc2_row[:, 0, :], fc2_b_row).then_inc(small_loaded, 16)
            for j in (1, 2, 3):
                sp.dma_start(fc2_row[:, j, :], fc2_b_row).then_inc(small_loaded, 16)
            sp.wait_ge(consts_ready, 2)
            with sp.Fori(0, NG) as i:
                sp.wait_ge(x_used, i)
                sp.dma_start(flat, x_groups[ds(i, 1)].rearrange("g p s n -> (g p) s n")).then_inc(x_loaded, 16)
                sp.wait_ge(w_parts_ready, i)
                for t, w in enumerate((w1, w3)):
                    we = w[ds(i, 1)].rearrange("e h c -> (e h) c")
                    sp.dma_start(wn[:, t, 0:CF, :], we[0:CF * P, :].rearrange("(p k) c -> p k c", k=CF))\
                        .then_inc(experts_loaded, 16)
                    sp.dma_start(wn[0:CR, t, CF, :], we[CF * P:HID, :]).then_inc(experts_loaded, 16)
                sp.wait_ge(w_turned, 2 * i)
                w2e = w2[ds(i, 1)].rearrange("e c h -> (e c) h")
                sp.dma_start(w2n[:, 0:HID], w2e).then_inc(w2_loaded, 16)
            sp.wait_ge(sched_ready, 1)
            sp.wait_ge(scattered, NG * 2 * NJ * 16)

            def write_pad(row):
                sp.dma_start(rows[ds(row, MT), :].rearrange("(h p) w -> p h w", h=2), pad[:, :, :])\
                    .then_inc(pads_written, 16)

            write_pad(NE * REG)
            for e in range(NE):
                write_pad(sp.value_load(pad_row[0:1, e:e + 1], min_val=0, max_val=NE * REG - MT))
            sp.wait_ge(pads_written, 16 * (NE + 1))

            def load(t, b):
                row = sp.value_load(tile_row[0:1, ds(t, 1)], min_val=0, max_val=NE * REG)
                sp.dma_start(xin[:, b, :, :], rows[ds(row, MT), :].rearrange("(h p) w -> p h w", h=2))\
                    .then_inc(xin_loaded[b], 16)

            load(0, 0)
            load(1, 1)
            with sp.Fori(0, (NT - 1) // 2) as k:
                for b in range(2):
                    sp.wait_ge(xt_turned, 2 * k + b + 1)
                    sp.wait_ge(route_ready, 2 * k + b + 1)
                    load(2 * k + b + 2, b)

            sp.wait_ge(y_scattered[0], 32 * ((NT + 1) // 2))
            sp.wait_ge(y_scattered[1], 32 * (NT // 2))
            res_v = results.rearrange("(k i s b f p) c -> i k s p f b c", k=2, i=NG, s=2, b=2, p=P)

            def load_results(i, b):
                for k in range(2):
                    for s in range(2):
                        for f in range(2):
                            src = res_v[ds(i, 1), k, s, :, f].rearrange("i p b c -> (i p) b c")
                            sp.dma_start(res[:, b, k, 4 * s + 2 * f:4 * s + 2 * f + 2, :], src)\
                                .then_inc(res_loaded[b], 16)

            load_results(0, 0)
            load_results(1, 1)
            with sp.Fori(0, NG // 2 - 1) as k:
                for b in range(2):
                    sp.wait_ge(t3_ready, 2 * k + b + 1)
                    load_results(2 * k + b + 2, b)

        @block.gpsimd
        def _(pool):
            step = [0]

            def then(ins):
                step[0] += 1
                ins.then_inc(consts_step, 1)
                pool.wait_ge(consts_step, step[0])

            g = nc.gpsimd
            g.memset(ones[:, :], 1.0).then_inc(consts_ready, 1)
            g.memset(ident[:, :], 0.0)
            g.memset(ident16[:, :], 0.0)
            g.memset(diag_g1[:, 0:C], 0.0)
            g.memset(pair_mean[:, :], 0.5)
            g.memset(before[:, :], 1.0)
            g.memset(head_of[:, :], 1.0)
            g.memset(v_mask[:, :, :], 1.0)
            g.memset(v_heads[:, :, :], 1.0)
            g.memset(scan_keep[:, :, :], 1.0)
            g.memset(q_aug[:, :], 0.0)
            g.memset(k_aug[:, :], 0.0)
            g.memset(c_mhalf[:, :], -0.5)
            g.memset(c_64th[:, :], 1.0 / C)
            g.memset(c_eps[:, :], EPS)
            g.memset(c_group[:, :, :], float(GT))
            g.memset(xpad[:, :, :, :], 0.0)
            g.memset(hsum[:, :, :, :], 0.0)
            g.memset(n1[:, :, C:C + 1], 1.0)
            then(g.memset(picked[:, :, 0:1], 0.0))
            for m in (ident, ident16):
                g.affine_select(out=m[:, :], in_=m[:, :], compare_op=ALU.not_equal, fill=1.0, base=0,
                                pattern=[[-1, P]], channel_multiplier=1)
            pm = pair_mean[:, :].rearrange("p (a b) -> p a b", b=2)
            then(g.affine_select(out=pm, in_=pm, compare_op=ALU.is_ge, fill=0.0, base=0,
                                 pattern=[[-2, C], [0, 2]], channel_multiplier=1))
            g.affine_select(out=pm, in_=pm, compare_op=ALU.is_ge, fill=0.0, base=1,
                            pattern=[[2, C], [0, 2]], channel_multiplier=-1)
            g.affine_select(out=before[:, :], in_=before[:, :], compare_op=ALU.is_gt, fill=0.0, base=0,
                            pattern=[[1, P]], channel_multiplier=-1)
            hc = head_of[0:C, :]
            g.affine_select(out=hc, in_=hc, compare_op=ALU.is_ge, fill=0.0, base=0,
                            pattern=[[-DH, HEADS]], channel_multiplier=1)
            vm = v_mask[:, :, :].rearrange("p a (h d) -> p a h d", h=HEADS)
            g.affine_select(out=vm, in_=vm, compare_op=ALU.is_ge, fill=0.0, base=0,
                            pattern=[[P, 2], [-M, HEADS], [0, DH]], channel_multiplier=1)
            then(g.affine_select(out=v_heads[:, :, :], in_=v_heads[:, :, :], compare_op=ALU.is_ge, fill=0.0,
                                 base=0, pattern=[[P, 2], [-M, HEADS]], channel_multiplier=1))
            g.affine_select(out=hc, in_=hc, compare_op=ALU.is_ge, fill=0.0, base=DH - 1,
                            pattern=[[DH, HEADS]], channel_multiplier=-1)
            g.affine_select(out=vm, in_=vm, compare_op=ALU.is_ge, fill=0.0, base=M - 1,
                            pattern=[[-P, 2], [M, HEADS], [0, DH]], channel_multiplier=-1)
            then(g.affine_select(out=v_heads[:, :, :], in_=v_heads[:, :, :], compare_op=ALU.is_ge, fill=0.0,
                                 base=M - 1, pattern=[[-P, 2], [M, HEADS]], channel_multiplier=-1))
            for b in range(GB):
                g.tensor_copy(vblk[:, b, :, C:C + HEADS], v_heads[:, :, :])
            g.affine_select(out=scan_keep[:, :, :], in_=scan_keep[:, :, :], compare_op=ALU.not_equal, fill=0.0,
                            base=0, pattern=[[0, NE], [1, NJ + 1]], channel_multiplier=0)
            g.affine_select(out=q_aug[:, C:C + 1], in_=q_aug[:, C:C + 1], compare_op=ALU.not_equal, fill=1.0,
                            base=-C, pattern=[[0, 1]], channel_multiplier=1)
            g.affine_select(out=k_aug[:, C:C + 1], in_=k_aug[:, C:C + 1], compare_op=ALU.not_equal, fill=1.0,
                            base=-(C + 1), pattern=[[0, 1]], channel_multiplier=1)
            g.iota(descend[:, :], [[-1, BUCKETS]], base=BUCKETS, channel_multiplier=0,
                   allow_small_or_imprecise_dtypes=True)
            g.iota(region[:, :, :], [[REG // MT, NE], [0, NJ]], base=0, channel_multiplier=0,
                   allow_small_or_imprecise_dtypes=True)
            for k in range(2):
                for s in range(2):
                    for f in range(2):
                        j = 4 * s + 2 * f
                        g.iota(srow[:, k, j:j + 2, ROW - 1:ROW].rearrange("p b o -> p (b o)"), [[N, 2]],
                               base=k * T + 2 * s * N + f * P - GT, channel_multiplier=1,
                               allow_small_or_imprecise_dtypes=True)
            g.memset(wn[:, :, CF, :], 0.0)
            g.memset(w2n[:, HID:CH * P], 0.0)
            g.memset(pad[:, :, :], 0.0)
            for m, n in ((k_rows, T // MT), (g_no, NS)):
                g.iota(m[:, :], [[1, n]], base=0, channel_multiplier=0, allow_small_or_imprecise_dtypes=True)
            then(g.memset(r1[:, :], 0.0))
            g.memset(pad[:, :, ROW - 1:ROW], float(DUMP))
            g.tensor_scalar(g_row[:, :], g_no[:, :], float(MT), None, ALU.mult)
            g.tensor_scalar(k_rows[:, :], k_rows[:, :], float(MT), None, ALU.mult)
            g.tensor_scalar(region[:, :, :], region[:, :, :], float(MT), None, ALU.mult)
            pool.wait_ge(small_loaded, 16 * NSMALL)
            g.tensor_tensor(diag_g1[:, 0:C], ident[0:C, 0:C], g1[:, 0:1].broadcast_to([C, C]), ALU.mult)
            g.tensor_copy(fc2_row[:, 4:8, :], fc2_row[:, 0:4, :])
            rot = proj[:, C:C + M].rearrange("c (h n) -> c h n", h=HASHES)
            g.tensor_scalar(rot[:, :, BUCKETS // 2:], rot[:, :, 0:BUCKETS // 2], -1.0, None, ALU.mult)\
                .then_inc(consts_ready, 1)

            with pool.Fori(0, NG) as i:
                pool.wait_ge(gvar_ready, i + 1)
                g.tensor_tensor(grstd[:, :], gvar[:, :], c_mhalf[:, 0:2], ALU.pow).then_inc(grstd_ready, 1)
                n = 0

                def step_done(ins):
                    nonlocal n
                    n += 1
                    ins.then_inc(pool_step, 1)
                    pool.wait_ge(pool_step, i * POOL_STEPS + n)

                pool.wait_ge(vare_ready, 3 * i + 1)
                g.tensor_tensor(r1[:, :], vare[:, :], c_mhalf[:, :], ALU.pow).then_inc(r_ready, 1)
                pool.wait_ge(r_ready, 4 * i + 1)
                step_done(g.tensor_tensor(r1sq[:, :], r1[:, :], r1[:, :], ALU.mult))
                step_done(g.tensor_tensor(uvar[:, :], r1sq[:, :], v64[:, :], ALU.mult))
                step_done(g.tensor_tensor(uvare[:, :], uvar[:, :], c_eps[:, :], ALU.add))
                step_done(g.tensor_tensor(r2[:, :], uvare[:, :], c_mhalf[:, :], ALU.pow))
                g.tensor_tensor(r12[:, :], r1[:, :], r2[:, :], ALU.mult).then_inc(r_ready, 1)
                pool.wait_ge(vare_ready, 3 * i + 2)
                g.tensor_tensor(r1[:, :], vare[:, :], c_mhalf[:, :], ALU.pow).then_inc(r_ready, 1)
                pool.wait_ge(x2_ready, i + 1)
                g.tensor_tensor(x2t[:, :, :], x2[:, :, :], tok[:, :, :], ALU.add).then_inc(x2t_ready, 1)
                pool.wait_ge(vare_ready, 3 * i + 3)
                g.tensor_tensor(r1[:, :], vare[:, :], c_mhalf[:, :], ALU.pow).then_inc(r_ready, 1)
                pool.wait_ge(scattered, i * 2 * NJ * 16)
                dst = srow[:, :, :, ROW - 1]
                g.tensor_tensor(dst, dst, c_group[:, :, :], ALU.add).then_inc(dst_ready, 1)
                pool.wait_ge(srow_ready, i + 1)
                pool.wait_ge(whi_ready, i + 1)
                pool.sem_inc(waited, 1)
                g.tensor_copy(srow[:, 1, :, 0:C], srow[:, 0, :, 0:C]).then_inc(srow2_ready, 1)
                pool.wait_ge(srow2_ready, i + 1)
                pool.wait_ge(pos_ready, i + 1)
                pool.sem_inc(waited, 1)
                for j in range(NJ):
                    for k in range(2):
                        g.indirect_dma_start(
                            rows[0:NE * REG, :], bass.IndirectOffsetOnAxis(ap=pos[:, k, j:j + 1], axis=0),
                            srow[:, k, j, :], None).then_inc(scattered, 16)
                pool.wait_ge(w_max_ready, i + 1)
                pool.sem_inc(waited, 1)
                g.partition_all_reduce(wmax_all[:, :], wmax[:, :], P, bass.bass_isa.ReduceOp.max)\
                    .then_inc(w_max_all, 1)

            def take_route(nth, b, free=None):
                pool.wait_ge(xin_loaded[b], 16 * (nth + 1))
                if free is not None:
                    pool.wait_ge(yout_ready[b], free)
                pool.sem_inc(waited, 1)
                g.tensor_copy(route[:, b, :, :], xin[:, b, :, C:C + 2]).then_inc(route_ready, 1)

            def store(nth, b):
                pool.wait_ge(yout_ready[b], nth + 1)
                pool.sem_inc(waited, 1)
                for h in range(2):
                    g.indirect_dma_start(
                        results[:, :], bass.IndirectOffsetOnAxis(ap=dest[:, b, h:h + 1], axis=0),
                        yout[:, b, h, :], None, bounds_check=DUMP - 1, oob_is_err=False)\
                        .then_inc(y_scattered[b], 16)

            take_route(0, 0)
            take_route(0, 1)
            with pool.Fori(0, (NT - 1) // 2) as k:
                take_route(k + 1, 0, k + 1)
                store(k, 0)
                take_route(k + 1, 1, k + 1)
                store(k, 1)
            store((NT - 1) // 2, 0)



        @block.tensor
        def _(pe):
            mm = nc.tensor.matmul
            turn = nc.tensor.transpose
            pe.wait_ge(consts_ready, 2)
            mm(bk12[0:C + 1, 0, 0:C + M + 2 * C], diag_g1[:, :], proj[:, :], start=True, stop=True)
            for a in range(2):
                mm(bk12[:, 1, a:a + 1], fc1_n[:, a * P:(a + 1) * P], b2c[:, :], start=True, stop=True)
            turn(bk12[0:C, 1, 8:8 + NE], router_n[:, :], ident[0:NE, 0:NE]).then_inc(pe_setup, 1)
            pe.wait_ge(dve_setup, DVE_SETUP)

            with pe.Fori(0, NG) as i:
                pe.wait_ge(mean_ready, i + 1)
                mm(gmean_ps, pair_mean[:, :], mv[:, :, 0], start=True, stop=True).then_inc(gmean_ready, 1)
                pe.wait_ge(chvar_ready, i + 1)
                mm(gvar_ps, pair_mean[:, :], chvar[:, :], start=True, stop=True).then_inc(gvar_done, 1)
                pe.wait_ge(conv_ready, i + 1)
                for s in range(2):
                    for f in range(2):
                        o = t_ps[:, (2 * s + f) * P:(2 * s + f + 1) * P]
                        h0 = f * HH // 2
                        mm(o, xres[:, s, h0:h0 + 8, :], ident[:, :], start=True, stop=False)
                        for dy in range(3):
                            last = mm(o, hsum[:, s, h0 + dy:h0 + dy + 8, :], ident[:, :], start=False, stop=dy == 2)
                last.then_inc(t_ready, 1)
                pe.wait_ge(n_ready, 3 * i + 1)
                for j in range(NJ):
                    last = turn(bk12[0:C + 1, j // 4, (j % 4) * P:(j % 4 + 1) * P], n1[:, j, :], ident[:, :])
                    if j % 4 == 3:
                        last.then_inc(nt_turned, 1)
                pe.wait_ge(nt_act, 3 * i + 1)
                pe.wait_ge(nt_dve, 3 * i + 1)
                for j in range(NJ):
                    last = mm(rot_ps[:, j * M:(j + 1) * M], n1t[:, j * P:(j + 1) * P], rot_aug[:, :],
                              start=True, stop=True)
                last.then_inc(rot_ready, 1)
                pe.wait_ge(w_stored_act, i)
                for h in range(2):
                    last = mm(bk34[0:C + 1, h, :], q_aug[:, :], n1t[:, h * 512:(h + 1) * 512], start=True, stop=True)
                last.then_inc(q_ready, 1)
                pe.wait_ge(onehot_ready, i + 1)
                oh_v = onehot[:, :, :].rearrange("p (j h) k -> p j (h k)", j=NJ)
                for b in range(GB):
                    for f in range(2):
                        j = 4 * (b // 2) + 2 * f + b % 2
                        last = mm(pool_ps[M * b:M * (b + 1), :], oh_v[:, j, :], n1[:, j, :],
                                  start=f == 0, stop=f == 1)
                last.then_inc(pool_ready, 1)
                pe.wait_ge(pooled_ready, i + 1)
                turn(poolt_ps, pooled[:, :], ident[:, :]).then_inc(poolt_ready, 1)
                pe.wait_ge(pooledt_ready, i + 1)
                mm(k_ps, k_aug[:, :], pooled_t[:, :], start=True, stop=True)
                pe.wait_ge(rep_ready, i + 1)
                for b in range(GB):
                    last = mm(v_ps[:, b, :], pooled_rep[:, b, :, :].rearrange("c h m -> c (h m)"), v_aug[:, :],
                              start=True, stop=True)
                last.then_inc(kv_ready, 1)

                def scores(p):
                    for bp in range(2):
                        j, b = 2 * p + bp, 2 * (p // 2) + bp
                        last = mm(bk56[:, p % 2, bp * 256:(bp + 1) * 256], qt[:, j * P:(j + 1) * P],
                                  kblk[:, b, :, :].rearrange("c h m -> c (h m)"), start=True, stop=True)
                    last.then_inc(s_ready, 1)

                pe.wait_ge(qt_ready, i + 1)
                pe.wait_ge(blk_ready, i + 1)
                pe.wait_ge(w_stored_dve, i)
                scores(0)
                scores(1)
                for p in range(4):
                    pe.wait_ge(prob_ready, 4 * i + p + 1)
                    if p >= 2:
                        pe.wait_ge(probt_ready, 4 * i + p - 1)
                    for a in range(4):
                        last = turn(bk34[:, p % 2, a * P:(a + 1) * P], prob[:, p % 2, a, :], ident[:, :])
                    last.then_inc(probt_turned, 1)
                    if p < 2:
                        pe.wait_ge(ssub_ready, 4 * i + p + 1)
                        scores(p + 2)
                    pe.wait_ge(probt_ready, 4 * i + p + 1)
                    for bp in range(2):
                        b = 2 * (p // 2) + bp
                        for ch in range(2):
                            last = mm(av_ps[p // 2][:, 2 * (p % 2) + bp, :], prob_t[:, p % 2, 2 * bp + ch, :],
                                      vblk[:, b, ch, :], start=ch == 0, stop=ch == 1)
                    last.then_inc(av_ready, 1)
                pe.wait_ge(n_ready, 3 * i + 2)
                pe.sem_inc(waited, 1)
                for j in range(NJ):
                    last = turn(bk12[0:C, j // 4, (j % 4) * P:(j % 4 + 1) * P], n2[:, j, :], ident[:, :])
                    if j % 4 == 3:
                        last.then_inc(nt_turned, 1)
                for h in range(2):
                    if h == 0:
                        pe.wait_ge(nt_act, 3 * i + 2)
                    else:
                        pe.wait_ge(nt_dve, 3 * i + 2)
                    for a in range(2):
                        if h == 1:
                            pe.wait_ge(hid_ready, 4 * i + a + 1)
                        mm(bk56[:, a, :], fc1_s[:, a * P:(a + 1) * P], n2t[:, h * 512:(h + 1) * 512],
                           start=True, stop=True).then_inc(fc1_ready, 1)
                pe.wait_ge(hid_ready, 4 * i + 4)
                for j in range(NJ):
                    mm(y_ps[:, j, :], ones[0:1, :], fc2_row[:, j, :], start=True, stop=False)
                    for a in range(2):
                        last = mm(y_ps[:, j, :], hid[:, a, j * P:(j + 1) * P], fc2_s[:, a, :],
                                  start=False, stop=a == 1)
                last.then_inc(y_ready, 1)
                pe.wait_ge(n_ready, 3 * i + 3)
                pe.sem_inc(waited, 1)
                for j in range(NJ):
                    last = turn(bk12[0:C, j // 4, (j % 4) * P:(j % 4 + 1) * P], wtok[:, j, :], ident[:, :])
                    if j % 4 == 3:
                        last.then_inc(nt_turned, 1)
                pe.wait_ge(nt_act, 3 * i + 3)
                pe.wait_ge(nt_dve, 3 * i + 3)
                for j in range(NJ):
                    last = mm(l_ps[:, j, :], wtok_t[:, j * P:(j + 1) * P], router_t[:, :], start=True, stop=True)
                last.then_inc(router_ready, 1)
                pe.wait_ge(passed_ready, i + 1)
                mm(pos_ps, before[:, :], picked[:, :, 1:NJ + 1], start=True, stop=False)
                mm(pos_ps, ones[:, :], passed[:, :, 0:NJ], start=False, stop=True).then_inc(pos_counted, 1)
                pe.wait_ge(w_parts_ready, i + 1)
                pe.sem_inc(waited, 1)
                for q in range(24):
                    t, ch, part = q // (2 * CH), q // 2 % CH, q % 2
                    for copy in range(2):
                        last = turn(w_dst16[q // 8][copy * C:(copy + 1) * C, (q % 8) * P:(q % 8 + 1) * P],
                                    (w_hi, w_lo)[part][:, t, ch, :], ident16[:, :])
                    if q == 15:
                        last.then_inc(w_turned, 1)
                pe.wait_ge(w2_loaded, 16 * i + 16)
                pe.sem_inc(waited, 1)
                for ch in range(CH):
                    src = w2n[:, ch:CF * P:CF] if ch < CF else w2n[:, CF * P:CH * P]
                    last = turn(bk56[:, 1, ch * C:(ch + 1) * C], src, ident[0:C, 0:C])
                last.then_inc(w_turned, 1)

            pe.wait_ge(dve_step, NG * DVE_STEPS)
            mm(bk7[:, 0:NE], ones[:, :], picked[:, :, 0], start=True, stop=True).then_inc(counted, 1)
            pe.wait_ge(w_stored_act, NG)
            pe.wait_ge(w_stored_dve, NG)
            pe.wait_ge(sched_ready, 1)
            xt_ps = bk7[:, :].bitcast(F16)

            def turn_rows(t, b, nth):
                pe.wait_ge(xin_loaded[b], 16 * (nth + 1))
                if not (isinstance(t, int) and t == 0):
                    pe.wait_ge(xs_ready, t)
                for h in range(2):
                    last = turn(xt_ps[:, h * P:(h + 1) * P], xin[:, b, h, 0:C].bitcast(F16), ident16[:, :])
                last.then_inc(xt_turned, 1)

            def up(t, b):
                e = pe.value_load(tile_expert[0:1, ds(t, 1)], min_val=0, max_val=NE - 1)
                pe.wait_ge(xs_ready, t + 1)
                for q in range(CH // 2):
                    m = (3 * b + q) % 2
                    first = isinstance(t, int) and q < 2
                    for w, bank, free, ready in ((0, bk12, silu_ready, h1_ready), (1, bk34, h_ready, h3_ready)):
                        if not first:
                            pe.wait_ge(free, 3 * t + q - 1)
                        for ch in range(2):
                            for part in range(2):
                                last = mm(bank[:, m, ch * MT:(ch + 1) * MT],
                                          w13[:, ds(e, 1), w, 2 * q + ch, part, :].rearrange("p o n -> p (o n)"),
                                          xs[:, b, :], start=part == 0, stop=part == 1)
                        last.then_inc(ready, 1)

            def down(t, b, nth):
                e = pe.value_load(tile_expert[0:1, ds(t, 1)], min_val=0, max_val=NE - 1)
                pe.wait_ge(h_ready, 3 * t + 3)
                pe.wait_ge(yout_ready[b], nth)
                for h in range(2):
                    for ch in range(CH):
                        last = mm(bk56[:, b, h * C:(h + 1) * C], hbuf[:, b, ch, h * P:(h + 1) * P],
                                  w2s[:, ds(e, 1), ch, :].rearrange("p o n -> p (o n)"),
                                  start=ch == 0, stop=ch == CH - 1)
                last.then_inc(e_y_ready, 1)

            turn_rows(0, 0, 0)
            turn_rows(1, 1, 0)
            up(0, 0)
            with pe.Fori(0, (NT - 1) // 2) as k:
                turn_rows(2 * k + 2, 0, k + 1)
                up(2 * k + 1, 1)
                down(2 * k, 0, k)
                turn_rows(2 * k + 3, 1, k + 1)
                up(2 * k + 2, 0)
                down(2 * k + 1, 1, k)
            down(NT - 1, 0, (NT - 1) // 2)

            with pe.Fori(0, NG // 2) as k:
                for b in range(2):
                    pe.wait_ge(t3_ready, 2 * k + b + 1)
                    pe.wait_ge(og_ready[b], k)
                    for a in range(4):
                        last = turn(bk12[:, b, a * P:(a + 1) * P], t3[:, b, 2 * a:2 * a + 2, :], ident[:, :])
                    last.then_inc(o_turned[b], 1)

        @block.scalar
        def _(act):
            f = nc.scalar.activation
            act.wait_ge(consts_ready, 1)
            with act.Fori(0, NG) as i:
                act.wait_ge(t_ready, i + 1)
                f(tok[:, :, :], t_ps.rearrange("p (j c) -> p j c", j=NJ), ACT.Copy).then_inc(tok_ready, 1)
                act.wait_ge(cent_ready, 3 * i + 1)
                f(sq[:, :, :], cent[:, :, :], ACT.Square).then_inc(sq_ready, 1)
                act.wait_ge(nt_turned, 6 * i + 1)
                f(n1t[:, 0:512], bk12[0:C + 1, 0, :], ACT.Copy).then_inc(nt_act, 1)
                act.wait_ge(q_ready, i + 1)
                f(qt[:, :], bk34[0:C + 1, :, :].rearrange("c a n -> c (a n)"), ACT.Copy).then_inc(qt_ready, 1)
                act.wait_ge(pooledt_ready, i + 1)
                for b in range(GB):
                    ins = f(pooled_rep[:, b, :, :],
                            pooled_t[0:C + 1, M * b:M * (b + 1)].unsqueeze(1).broadcast_to([C + 1, 4, M]), ACT.Copy)
                ins.then_inc(rep_ready, 1)
                for p in range(4):
                    act.wait_ge(ssub_ready, 4 * i + p + 1)
                    if p >= 2:
                        act.wait_ge(probt_turned, 4 * i + p - 1)
                    f(prob[:, p % 2, :, :].rearrange("p a n -> p (a n)"),
                      ssub[:, p % 2, :, :].rearrange("p h m -> p (h m)"), ACT.Exp, scale=DH ** -0.5)\
                        .then_inc(prob_ready, 1)
                    act.wait_ge(probt_turned, 4 * i + p + 1)
                    if p >= 2:
                        act.wait_ge(av_ready, 4 * i + p - 1)
                    f(prob_t[:, p % 2, :, :].rearrange("p a n -> p (a n)"), bk34[:, p % 2, :], ACT.Copy)\
                        .then_inc(probt_ready, 1)
                act.wait_ge(cent_ready, 3 * i + 2)
                f(sq[:, :, :], cent[:, :, :], ACT.Square).then_inc(sq_ready, 1)
                act.wait_ge(nt_turned, 6 * i + 3)
                f(n2t[:, 0:512], bk12[0:C, 0, :], ACT.Copy).then_inc(nt_act, 1)
                for h in range(2):
                    for a in range(2):
                        act.wait_ge(fc1_ready, 4 * i + 2 * h + a + 1)
                        f(hid[:, a, h * 512:(h + 1) * 512], bk56[:, a, :], ACT.Gelu, bias=fc1_bias[:, a:a + 1])\
                            .then_inc(hid_ready, 1)
                act.wait_ge(cent_ready, 3 * i + 3)
                f(sq[:, :, :], cent[:, :, :], ACT.Square).then_inc(sq_ready, 1)
                act.wait_ge(nt_turned, 6 * i + 5)
                f(wtok_t[:, 0:512], bk12[0:C, 0, :], ACT.Copy).then_inc(nt_act, 1)
                act.wait_ge(n_ready, 3 * i + 3)
                act.wait_ge(scattered, i * 2 * NJ * 16)
                hi = srow[:, 0, :, 0:C // 2].bitcast(F16)
                f(hi, wtok[:, :, :], ACT.Copy, scale=XS).then_inc(whi_ready, 1)
                act.wait_ge(lsub_ready, i + 1)
                f(lexp[:, :, :], lsub[:, :, :], ACT.Exp).then_inc(lexp_ready, 1)
                act.wait_ge(w_scale_ready, i + 1)
                act.wait_ge(w_turned, 2 * i)
                for t in range(2):
                    f(w_hi[:, t, :, :].rearrange("p k c -> p (k c)"), wn[:, t, :, :].rearrange("p k c -> p (k c)"),
                      ACT.Copy, scale=wscale[:, t:t + 1].bitcast(F32)).then_inc(w_hi_ready, 1)
                act.wait_ge(w_turned, 2 * i + 1)
                act.sem_inc(waited, 1)
                f(w13_q[:, ds(i, 1), 0:16, :].rearrange("p o q n -> p (o q n)"),
                  bk34[:, :, :].rearrange("p a n -> p (a n)").bitcast(F16), ACT.Copy).then_inc(w_stored_act, 1)

            act.wait_ge(sched_ready, 1)

            def store_xs(t, b):
                act.wait_ge(xt_turned, t + 1)
                if not isinstance(t, int):
                    act.wait_ge(h3_ready, 3 * t - 3)
                f(xs[:, b, :], bk7[:, :].bitcast(F16)[:, 0:MT], ACT.Copy).then_inc(xs_ready, 1)

            def silus(t, b):
                e = act.value_load(tile_expert[0:1, ds(t, 1)], min_val=0, max_val=NE - 1)
                back = wback[:, ds(e, 1), 0:1].rearrange("p o n -> p (o n)").bitcast(F32)
                for q in range(CH // 2):
                    m = (3 * b + q) % 2
                    act.wait_ge(h1_ready, 3 * t + q + 1)
                    if not (isinstance(t, int) and q < 2):
                        act.wait_ge(h_ready, 3 * t + q - 1)
                    act.sem_inc(waited, 1)
                    f(silu[:, m, :], bk12[:, m, :], ACT.Silu, scale=back).then_inc(silu_ready, 1)

            store_xs(0, 0)
            store_xs(1, 1)
            silus(0, 0)
            with act.Fori(0, (NT - 1) // 2) as k:
                store_xs(2 * k + 2, 0)
                silus(2 * k + 1, 1)
                store_xs(2 * k + 3, 1)
                silus(2 * k + 2, 0)

            out_rows = out.rearrange("b c h w -> (b c) (h w)").rearrange("(g s p) n -> g p s n", g=NG, s=2)
            with act.Fori(0, NG // 2) as k:
                for b in range(2):
                    act.wait_ge(o_turned[b], k + 1)
                    act.wait_ge(out_stored[b], 16 * k)
                    f(og[:, b, :], bk12[:, b, :], ACT.Copy).then_inc(og_ready[b], 1)
                    act.wait_ge(og_ready[b], k + 1)
                    act.dma_start(out_rows[ds(2 * k + b, 1)].rearrange("g p s n -> (g p) s n"),
                                  og[:, b, :].rearrange("p (s n) -> p s n", s=2)).then_inc(out_stored[b], 16)
            for b in range(2):
                act.wait_ge(out_stored[b], 16 * (NG // 2))

        @block.vector
        def _(dve):
            v = nc.vector
            tt = v.tensor_tensor

            def wide(col, n):
                return col.unsqueeze(2).broadcast_to([col.shape[0], col.shape[1], n])

            setup = [0]

            def setup_done(ins, wait=True):
                setup[0] += 1
                ins.then_inc(dve_setup, 1)
                if wait:
                    dve.wait_ge(dve_setup, setup[0])

            dve.wait_ge(pe_setup, 1)
            setup_done(v.tensor_copy(q_aug[:, 0:C], bk12[0:C + 1, 0, 0:C]), wait=False)
            setup_done(v.tensor_copy(rot_aug[:, :], bk12[0:C + 1, 0, C:C + M]), wait=False)
            setup_done(v.tensor_copy(k_aug[0:C + 1, 0:C], bk12[0:C + 1, 0, C + M:2 * C + M]), wait=False)
            setup_done(v.tensor_copy(v_aug[:, :], bk12[0:C + 1, 0, 2 * C + M:3 * C + M]), wait=False)
            setup_done(v.tensor_copy(router_t[:, :], bk12[0:C, 1, 8:8 + NE]), wait=False)
            setup_done(v.tensor_scalar(fc1_s[:, :], fc1_n[:, :], g2[:, 0:1], None, ALU.mult), wait=False)
            setup_done(tt(fc1_bias[:, :], bk12[:, 1, 0:2], fc1_bias0[:, :], ALU.add))
            assert setup[0] == DVE_SETUP

            with dve.Fori(0, NG) as i:
                n = 0

                def done(ins):
                    nonlocal n
                    n += 1
                    ins.then_inc(dve_step, 1)
                    dve.wait_ge(dve_step, i * DVE_STEPS + n)

                dve.wait_ge(x_loaded, 16 * i + 16)
                xf = xg[:, :, :, :].rearrange("p s h w -> p s (h w)")
                v.bn_stats(bst[:, 0, :], xf[:, 0, :])
                done(v.bn_stats(bst[:, 1, :], xf[:, 1, :]))
                v.tensor_copy(cnt[:, :], ones[:, 0:1])
                v.bn_aggr(mv[:, 0, :], bst[:, 0, :])
                v.bn_aggr(mv[:, 1, :], bst[:, 1, :]).then_inc(mean_ready, 1)
                dve.wait_ge(mean_ready, i + 1)
                dve.wait_ge(gmean_ready, i + 1)
                done(tt(dmean[:, :], mv[:, :, 0], gmean_ps, ALU.subtract))
                done(tt(dmean2[:, :], dmean[:, :], dmean[:, :], ALU.mult))
                tt(chvar[:, :], dmean2[:, :], mv[:, :, 1], ALU.add).then_inc(chvar_ready, 1)
                dve.wait_ge(gvar_done, i + 1)
                v.tensor_scalar(gvar[:, :], gvar_ps, EPS, None, ALU.add).then_inc(gvar_ready, 1)
                done(v.tensor_copy(gmean[:, :], gmean_ps))
                dve.wait_ge(grstd_ready, i + 1)
                for s in range(2):
                    ins = v.tensor_scalar(xpad[:, s, 1:HH + 1, 1:WW + 1], xg[:, s, :, :], gmean[:, s:s + 1],
                                          grstd[:, s:s + 1], ALU.subtract, ALU.mult)
                done(ins)
                inner = xpad[:, :, 1:HH + 1, :]
                hin = hsum[:, :, 1:HH + 1, :]
                for s in range(2):
                    ins = v.scalar_tensor_tensor(out=xres[:, s, :, :], in0=xg[:, s, :, :], scalar=bias2[:, 0:1],
                                                 in1=xpad[:, s, 1:HH + 1, 1:WW + 1], op0=ALU.add, op1=ALU.add)
                ins.then_inc(x_used, 1)
                done(tt(hin, inner[:, :, :, 0:WW], inner[:, :, :, 1:WW + 1], ALU.add))
                tt(hin, hin, inner[:, :, :, 2:WW + 2], ALU.add).then_inc(conv_ready, 1)

                def layer_norm(src, k):
                    done(v.tensor_reduce(ssum[:, :], src, AX.X, ALU.add))
                    v.scalar_tensor_tensor(out=cent[:, :, :], in0=wide(ssum[:, :], C), scalar=-1.0 / C, in1=src,
                                           op0=ALU.mult, op1=ALU.add).then_inc(cent_ready, 1)
                    dve.wait_ge(sq_ready, 3 * i + k)
                    done(v.tensor_reduce(ssq[:, :], sq[:, :, :], AX.X, ALU.add))
                    if k == 1:
                        v.tensor_scalar(v64[:, :], ssq[:, :], 1.0 / C, None, ALU.mult)
                    v.tensor_scalar(vare[:, :], ssq[:, :], 1.0 / C, EPS, ALU.mult, ALU.add).then_inc(vare_ready, 1)

                def store_turned(dst, rows_, k):
                    dve.wait_ge(nt_turned, 6 * i + 2 * k)
                    v.tensor_copy(dst[:, 512:1024], bk12[0:rows_, 1, :]).then_inc(nt_dve, 1)

                dve.wait_ge(tok_ready, i + 1)
                layer_norm(tok[:, :, :], 1)
                dve.wait_ge(r_ready, 4 * i + 1)
                tt(u[:, :, :], cent[:, :, :], wide(r1[:, :], C), ALU.mult)
                dve.wait_ge(r_ready, 4 * i + 2)
                tt(n1[:, :, 0:C], cent[:, :, :], wide(r12[:, :], C), ALU.mult).then_inc(n_ready, 1)
                store_turned(n1t, C + 1, 1)
                dve.wait_ge(rot_ready, i + 1)
                rot = rot_ps.rearrange("p (a k) -> p a k", k=BUCKETS)
                done(v.tensor_reduce(bmax[:, :], rot, AX.X, ALU.max))
                done(tt(beq[:, :, :], rot, wide(bmax[:, :], BUCKETS), ALU.is_equal))
                rank = descend[:, :].unsqueeze(1).broadcast_to([P, NJ * HASHES, BUCKETS])
                done(tt(beq[:, :, :], beq[:, :, :], rank, ALU.mult))
                done(v.tensor_reduce(bfirst[:, :], beq[:, :, :], AX.X, ALU.max))
                tt(onehot[:, :, :], beq[:, :, :], wide(bfirst[:, :], BUCKETS), ALU.is_equal).then_inc(onehot_ready, 1)
                dve.wait_ge(pool_ready, i + 1)
                n_in = pool_ps[:, C:C + 1]
                v.tensor_scalar(pooled[:, C + 1:C + 2], n_in, 1.0, MASKED, ALU.is_lt, ALU.mult)
                done(v.tensor_scalar(cnt[:, :], n_in, 1e-20, None, ALU.add))
                done(v.reciprocal(rcnt[:, :], cnt[:, :]))
                v.tensor_scalar(pooled[:, 0:C + 1], pool_ps, rcnt[:, 0:1], None, ALU.mult).then_inc(pooled_ready, 1)
                dve.wait_ge(poolt_ready, i + 1)
                v.tensor_copy(pooled_t[:, :], poolt_ps).then_inc(pooledt_ready, 1)
                dve.wait_ge(kv_ready, i + 1)
                for b in range(GB):
                    tt(kblk[:, b, :, :], k_ps[:, M * b:M * (b + 1)].unsqueeze(1).broadcast_to([C + 1, HEADS, M]),
                       wide(head_of[:, :], M), ALU.mult)
                for ch in range(2):
                    ins = tt(vblk[:, :, ch, 0:C], v_ps,
                             v_mask[:, ch, :].unsqueeze(1).broadcast_to([P, GB, C]), ALU.mult)
                ins.then_inc(blk_ready, 1)

                def centre(p):
                    dve.wait_ge(s_ready, 4 * i + p + 1)
                    s_ps = bk56[:, p % 2, :].rearrange("p (h m) -> p h m", m=M)
                    done(v.tensor_reduce(smax[:, p % 2, :], s_ps, AX.X, ALU.max))
                    if p >= 2:
                        dve.wait_ge(prob_ready, 4 * i + p - 1)
                    tt(ssub[:, p % 2, :, :], s_ps, wide(smax[:, p % 2, :], M), ALU.subtract).then_inc(ssub_ready, 1)

                def attended(s):
                    dve.wait_ge(av_ready, 4 * i + 2 * s + 2)
                    done(v.reciprocal(rden[:, s, :, :], av_ps[s][:, :, C:C + HEADS]))
                    o = av_ps[s][:, :, 0:C].rearrange("p j (h d) -> p j h d", d=DH)
                    r = rden[:, s, :, :].unsqueeze(3).broadcast_to([P, 4, HEADS, DH])
                    done(tt(att[:, s, :, :].rearrange("p j (h d) -> p j h d", d=DH), o, r, ALU.mult))

                centre(0)
                centre(1)
                centre(2)
                centre(3)
                attended(0)
                tt(x2[:, 0:4, :], u[:, 0:4, :], att[:, 0, :, :], ALU.add)
                attended(1)
                tt(x2[:, 4:8, :], u[:, 4:8, :], att[:, 1, :, :], ALU.add).then_inc(x2_ready, 1)
                dve.wait_ge(x2_ready, i + 1)
                layer_norm(x2[:, :, :], 2)
                dve.wait_ge(r_ready, 4 * i + 3)
                tt(n2[:, :, :], cent[:, :, :], wide(r1[:, :], C), ALU.mult).then_inc(n_ready, 1)
                store_turned(n2t, C, 2)
                dve.wait_ge(x2t_ready, i + 1)
                dve.wait_ge(y_ready, i + 1)
                done(tt(t2[:, :, :], x2t[:, :, :], y_ps, ALU.add))
                v.tensor_copy(t2_all[:, ds(i, 1), :, :].rearrange("p o j c -> p (o j c)"),
                              t2[:, :, :].rearrange("p j c -> p (j c)"))
                layer_norm(t2[:, :, :], 3)
                dve.wait_ge(r_ready, 4 * i + 4)
                tt(wtok[:, :, :], cent[:, :, :], wide(r1[:, :], C), ALU.mult).then_inc(n_ready, 1)
                store_turned(wtok_t, C, 3)
                dve.wait_ge(router_ready, i + 1)
                done(v.tensor_reduce(lmax[:, :], l_ps, AX.X, ALU.max))
                tt(lsub[:, :, :], l_ps, wide(lmax[:, :], NE), ALU.subtract).then_inc(lsub_ready, 1)
                dve.wait_ge(lexp_ready, i + 1)
                done(v.tensor_reduce(lden[:, :], lexp[:, :, :], AX.X, ALU.add))
                done(v.reciprocal(lrec[:, :], lden[:, :]))
                done(tt(pr[:, :, :], lexp[:, :, :], wide(lrec[:, :], NE), ALU.mult))
                order = descend[:, :].unsqueeze(1).broadcast_to([P, NJ, NE])

                def pick(src, k):
                    done(v.tensor_reduce(pk[:, k, :], src, AX.X, ALU.max))
                    done(tt(peq[:, :, :], src, wide(pk[:, k, :], NE), ALU.is_equal))
                    done(tt(peq[:, :, :], peq[:, :, :], order, ALU.mult))
                    done(v.tensor_reduce(pfirst[:, :], peq[:, :, :], AX.X, ALU.max))
                    done(tt(oh[:, k, :, :], peq[:, :, :], wide(pfirst[:, :], NE), ALU.is_equal))

                pick(pr[:, :, :], 0)
                done(v.scalar_tensor_tensor(out=prest[:, :, :], in0=oh[:, 0, :, :], scalar=-2.0, in1=pr[:, :, :],
                                            op0=ALU.mult, op1=ALU.add))
                pick(prest[:, :, :], 1)
                by_e = "p j e -> p e j"
                tt(picked[:, :, 1:NJ + 1], oh[:, 0, :, :].rearrange(by_e), oh[:, 1, :, :].rearrange(by_e), ALU.add)
                done(tt(gsum[:, :], pk[:, 0, :], pk[:, 1, :], ALU.add))
                flat9 = "p e j -> p (e j)"
                v.tensor_tensor_scan(passed[:, :, :].rearrange(flat9), scan_keep[:, :, :].rearrange(flat9),
                                     picked[:, :, :].rearrange(flat9), 0.0, ALU.mult, ALU.add)\
                    .then_inc(passed_ready, 1)
                done(v.tensor_scalar(gsum[:, :], gsum[:, :], 1e-9, None, ALU.add))
                done(v.reciprocal(grec[:, :], gsum[:, :]))
                dve.wait_ge(dst_ready, i + 1)
                for k in range(2):
                    tt(srow[:, k, :, C], pk[:, k, :], grec[:, :], ALU.mult)
                dve.wait_ge(whi_ready, i + 1)
                hi = srow[:, 0, :, 0:C // 2].bitcast(F16)
                lo = srow[:, 0, :, C // 2:C].bitcast(F16)
                v.scalar_tensor_tensor(out=lo, in0=wtok[:, :, :], scalar=XS, in1=hi, op0=ALU.mult,
                                       op1=ALU.subtract).then_inc(srow_ready, 1)
                dve.wait_ge(pos_counted, i + 1)
                v.tensor_copy(picked[:, :, 0], passed[:, :, NJ])
                done(tt(posall[:, :, :], pos_ps, region[:, :, :], ALU.add))
                for k in range(2):
                    ins = tt(posk[:, k, :, :], posall[:, :, :], oh[:, k, :, :].rearrange(by_e), ALU.mult)
                done(ins)
                for k in range(2):
                    ins = v.tensor_reduce(posf[:, k, :], posk[:, k, :, :].rearrange("p e j -> p j e"), AX.X, ALU.add)
                done(ins)
                v.tensor_copy(pos[:, :, :], posf[:, :, :]).then_inc(pos_ready, 1)
                dve.wait_ge(experts_loaded, 64 * i + 64)
                v.tensor_reduce(wmax[:, :], wn[:, :, :, :].rearrange("p t k c -> p t (k c)"), AX.X, ALU.max,
                                apply_absolute_value=True).then_inc(w_max_ready, 1)
                dve.wait_ge(w_max_all, i + 1)
                done(v.tensor_scalar(wmax[:, :], wmax_all[:, :], TINY, None, ALU.max))
                done(v.tensor_scalar(wexp[:, :], wmax[:, :].bitcast(U32), EXP_MASK, None, ALU.bitwise_and))
                v.tensor_scalar(wback[:, ds(i, 1), :].rearrange("p o t -> p (o t)"), wexp[:, :],
                                float(-BACK_EXP << 23), None, ALU.add)
                v.tensor_scalar(wscale[:, :], wexp[:, :], -1.0, float(SCALE_EXP << 23), ALU.mult, ALU.add)\
                    .then_inc(w_scale_ready, 1)
                for t in range(2):
                    dve.wait_ge(w_hi_ready, 2 * i + t + 1)
                    flat = "p k c -> p (k c)"
                    ins = v.scalar_tensor_tensor(
                        out=w_lo[:, t, :, :].rearrange(flat), in0=wn[:, t, :, :].rearrange(flat),
                        scalar=wscale[:, t:t + 1].bitcast(F32), in1=w_hi[:, t, :, :].rearrange(flat),
                        op0=ALU.mult, op1=ALU.subtract)
                ins.then_inc(w_parts_ready, 1)
                dve.wait_ge(w_turned, 2 * i + 2)
                v.tensor_copy(w13_q[:, ds(i, 1), 16:24, :].rearrange("p o q n -> p (o q n)"), w_dst16[2])
                v.tensor_copy(w2s[:, ds(i, 1), :, :].rearrange("p o k c -> p (o k c)"), bk56[:, 1, 0:CH * C])\
                    .then_inc(w_stored_dve, 1)
                assert n == DVE_STEPS, n

            n = 0

            def step_done(ins):
                nonlocal n
                n += 1
                ins.then_inc(sched_step, 1)
                dve.wait_ge(sched_step, n)

            dve.wait_ge(w_stored_dve, NG)
            dve.wait_ge(counted, 1)
            step_done(v.tensor_copy(cnt8[:, :], bk7[0:1, 0:NE]))
            nk = T // MT
            step_done(tt(over[:, :, :], wide(cnt8[:, :], nk), k_rows[:, :].unsqueeze(1).broadcast_to([1, NE, nk]),
                         ALU.is_gt))
            step_done(v.tensor_reduce(tiles[:, :], over[:, :, :], AX.X, ALU.add))
            tt(pad_row[:, :], cnt8[:, :], region[0:1, :, 0], ALU.add)
            v.tensor_scalar(adjust[:, :], tiles[:, :], -float(MT), float(REG), ALU.mult, ALU.add)
            step_done(v.tensor_tensor_scan(tiles_end[:, :], ones[0:1, 0:NE], tiles[:, :], 0.0, ALU.mult, ALU.add))
            step_done(tt(past[:, :, :], wide(g_no[:, :], NE), tiles_end[:, :].unsqueeze(1).broadcast_to([1, NS, NE]),
                         ALU.is_ge))
            step_done(v.tensor_reduce(n_past[:, :], past[:, :, :], AX.X, ALU.add))
            v.tensor_scalar(tile_expert[:, :], n_past[:, :], float(NE - 1), None, ALU.min)
            step_done(tt(past_a[:, :, :], past[:, :, :], adjust[:, :].unsqueeze(1).broadcast_to([1, NS, NE]),
                         ALU.mult))
            step_done(v.tensor_reduce(a_past[:, :], past_a[:, :, :], AX.X, ALU.add))
            step_done(tt(a_past[:, :], a_past[:, :], g_row[:, :], ALU.add))
            v.tensor_scalar(tile_row[:, :], a_past[:, :], float(NE * REG), None, ALU.min).then_inc(sched_ready, 1)
            dve.wait_ge(sched_ready, 1)

            def gated(t, b):
                e = dve.value_load(tile_expert[0:1, ds(t, 1)], min_val=0, max_val=NE - 1)
                back = wback[:, ds(e, 1), 1:2].rearrange("p o n -> p (o n)").bitcast(F32)
                for q in range(CH // 2):
                    m = (3 * b + q) % 2
                    dve.wait_ge(silu_ready, 3 * t + q + 1)
                    dve.wait_ge(h3_ready, 3 * t + q + 1)
                    v.scalar_tensor_tensor(out=hbuf[:, b, 2 * q:2 * q + 2, :].rearrange("p k n -> p (k n)"),
                                           in0=bk34[:, m, :], scalar=back, in1=silu[:, m, :],
                                           op0=ALU.mult, op1=ALU.mult).then_inc(h_ready, 1)

            def gate_out(t, b, nth):
                dve.wait_ge(e_y_ready, t + 1)
                dve.wait_ge(route_ready, t + 1)
                dve.wait_ge(y_scattered[b], 32 * nth)
                v.tensor_copy(dest[:, b, :], route[:, b, :, 1])
                tt(yout[:, b, :, :], bk56[:, b, 0:2 * C].rearrange("p (h c) -> p h c", h=2),
                   wide(route[:, b, :, 0], C), ALU.mult).then_inc(yout_ready[b], 1)

            gated(0, 0)
            with dve.Fori(0, (NT - 1) // 2) as k:
                gated(2 * k + 1, 1)
                gate_out(2 * k, 0, k)
                gated(2 * k + 2, 0)
                gate_out(2 * k + 1, 1, k)
            gate_out(NT - 1, 0, (NT - 1) // 2)

            with dve.Fori(0, NG // 2) as k:
                for b in range(2):
                    dve.wait_ge(res_loaded[b], 128 * (k + 1))
                    dve.wait_ge(o_turned[b], k)
                    tt(t3[:, b, :, :], res[:, b, 0, :, :], res[:, b, 1, :, :], ALU.add).then_inc(t3_sum, 1)
                    dve.wait_ge(t3_sum, 2 * k + b + 1)
                    tt(t3[:, b, :, :].rearrange("p j c -> p (j c)"), t3[:, b, :, :].rearrange("p j c -> p (j c)"),
                       t2_all[:, ds(2 * k + b, 1), :, :].rearrange("p o j c -> p (o j c)"), ALU.add)\
                        .then_inc(t3_ready, 1)


DVE_SETUP = 7
DVE_STEPS = 50
POOL_STEPS = 4


def kernel(**inputs):
    import numpy as np
    import concourse.bacc as bacc
    from concourse.bass_utils import run_bass_kernel_spmd

    names = ["x", "L0_conv_bias", "L1_attn_rotations", "L1_attn_norm1_g", "L1_attn_norm1_b", "L1_attn_q_w",
             "L1_attn_kv_w", "L1_attn_norm2_g", "L1_attn_norm2_b", "L1_attn_fc1_w", "L1_attn_fc1_b",
             "L1_attn_fc2_w", "L1_attn_fc2_b", "L1_ffn_router_w", "L1_ffn_w1", "L1_ffn_w2", "L1_ffn_w3"]
    nc = bacc.Bacc("TRN2", target_bir_lowering=False, num_devices=1)
    arrays, args = {}, []
    for name in names:
        a = np.ascontiguousarray(inputs[name])
        arrays[f"in_{name}"] = a
        args.append(nc.dram_tensor(f"in_{name}", a.shape, mybir.dt.from_np(a.dtype), kind="ExternalInput").ap())
    out = nc.dram_tensor("out_0", (B, C, HH, WW), F32, kind="ExternalOutput").ap()
    hybrid_block(nc, *args, out)
    r = run_bass_kernel_spmd(nc, [arrays], core_ids=[0])
    return r.results[0]["out_0"]
```

```python
from contextlib import ExitStack

import concourse.bass as bass
from concourse import mybir
from concourse.bass import ds

P = 128
B, C, HH, WW = 32, 64, 16, 16
N = HH * WW
T = B * N
GB = 4
NG = B // GB
GT = GB * N
NJ = GT // P
HASHES, BUCKETS = 4, 8
M = HASHES * BUCKETS
HEADS = 8
DH = C // HEADS
DFF = 4 * C
NE = 8
HID = 682
CF = 5
CR = HID - CF * P
CH = CF + 1
MT = 256
REG = T + MT
NT = (2 * T + NE * (MT - 1)) // MT
NS = NT + 1
ROW = C + 2
DUMP = 2 * T
XS = 2048.0
EPS = 1e-5
TINY = 1e-30
EXP_MASK = 0x7F800000
SCALE_EXP = 127 + 13 + 127
BACK_EXP = 13 + 11
MASKED = -1e30

ALU = mybir.AluOpType
ACT = mybir.ActivationFunctionType
F32 = mybir.dt.float32
F16 = mybir.dt.float16
U32 = mybir.dt.uint32
I32 = mybir.dt.int32
AX = mybir.AxisListType


def hybrid_block(nc, x, conv_bias, rotations, norm1_g, norm1_b, q_w, kv_w, norm2_g, norm2_b,
                 fc1_w, fc1_b, fc2_w, fc2_b, router_w, w1, w2, w3, out):
    with ExitStack() as ctx:
        def sb(name, shape, dt=F32):
            return ctx.enter_context(nc.sbuf_tensor(name, shape, dt))

        def sem(name):
            return ctx.enter_context(nc.semaphore(name))

        rows = nc.dram_tensor("expert_rows", (NE * REG + MT, ROW), F32).ap()
        results = nc.dram_tensor("expert_results", (DUMP, C), F32).ap()

        ident = sb("ident", [P, P])
        ident16 = sb("ident16", [P, P], F16)
        pair_mean = sb("pair_mean", [P, P])
        before = sb("before", [P, P])
        ones = sb("ones", [P, P])
        descend = sb("descend", [P, BUCKETS])
        head_of = sb("head_of", [C + 1, HEADS])
        v_mask = sb("v_mask", [P, 2, C])
        v_heads = sb("v_heads", [P, 2, HEADS])
        region = sb("region", [P, NE, NJ])
        scan_keep = sb("scan_keep", [P, NE, NJ + 1])
        c_mhalf = sb("c_mhalf", [P, NJ])
        c_64th = sb("c_64th", [P, NJ])
        c_eps = sb("c_eps", [P, NJ])
        c_group = sb("c_group", [P, 2, NJ])
        bias2 = sb("bias2", [P, 1])
        g1 = sb("g1", [C, 1])
        g2 = sb("g2", [P, 1])
        b2c = sb("b2c", [C, 1])
        fc1_bias0 = sb("fc1_bias0", [P, 2])
        fc1_bias = sb("fc1_bias", [P, 2])
        diag_g1 = sb("diag_g1", [C, C + 1])
        proj = sb("proj", [C, C + M + 2 * C])
        q_aug = sb("q_aug", [C + 1, C + 1])
        rot_aug = sb("rot_aug", [C + 1, M])
        k_aug = sb("k_aug", [C + 2, C + 1])
        v_aug = sb("v_aug", [C + 1, C])
        fc1_n = sb("fc1_n", [P, DFF])
        fc1_s = sb("fc1_s", [P, DFF])
        fc1_p = sb("fc1_p", [P, 2, DFF], F16)
        fc2_s = sb("fc2_s", [P, 2, C])
        fc2_bias = sb("fc2_bias", [P, C])
        router_n = sb("router_n", [NE, 2 * C])
        router_t = sb("router_t", [P, NE])
        router_p = sb("router_p", [P, 2, NE], F16)
        small_max = sb("small_max", [P, 2])
        small_max_all = sb("small_max_all", [P, 2])
        small_scale = sb("small_scale", [P, 2], U32)
        small_back = sb("small_back", [P, 2], U32)
        wn = sb("wn", [P, 2, CH, C])
        w2n = sb("w2n", [C, CH * P])
        w_hi = sb("w_hi", [P, 2, CH, C], F16)
        w_lo = sb("w_lo", [P, 2, CH, C], F16)
        w13 = sb("w13", [P, NE, 2, CH, 2, P], F16)
        w2s = sb("w2s", [P, NE, CH, C])
        wmax = sb("wmax", [P, 2])
        wmax_all = sb("wmax_all", [P, 2])
        wexp = sb("wexp", [P, 2], U32)
        wscale = sb("wscale", [P, 2], U32)
        wback = sb("wback", [P, NE, 2], U32)
        xg = sb("xg", [P, 2, HH, WW])
        xpad = sb("xpad", [P, 2, HH + 2, WW + 2])
        hsum = sb("hsum", [P, 2, HH + 2, WW])
        xres = sb("xres", [P, 2, HH, WW])
        bst = sb("bst", [P, 2, 6])
        mv = sb("mv", [P, 2, 2])
        dmean = sb("dmean", [P, 2])
        dmean2 = sb("dmean2", [P, 2])
        chvar = sb("chvar", [P, 2])
        gmean = sb("gmean", [P, 2])
        gvar = sb("gvar", [P, 2])
        grstd = sb("grstd", [P, 2])
        tok = sb("tok", [P, NJ, C])
        cent_a, cent_c = sb("cent_a", [P, NJ, C]), sb("cent_c", [P, NJ, C])
        sq_a, sq_c = sb("sq_a", [P, NJ, C]), sb("sq_c", [P, NJ, C])
        ssum_a, ssum_c = sb("ssum_a", [P, NJ]), sb("ssum_c", [P, NJ])
        ssq_a, ssq_c = sb("ssq_a", [P, NJ]), sb("ssq_c", [P, NJ])
        vare_a, vare_c = sb("vare_a", [P, NJ]), sb("vare_c", [P, NJ])
        r1, rc = sb("r1", [P, NJ]), sb("rc", [P, NJ])
        r1sq = sb("r1sq", [P, NJ])
        v64 = sb("v64", [P, NJ])
        uvar = sb("uvar", [P, NJ])
        uvare = sb("uvare", [P, NJ])
        r2 = sb("r2", [P, NJ])
        r12 = sb("r12", [P, NJ])
        u = sb("u", [P, NJ, C])
        n1 = sb("n1", [P, NJ, C + 1])
        res = sb("res", [P, 2, 2, NJ, C])
        n1t = res[0:C + 1, 0, :, :, :].rearrange("p k j c -> p (k j c)")
        qt = res[0:C + 1, 1, :, :, :].rearrange("p k j c -> p (k j c)")
        bmax = sb("bmax", [P, NJ * HASHES])
        beq = sb("beq", [P, NJ * HASHES, BUCKETS])
        bfirst = sb("bfirst", [P, NJ * HASHES])
        onehot = sb("onehot", [P, NJ * HASHES, BUCKETS])
        cnt = sb("cnt", [P, 1])
        rcnt = sb("rcnt", [P, 1])
        pooled = sb("pooled", [P, C + 2])
        pooled_t = sb("pooled_t", [C + 2, P])
        pooled_rep = sb("pooled_rep", [C + 1, GB, 4, M])
        kblk = sb("kblk", [C + 1, GB, HEADS, M])
        vblk = sb("vblk", [P, GB, 2, C + HEADS])
        smax = sb("smax", [P, 2, 2 * HEADS])
        ssub = sb("ssub", [P, 2, 2 * HEADS, M])
        silu = ssub[:, :, :, :].rearrange("p b h m -> p b (h m)")
        prob = sb("prob", [P, 2, 4, P])
        prob_t = sb("prob_t", [P, 2, 4, P])
        rden = sb("rden", [P, 2, 4, HEADS])
        att = sb("att", [P, 2, 4, C])
        x2 = sb("x2", [P, NJ, C])
        u_tok = sb("u_tok", [P, NJ, C])
        x2t = sb("x2t", [P, NJ, C])
        n2s = sb("n2s", [P, NJ, 2 * C], F16)
        n2 = sb("n2", [P, NJ, C])
        hbuf = sb("hbuf", [P, 2, CH, MT])
        hid = hbuf[:, :, :, :].rearrange("p b k n -> p (b k n)")[:, 0:2 * GT].rearrange("p (a n) -> p a n", a=2)
        t3 = sb("t3", [P, 2, NJ, C])
        og = sb("og", [P, 2, 2 * N])
        n2t = t3[:, 0, :, :].rearrange("p j c -> p (j c)").bitcast(F16)
        wtok_t = t3[:, 1, :, :].rearrange("p j c -> p (j c)").bitcast(F16)
        t2 = sb("t2", [P, NJ, C])
        t2_all = sb("t2_all", [P, NG, NJ, C])
        wtok = sb("wtok", [P, NJ, C])
        lmax = sb("lmax", [P, NJ])
        lsub = sb("lsub", [P, NJ, NE])
        lexp = sb("lexp", [P, NJ, NE])
        lden = sb("lden", [P, NJ])
        lrec = sb("lrec", [P, NJ])
        pr = sb("pr", [P, NJ, NE])
        pk = sb("pk", [P, 2, NJ])
        peq = sb("peq", [P, NJ, NE])
        pfirst = sb("pfirst", [P, NJ])
        oh = sb("oh", [P, 2, NJ, NE])
        prest = sb("prest", [P, NJ, NE])
        gsum = sb("gsum", [P, NJ])
        grec = sb("grec", [P, NJ])
        picked = sb("picked", [P, NE, NJ + 1])
        passed = sb("passed", [P, NE, NJ + 1])
        posall = sb("posall", [P, NE, NJ])
        posk = sb("posk", [P, 2, NE, NJ])
        posf = sb("posf", [P, 2, NJ])
        pos = sb("pos", [P, 2, NJ], U32)
        srow = sb("srow", [P, 2, NJ, ROW])

        cnt8 = sb("cnt8", [P, NE])
        k_rows = sb("k_rows", [P, T // MT])
        over = sb("over", [P, NE, T // MT])
        tiles = sb("tiles", [P, NE])
        tiles_end = sb("tiles_end", [P, NE])
        adjust = sb("adjust", [P, NE])
        g_no = sb("g_no", [P, NS])
        g_row = sb("g_row", [P, NS])
        past = sb("past", [P, NS, NE])
        past_a = sb("past_a", [P, NS, NE])
        n_past = sb("n_past", [P, NS])
        a_past = sb("a_past", [P, NS])
        tile_expert = sb("tile_expert", [P, NS], U32)
        tile_expert_f = sb("tile_expert_f", [P, NS])
        e_no = sb("e_no", [P, NE])
        tile_back = sb("tile_back", [P, NS, 2])
        tile_row = sb("tile_row", [P, NS], U32)
        pad_row = sb("pad_row", [P, NE], U32)
        pad = sb("pad", [P, 2, ROW])
        xin = sb("xin", [P, 2, 2, ROW])
        xs = sb("xs", [P, 2, MT], F16)
        route = sb("route", [P, 2, 2, 2])
        dest = sb("dest", [P, 2, 2], U32)
        yout = sb("yout", [P, 2, 2, C])

        def ps(name, shape, dt=F32):
            return ctx.enter_context(nc.psum_tensor(name, shape, dt))

        bk0 = ps("bk0", [P, 512])
        bk12 = ps("bk12", [P, 2, 512])
        bk34 = ps("bk34", [P, 2, 512])
        bk56 = ps("bk56", [P, 2, 512])
        bk7 = ps("bk7", [P, 512])

        bk5, bk6 = bk56[:, 0, :], bk56[:, 1, :]
        t_ps = bk0[:, :]
        gmean_ps = bk0[:, 0:2]
        gvar_ps = bk0[:, 8:10]
        rot_ps = bk5[:, 0:256]
        pool_ps = bk5[:, 256:256 + C + 1]
        poolt_ps = bk5[0:C + 2, 384:512]
        av_ps = bk5[:, 0:4 * (C + HEADS)].rearrange("p (j c) -> p j c", j=4)
        k_ps = bk34[0:C + 1, 0, 0:P]
        v_ps = bk34[:, 0, 256:512].rearrange("p (b c) -> p b c", b=GB)
        fc1_ps = [bk7[:, :], bk6]
        y_ps = bk7[:, :].rearrange("p (j c) -> p j c", j=NJ)
        l_ps = bk7[:, 0:NJ * NE].rearrange("p (j e) -> p j e", j=NJ)
        pos_ps = bk7[:, 128:128 + NE * NJ].rearrange("p (e j) -> p e j", e=NE)
        w13_q = w13[:, :, :, :, :, :].rearrange("p e t k a n -> p e (t k a) n")
        w_turn_ps = [bk6.bitcast(F16), bk7[:, :].bitcast(F16), bk6.bitcast(F16)]

        waited = sem("waited")
        small_loaded = sem("small_loaded")
        experts_loaded = sem("experts_loaded")
        w2_loaded = sem("w2_loaded")
        sched_ready = sem("sched_ready")
        counted = sem("counted")
        pads_written = sem("pads_written")
        xin_loaded = [sem(f"xin_loaded{b}") for b in range(2)]
        xt_turned = sem("xt_turned")
        xs_ready = sem("xs_ready")
        h1_ready = sem("h1_ready")
        h3_ready = sem("h3_ready")
        silu_ready = sem("silu_ready")
        h_ready = sem("h_ready")
        e_y_ready = sem("e_y_ready")
        route_ready = sem("route_ready")
        yout_ready = [sem(f"yout_ready{b}") for b in range(2)]
        y_scattered = [sem(f"y_scattered{b}") for b in range(2)]
        res_loaded = [sem(f"res_loaded{b}") for b in range(2)]
        t3_ready = sem("t3_ready")
        t3_sum = sem("t3_sum")
        sched_step = sem("sched_step")
        o_turned = [sem(f"o_turned{b}") for b in range(2)]
        og_ready = [sem(f"og_ready{b}") for b in range(2)]
        out_stored = [sem(f"out_stored{b}") for b in range(2)]
        consts_step = sem("consts_step")
        consts_ready = sem("consts_ready")
        pe_setup = sem("pe_setup")
        dve_setup = sem("dve_setup")
        w_max_ready = sem("w_max_ready")
        w_scale_ready = sem("w_scale_ready")
        w_max_all = sem("w_max_all")
        w_hi_ready = sem("w_hi_ready")
        w_parts_ready = sem("w_parts_ready")
        w_turned = sem("w_turned")
        w_stored_act = sem("w_stored_act")
        w_stored_dve = sem("w_stored_dve")
        x_loaded = sem("x_loaded")
        x_used = sem("x_used")
        mean_ready = sem("mean_ready")
        gmean_ready = sem("gmean_ready")
        chvar_ready = sem("chvar_ready")
        gvar_done = sem("gvar_done")
        gvar_ready = sem("gvar_ready")
        grstd_ready = sem("grstd_ready")
        conv_ready = sem("conv_ready")
        t_ready = sem("t_ready")
        tok_ready = sem("tok_ready")
        rot_ready = sem("rot_ready")
        q_ready = sem("q_ready")
        qt_ready = sem("qt_ready")
        onehot_ready = sem("onehot_ready")
        pool_ready = sem("pool_ready")
        pooled_ready = sem("pooled_ready")
        poolt_ready = sem("poolt_ready")
        pooledt_ready = sem("pooledt_ready")
        rep_ready = sem("rep_ready")
        kv_ready = sem("kv_ready")
        blk_ready = sem("blk_ready")
        s_ready = sem("s_ready")
        ssub_ready = sem("ssub_ready")
        prob_ready = sem("prob_ready")
        probt_turned = sem("probt_turned")
        probt_ready = sem("probt_ready")
        av_ready = sem("av_ready")
        x2t_ready = sem("x2t_ready")
        x2_ready = sem("x2_ready")
        fc1_ready = sem("fc1_ready")
        hid_ready = sem("hid_ready")
        y_ready = sem("y_ready")
        router_ready = sem("router_ready")
        lsub_ready = sem("lsub_ready")
        lexp_ready = sem("lexp_ready")
        passed_ready = sem("passed_ready")
        pos_ready = sem("pos_ready")
        pos_counted = sem("pos_counted")
        wtok_ready = sem("wtok_ready")
        whi_ready = sem("whi_ready")
        dst_ready = sem("dst_ready")
        srow_ready = sem("srow_ready")
        srow2_ready = sem("srow2_ready")
        scattered = sem("scattered")

        small_max_ready = sem("small_max_ready")
        small_max_all_ready = sem("small_max_all_ready")
        cent1_ready = sem("cent1_ready")
        sq1_ready = sem("sq1_ready")
        vare1_ready = sem("vare1_ready")
        r12_step = sem("r12_step")
        r12_ready = sem("r12_ready")
        n1_ready = sem("n1_ready")
        n1_turned = sem("n1_turned")
        n1t_ready = sem("n1t_ready")
        u_ready = sem("u_ready")
        tok_used = sem("tok_used")
        ut_ready = sem("ut_ready")
        cent2_ready = sem("cent2_ready")
        sq2_ready = sem("sq2_ready")
        vare_c_ready = sem("vare_c_ready")
        rc_ready = sem("rc_ready")
        n2_ready = sem("n2_ready")
        n2hi_ready = sem("n2hi_ready")
        n2s_ready = sem("n2s_ready")
        n2_turned = sem("n2_turned")
        n2t_ready = sem("n2t_ready")
        t2_ready = sem("t2_ready")
        cent3_ready = sem("cent3_ready")
        sq3_ready = sem("sq3_ready")
        wt_turned = sem("wt_turned")
        wt_ready = sem("wt_ready")
        att_read = sem("att_read")
        sums_kept = sem("sums_kept")
        a_step, b_step, c_step, w_step = sem("a_step"), sem("b_step"), sem("c_step"), sem("w_step")

        x_rows = x.rearrange("b c h w -> (b c) (h w)")
        x_groups = x_rows.rearrange("(g s p) n -> g p s n", g=NG, s=2)

        block = ctx.enter_context(nc.Block())

        NSMALL = 18

        @block.sync
        def _(sp):
            flat = xg[:, :, :, :].rearrange("p s h w -> p s (h w)")
            sp.dma_start(bias2[0:C, :], conv_bias.rearrange("(c o) -> c o", o=1)).then_inc(small_loaded, 16)
            sp.dma_start(bias2[C:P, :], conv_bias.rearrange("(c o) -> c o", o=1)).then_inc(small_loaded, 16)
            sp.dma_start(g1[:, :], norm1_g.rearrange("(c o) -> c o", o=1)).then_inc(small_loaded, 16)
            sp.dma_start(diag_g1[:, C:C + 1], norm1_b.rearrange("(c o) -> c o", o=1)).then_inc(small_loaded, 16)
            for h in range(2):
                sp.dma_start(g2[h * C:(h + 1) * C, :], norm2_g.rearrange("(c o) -> c o", o=1))\
                    .then_inc(small_loaded, 16)
                sp.dma_start(fc1_n[h * C:(h + 1) * C, :], fc1_w).then_inc(small_loaded, 16)
            sp.dma_start(b2c[:, :], norm2_b.rearrange("(c o) -> c o", o=1)).then_inc(small_loaded, 16)
            sp.dma_start(proj[:, 0:C], q_w).then_inc(small_loaded, 16)
            rot_dst = proj[:, C:C + M].rearrange("c (h n) -> c h n", h=HASHES)
            sp.dma_start(rot_dst[:, :, 0:BUCKETS // 2], rotations.rearrange("o c h n -> (o c) h n")).then_inc(small_loaded, 16)
            sp.dma_start(proj[:, C + M:], kv_w).then_inc(small_loaded, 16)
            for a in range(2):
                sp.dma_start(fc1_bias0[:, a:a + 1], fc1_b[a * P:(a + 1) * P].rearrange("(p o) -> p o", o=1))\
                    .then_inc(small_loaded, 16)
            sp.dma_start(fc2_s[:, :, :], fc2_w.rearrange("(a p) c -> p a c", a=2)).then_inc(small_loaded, 16)
            for h in range(2):
                sp.dma_start(router_n[:, h * C:(h + 1) * C], router_w).then_inc(small_loaded, 16)
            sp.dma_start(fc2_bias[:, :], fc2_b.rearrange("(o c) -> o c", o=1).broadcast_to([P, C]))\
                .then_inc(small_loaded, 16)
            sp.wait_ge(consts_ready, 2)

            def iteration(a=None, b=None, c=None, d=None):
                if a is not None:
                    wait(sp, x_used, a)
                    sp.dma_start(flat, x_groups[ds(a, 1)].rearrange("g p s n -> (g p) s n")).then_inc(x_loaded, 16)
                if c is not None:
                    wait(sp, w_parts_ready, c)
                    for t, w in enumerate((w1, w3)):
                        we = w[ds(c, 1)].rearrange("e h c -> (e h) c")
                        sp.dma_start(wn[:, t, 0:CF, :], we[0:CF * P, :].rearrange("(p k) c -> p k c", k=CF))\
                            .then_inc(experts_loaded, 16)
                        sp.dma_start(wn[0:CR, t, CF, :], we[CF * P:HID, :]).then_inc(experts_loaded, 16)
                    wait(sp, w_turned, 4 * c)
                    w2e = w2[ds(c, 1)].rearrange("e c h -> (e c) h")
                    sp.dma_start(w2n[:, 0:HID], w2e).then_inc(w2_loaded, 16)

            pipeline(sp, iteration)
            sp.wait_ge(sched_ready, 1)
            sp.wait_ge(scattered, NG * 2 * NJ * 16)

            def write_pad(row):
                sp.dma_start(rows[ds(row, MT), :].rearrange("(h p) w -> p h w", h=2), pad[:, :, :])\
                    .then_inc(pads_written, 16)

            write_pad(NE * REG)
            for e in range(NE):
                write_pad(sp.value_load(pad_row[0:1, e:e + 1], min_val=0, max_val=NE * REG - MT))
            sp.wait_ge(pads_written, 16 * (NE + 1))

            def load(t, b):
                row = sp.value_load(tile_row[0:1, ds(t, 1)], min_val=0, max_val=NE * REG)
                sp.dma_start(xin[:, b, :, :], rows[ds(row, MT), :].rearrange("(h p) w -> p h w", h=2))\
                    .then_inc(xin_loaded[b], 16)

            load(0, 0)
            load(1, 1)
            with sp.Fori(0, (NT - 1) // 2) as k:
                for b in range(2):
                    sp.wait_ge(xt_turned, 2 * k + b + 1)
                    sp.wait_ge(route_ready, 2 * k + b + 1)
                    load(2 * k + b + 2, b)

            sp.wait_ge(y_scattered[0], 32 * ((NT + 1) // 2))
            sp.wait_ge(y_scattered[1], 32 * (NT // 2))
            res_v = results.rearrange("(k i s b f p) c -> i k s p f b c", k=2, i=NG, s=2, b=2, p=P)

            def load_results(i, b):
                for k in range(2):
                    for s in range(2):
                        for f in range(2):
                            src = res_v[ds(i, 1), k, s, :, f].rearrange("i p b c -> (i p) b c")
                            sp.dma_start(res[:, b, k, 4 * s + 2 * f:4 * s + 2 * f + 2, :], src)\
                                .then_inc(res_loaded[b], 16)

            load_results(0, 0)
            load_results(1, 1)
            with sp.Fori(0, NG // 2 - 1) as k:
                for b in range(2):
                    sp.wait_ge(t3_ready, 2 * k + b + 1)
                    load_results(2 * k + b + 2, b)

        @block.gpsimd
        def _(pool):
            step = [0]

            def then(ins):
                step[0] += 1
                ins.then_inc(consts_step, 1)
                pool.wait_ge(consts_step, step[0])

            g = nc.gpsimd
            g.memset(ones[:, :], 1.0).then_inc(consts_ready, 1)
            g.memset(ident[:, :], 0.0)
            g.memset(ident16[:, :], 0.0)
            g.memset(diag_g1[:, 0:C], 0.0)
            g.memset(pair_mean[:, :], 0.5)
            g.memset(before[:, :], 1.0)
            g.memset(head_of[:, :], 1.0)
            g.memset(v_mask[:, :, :], 1.0)
            g.memset(v_heads[:, :, :], 1.0)
            g.memset(scan_keep[:, :, :], 1.0)
            g.memset(q_aug[:, :], 0.0)
            g.memset(k_aug[:, :], 0.0)
            g.memset(c_mhalf[:, :], -0.5)
            g.memset(c_64th[:, :], 1.0 / C)
            g.memset(c_eps[:, :], EPS)
            g.memset(c_group[:, :, :], float(GT))
            g.memset(xpad[:, :, :, :], 0.0)
            g.memset(hsum[:, :, :, :], 0.0)
            g.memset(n1[:, :, C:C + 1], 1.0)
            then(g.memset(picked[:, :, 0:1], 0.0))
            for m in (ident, ident16):
                g.affine_select(out=m[:, :], in_=m[:, :], compare_op=ALU.not_equal, fill=1.0, base=0,
                                pattern=[[-1, P]], channel_multiplier=1)
            pm = pair_mean[:, :].rearrange("p (a b) -> p a b", b=2)
            then(g.affine_select(out=pm, in_=pm, compare_op=ALU.is_ge, fill=0.0, base=0,
                                 pattern=[[-2, C], [0, 2]], channel_multiplier=1))
            g.affine_select(out=pm, in_=pm, compare_op=ALU.is_ge, fill=0.0, base=1,
                            pattern=[[2, C], [0, 2]], channel_multiplier=-1)
            g.affine_select(out=before[:, :], in_=before[:, :], compare_op=ALU.is_gt, fill=0.0, base=0,
                            pattern=[[1, P]], channel_multiplier=-1)
            hc = head_of[0:C, :]
            g.affine_select(out=hc, in_=hc, compare_op=ALU.is_ge, fill=0.0, base=0,
                            pattern=[[-DH, HEADS]], channel_multiplier=1)
            vm = v_mask[:, :, :].rearrange("p a (h d) -> p a h d", h=HEADS)
            g.affine_select(out=vm, in_=vm, compare_op=ALU.is_ge, fill=0.0, base=0,
                            pattern=[[P, 2], [-M, HEADS], [0, DH]], channel_multiplier=1)
            then(g.affine_select(out=v_heads[:, :, :], in_=v_heads[:, :, :], compare_op=ALU.is_ge, fill=0.0,
                                 base=0, pattern=[[P, 2], [-M, HEADS]], channel_multiplier=1))
            g.affine_select(out=hc, in_=hc, compare_op=ALU.is_ge, fill=0.0, base=DH - 1,
                            pattern=[[DH, HEADS]], channel_multiplier=-1)
            g.affine_select(out=vm, in_=vm, compare_op=ALU.is_ge, fill=0.0, base=M - 1,
                            pattern=[[-P, 2], [M, HEADS], [0, DH]], channel_multiplier=-1)
            then(g.affine_select(out=v_heads[:, :, :], in_=v_heads[:, :, :], compare_op=ALU.is_ge, fill=0.0,
                                 base=M - 1, pattern=[[-P, 2], [M, HEADS]], channel_multiplier=-1))
            for b in range(GB):
                g.tensor_copy(vblk[:, b, :, C:C + HEADS], v_heads[:, :, :])
            g.affine_select(out=scan_keep[:, :, :], in_=scan_keep[:, :, :], compare_op=ALU.not_equal, fill=0.0,
                            base=0, pattern=[[0, NE], [1, NJ + 1]], channel_multiplier=0)
            g.affine_select(out=q_aug[:, C:C + 1], in_=q_aug[:, C:C + 1], compare_op=ALU.not_equal, fill=1.0,
                            base=-C, pattern=[[0, 1]], channel_multiplier=1)
            g.affine_select(out=k_aug[:, C:C + 1], in_=k_aug[:, C:C + 1], compare_op=ALU.not_equal, fill=1.0,
                            base=-(C + 1), pattern=[[0, 1]], channel_multiplier=1)
            g.iota(descend[:, :], [[-1, BUCKETS]], base=BUCKETS, channel_multiplier=0,
                   allow_small_or_imprecise_dtypes=True)
            g.iota(region[:, :, :], [[REG // MT, NE], [0, NJ]], base=0, channel_multiplier=0,
                   allow_small_or_imprecise_dtypes=True)
            for k in range(2):
                for s in range(2):
                    for f in range(2):
                        j = 4 * s + 2 * f
                        g.iota(srow[:, k, j:j + 2, ROW - 1:ROW].rearrange("p b o -> p (b o)"), [[N, 2]],
                               base=k * T + 2 * s * N + f * P - GT, channel_multiplier=1,
                               allow_small_or_imprecise_dtypes=True)
            g.memset(wn[:, :, CF, :], 0.0)
            g.memset(w2n[:, HID:CH * P], 0.0)
            g.memset(pad[:, :, :], 0.0)
            for m, n in ((k_rows, T // MT), (g_no, NS), (e_no, NE)):
                g.iota(m[:, :], [[1, n]], base=0, channel_multiplier=0, allow_small_or_imprecise_dtypes=True)
            then(g.memset(r1[:, :], 0.0))
            g.memset(pad[:, :, ROW - 1:ROW], float(DUMP))
            g.tensor_scalar(g_row[:, :], g_no[:, :], float(MT), None, ALU.mult)
            g.tensor_scalar(k_rows[:, :], k_rows[:, :], float(MT), None, ALU.mult)
            g.tensor_scalar(region[:, :, :], region[:, :, :], float(MT), None, ALU.mult)
            pool.wait_ge(small_loaded, 16 * NSMALL)
            g.tensor_tensor(diag_g1[:, 0:C], ident[0:C, 0:C], g1[:, 0:1].broadcast_to([C, C]), ALU.mult)
            rot = proj[:, C:C + M].rearrange("c (h n) -> c h n", h=HASHES)
            g.tensor_scalar(rot[:, :, BUCKETS // 2:], rot[:, :, 0:BUCKETS // 2], -1.0, None, ALU.mult)\
                .then_inc(consts_ready, 1)

            pool.wait_ge(small_max_ready, 1)
            pool.sem_inc(waited, 1)
            g.partition_all_reduce(small_max_all[:, :], small_max[:, :], P, bass.bass_isa.ReduceOp.max)\
                .then_inc(small_max_all_ready, 1)

            def group_rstd(a):
                pool.wait_ge(gvar_ready, a + 1)
                g.tensor_tensor(grstd[:, :], gvar[:, :], c_mhalf[:, 0:2], ALU.pow).then_inc(grstd_ready, 1)

            def token_rstd(a):
                n = 0

                def step_done(ins):
                    nonlocal n
                    n += 1
                    ins.then_inc(r12_step, 1)
                    pool.wait_ge(r12_step, a * 5 + n)

                pool.wait_ge(vare1_ready, a + 1)
                step_done(g.tensor_tensor(r1[:, :], vare_a[:, :], c_mhalf[:, :], ALU.pow))
                step_done(g.tensor_tensor(r1sq[:, :], r1[:, :], r1[:, :], ALU.mult))
                step_done(g.tensor_tensor(uvar[:, :], r1sq[:, :], v64[:, :], ALU.mult))
                step_done(g.tensor_tensor(uvare[:, :], uvar[:, :], c_eps[:, :], ALU.add))
                step_done(g.tensor_tensor(r2[:, :], uvare[:, :], c_mhalf[:, :], ALU.pow))
                g.tensor_tensor(r12[:, :], r1[:, :], r2[:, :], ALU.mult).then_inc(r12_ready, 1)

            def late_rstd(c, k):
                pool.wait_ge(vare_c_ready, 2 * c + k)
                g.tensor_tensor(rc[:, :], vare_c[:, :], c_mhalf[:, :], ALU.pow).then_inc(rc_ready, 1)

            def residual(b):
                pool.wait_ge(att_read, 2 * b + 2)
                wait(pool, t2_ready, b)
                g.tensor_tensor(x2t[:, :, :].rearrange("p j c -> p (j c)"),
                                u_tok[:, :, :].rearrange("p j c -> p (j c)"),
                                att[:, :, :, :].rearrange("p s j c -> p (s j c)"), ALU.add).then_inc(x2t_ready, 1)

            def token_sum(a):
                pool.wait_ge(tok_ready, a + 1)
                wait(pool, x2t_ready, a)
                g.tensor_tensor(u_tok[:, :, :], tok[:, :, :],
                                fc2_bias[:, :].unsqueeze(1).broadcast_to([P, NJ, C]), ALU.add).then_inc(tok_used, 1)
                pool.wait_ge(tok_used, a + 1)
                pool.wait_ge(u_ready, a + 1)
                g.tensor_tensor(u_tok[:, :, :], u_tok[:, :, :], u[:, :, :], ALU.add).then_inc(ut_ready, 1)

            def complete_rows(c):
                wait(pool, scattered, c * 2 * NJ * 16)
                dst = srow[:, :, :, ROW - 1]
                g.tensor_tensor(dst, dst, c_group[:, :, :], ALU.add).then_inc(dst_ready, 1)
                pool.wait_ge(srow_ready, c + 1)
                pool.sem_inc(waited, 1)
                g.tensor_copy(srow[:, 1, :, 0:C], srow[:, 0, :, 0:C]).then_inc(srow2_ready, 1)

            def scatter(c, tiles_):
                pool.wait_ge(srow2_ready, c + 1)
                pool.wait_ge(pos_ready, c + 1)
                pool.sem_inc(waited, 1)
                for j in tiles_:
                    for k in range(2):
                        g.indirect_dma_start(
                            rows[0:NE * REG, :], bass.IndirectOffsetOnAxis(ap=pos[:, k, j:j + 1], axis=0),
                            srow[:, k, j, :], None).then_inc(scattered, 16)

            def largest_weight(c):
                pool.wait_ge(w_max_ready, c + 1)
                pool.sem_inc(waited, 1)
                g.partition_all_reduce(wmax_all[:, :], wmax[:, :], P, bass.bass_isa.ReduceOp.max)\
                    .then_inc(w_max_all, 1)

            def iteration(a=None, b=None, c=None, d=None):
                run(c, late_rstd, 1)
                run(d, scatter, (4,))
                run(a, group_rstd)
                run(c, largest_weight)
                run(d, scatter, (5, 6, 7))
                run(c, late_rstd, 2)
                run(a, token_rstd)
                run(c, complete_rows)
                run(b, residual)
                run(a, token_sum)
                run(c, scatter, (0, 1, 2, 3))

            pipeline(pool, iteration)

            def take_route(nth, b, free=None):
                pool.wait_ge(xin_loaded[b], 16 * (nth + 1))
                if free is not None:
                    pool.wait_ge(yout_ready[b], free)
                pool.sem_inc(waited, 1)
                g.tensor_copy(route[:, b, :, :], xin[:, b, :, C:C + 2]).then_inc(route_ready, 1)

            def store(nth, b):
                pool.wait_ge(yout_ready[b], nth + 1)
                pool.sem_inc(waited, 1)
                for h in range(2):
                    g.indirect_dma_start(
                        results[:, :], bass.IndirectOffsetOnAxis(ap=dest[:, b, h:h + 1], axis=0),
                        yout[:, b, h, :], None, bounds_check=DUMP - 1, oob_is_err=False)\
                        .then_inc(y_scattered[b], 16)

            take_route(0, 0)
            take_route(0, 1)
            with pool.Fori(0, (NT - 1) // 2) as k:
                take_route(k + 1, 0, k + 1)
                store(k, 0)
                take_route(k + 1, 1, k + 1)
                store(k, 1)
            store((NT - 1) // 2, 0)


        @block.tensor
        def _(pe):
            mm = nc.tensor.matmul
            turn = nc.tensor.transpose
            pe.wait_ge(consts_ready, 2)
            mm(bk12[0:C + 1, 0, 0:C + M + 2 * C], diag_g1[:, :], proj[:, :], start=True, stop=True)
            for a in range(2):
                mm(bk12[:, 1, a:a + 1], fc1_n[0:C, a * P:(a + 1) * P], b2c[:, :], start=True, stop=True)
            turn(bk12[:, 1, 8:8 + NE], router_n[:, :], ident[0:NE, 0:NE]).then_inc(pe_setup, 1)
            pe.wait_ge(dve_setup, DVE_SETUP)

            def pair_means(a):
                wait(pe, n1t_ready, 2 * a)
                pe.wait_ge(mean_ready, a + 1)
                mm(gmean_ps, pair_mean[:, :], mv[:, :, 0], start=True, stop=True).then_inc(gmean_ready, 1)

            def pair_variances(a):
                pe.wait_ge(chvar_ready, a + 1)
                mm(gvar_ps, pair_mean[:, :], chvar[:, :], start=True, stop=True).then_inc(gvar_done, 1)

            def convolution(a):
                pe.wait_ge(conv_ready, a + 1)
                for s in range(2):
                    for f in range(2):
                        o = t_ps[:, (2 * s + f) * P:(2 * s + f + 1) * P]
                        h0 = f * HH // 2
                        mm(o, xres[:, s, h0:h0 + 8, :], ident[:, :], start=True, stop=False)
                        for dy in range(3):
                            last = mm(o, hsum[:, s, h0 + dy:h0 + dy + 8, :], ident[:, :], start=False, stop=dy == 2)
                last.then_inc(t_ready, 1)

            def turn_n1(a):
                pe.wait_ge(n1_ready, a + 1)
                for h in range(2):
                    if h == 1:
                        pe.wait_ge(n1t_ready, 2 * a + 1)
                    for j in range(4):
                        last = turn(bk0[0:C + 1, j * P:(j + 1) * P], n1[:, 4 * h + j, :], ident[:, :])
                    last.then_inc(n1_turned, 1)

            def rotate(a):
                pe.wait_ge(n1t_ready, 2 * a + 2)
                wait(pe, att_read, 2 * a)
                for j in range(NJ):
                    last = mm(rot_ps[:, j * M:(j + 1) * M], n1t[:, j * P:(j + 1) * P], rot_aug[:, :],
                              start=True, stop=True)
                last.then_inc(rot_ready, 1)

            def queries(a):
                wait(pe, probt_ready, 4 * a)
                for h in range(2):
                    last = mm(bk34[0:C + 1, h, :], q_aug[:, :], n1t[:, h * 512:(h + 1) * 512], start=True, stop=True)
                last.then_inc(q_ready, 1)

            def bucket_sums(b):
                pe.wait_ge(onehot_ready, b + 1)
                oh_v = onehot[:, :, :].rearrange("p (j h) k -> p j (h k)", j=NJ)
                for m in range(GB):
                    for f in range(2):
                        j = 4 * (m // 2) + 2 * f + m % 2
                        last = mm(pool_ps[M * m:M * (m + 1), :], oh_v[:, j, :], n1[:, j, :],
                                  start=f == 0, stop=f == 1)
                last.then_inc(pool_ready, 1)

            def turn_pooled(b):
                pe.wait_ge(pooled_ready, b + 1)
                turn(poolt_ps, pooled[:, :], ident[:, :]).then_inc(poolt_ready, 1)

            def keys_values(b):
                pe.wait_ge(pooledt_ready, b + 1)
                pe.wait_ge(qt_ready, b + 1)
                mm(k_ps, k_aug[:, :], pooled_t[:, :], start=True, stop=True)
                pe.wait_ge(rep_ready, b + 1)
                for m in range(GB):
                    last = mm(v_ps[:, m, :], pooled_rep[:, m, :, :].rearrange("c h m -> c (h m)"), v_aug[:, :],
                              start=True, stop=True)
                last.then_inc(kv_ready, 1)

            def scores(b, p):
                if p == 0:
                    pe.wait_ge(blk_ready, b + 1)
                if p >= 2:
                    pe.wait_ge(ssub_ready, 4 * b + p - 1)
                for bp in range(2):
                    j, m = 2 * p + bp, 2 * (p // 2) + bp
                    last = mm(bk12[:, p % 2, bp * 256:(bp + 1) * 256], qt[:, j * P:(j + 1) * P],
                              kblk[:, m, :, :].rearrange("c h m -> c (h m)"), start=True, stop=True)
                last.then_inc(s_ready, 1)

            def turn_prob(b, p):
                pe.wait_ge(prob_ready, 4 * b + p + 1)
                wait(pe, probt_ready, 4 * b + p - 1)
                for a in range(4):
                    last = turn(bk34[:, p % 2, a * P:(a + 1) * P], prob[:, p % 2, a, :], ident[:, :])
                last.then_inc(probt_turned, 1)

            def attend(b, p):
                pe.wait_ge(probt_ready, 4 * b + p + 1)
                if p == 2:
                    pe.wait_ge(att_read, 2 * b + 1)
                for bp in range(2):
                    m = 2 * (p // 2) + bp
                    for ch in range(2):
                        last = mm(av_ps[:, 2 * (p % 2) + bp, :], prob_t[:, p % 2, 2 * bp + ch, :],
                                  vblk[:, m, ch, :], start=ch == 0, stop=ch == 1)
                last.then_inc(av_ready, 1)

            def turn_n2(c):
                pe.wait_ge(n2s_ready, c + 1)
                wait(pe, w_stored_act, 2 * c)
                wait(pe, w_stored_dve, 2 * c)
                for j in range(NJ):
                    last = turn(bk6.bitcast(F16)[:, j * P:(j + 1) * P], n2s[:, j, :], ident16[:, :])
                last.then_inc(n2_turned, 1)

            def fc1(c):
                pe.wait_ge(n2t_ready, c + 1)
                for q in range(4):
                    h, a = q // 2, q % 2
                    if q >= 2:
                        pe.wait_ge(hid_ready, 4 * c + q - 1)
                    for part in range(2):
                        last = mm(fc1_ps[a], fc1_p[:, part, a * P:(a + 1) * P], n2t[:, h * 512:(h + 1) * 512],
                                  start=part == 0, stop=part == 1)
                    last.then_inc(fc1_ready, 1)

            def fc2(c):
                for j in range(NJ):
                    if j % 4 == 0:
                        pe.wait_ge(hid_ready, 4 * c + 3 + j // 4)
                    for a in range(2):
                        last = mm(y_ps[:, j, :], hid[:, a, j * P:(j + 1) * P], fc2_s[:, a, :],
                                  start=a == 0, stop=a == 1)
                last.then_inc(y_ready, 1)

            def turn_wtok(c):
                pe.wait_ge(srow_ready, c + 1)
                for j in range(NJ):
                    last = turn(bk6.bitcast(F16)[:, j * P:(j + 1) * P], srow[:, 0, j, 0:C].bitcast(F16),
                                ident16[:, :])
                last.then_inc(wt_turned, 1)

            def router(c):
                pe.wait_ge(wt_ready, c + 1)
                for j in range(NJ):
                    for part in range(2):
                        last = mm(l_ps[:, j, :], wtok_t[:, j * P:(j + 1) * P], router_p[:, part, :],
                                  start=part == 0, stop=part == 1)
                last.then_inc(router_ready, 1)

            def places(c):
                pe.wait_ge(passed_ready, c + 1)
                mm(pos_ps, before[:, :], picked[:, :, 1:NJ + 1], start=True, stop=False)
                mm(pos_ps, ones[:, :], passed[:, :, 0:NJ], start=False, stop=True).then_inc(pos_counted, 1)

            def turn_weights(c, part):
                if part == 0:
                    pe.wait_ge(w_parts_ready, c + 1)
                if part == 1:
                    pe.wait_ge(pos_ready, c + 1)
                if part >= 2:
                    pe.wait_ge(w_stored_act, 2 * c + part - 1)
                if part == 3:
                    pe.wait_ge(w2_loaded, 16 * c + 16)
                    pe.sem_inc(waited, 1)
                    for ch in range(CH):
                        src = w2n[:, ch:CF * P:CF] if ch < CF else w2n[:, CF * P:CH * P]
                        last = turn(bk7[:, ch * C:(ch + 1) * C], src, ident[0:C, 0:C])
                else:
                    pe.sem_inc(waited, 1)
                    for q in range(8 * part, 8 * part + 8):
                        t, ch, low = q // (2 * CH), q // 2 % CH, q % 2
                        for copy in range(2):
                            last = turn(w_turn_ps[part][copy * C:(copy + 1) * C, (q % 8) * P:(q % 8 + 1) * P],
                                        (w_hi, w_lo)[low][:, t, ch, :], ident16[:, :])
                last.then_inc(w_turned, 1)

            def iteration(a=None, b=None, c=None, d=None):
                run(b, bucket_sums)
                run(a, pair_means)
                run(b, turn_pooled)
                run(a, pair_variances)
                run(b, keys_values)
                run(c, turn_n2)
                run(b, scores, 0)
                run(b, scores, 1)
                run(c, fc1)
                run(a, convolution)
                run(b, turn_prob, 0)
                run(b, scores, 2)
                run(c, fc2)
                run(b, turn_prob, 1)
                run(b, scores, 3)
                run(b, attend, 0)
                run(b, attend, 1)
                run(b, turn_prob, 2)
                run(b, turn_prob, 3)
                run(b, attend, 2)
                run(a, turn_n1)
                run(c, turn_wtok)
                run(b, attend, 3)
                run(c, router)
                run(a, rotate)
                run(a, queries)
                run(c, turn_weights, 0)
                run(c, places)
                for part in (1, 2, 3):
                    run(c, turn_weights, part)

            pipeline(pe, iteration)

            pe.wait_ge(sums_kept, NG)
            pe.wait_ge(w_stored_act, 2 * NG)
            pe.wait_ge(w_stored_dve, 2 * NG)
            mm(bk7[:, 0:NE], ones[:, :], picked[:, :, 0], start=True, stop=True).then_inc(counted, 1)
            pe.wait_ge(sched_ready, 1)
            xt_ps = bk7[:, :].bitcast(F16)

            def turn_rows(t, b, nth):
                pe.wait_ge(xin_loaded[b], 16 * (nth + 1))
                wait(pe, xs_ready, t)
                for h in range(2):
                    last = turn(xt_ps[:, h * P:(h + 1) * P], xin[:, b, h, 0:C].bitcast(F16), ident16[:, :])
                last.then_inc(xt_turned, 1)

            def expert_of(t):
                return pe.value_load(tile_expert[0:1, ds(t, 1)], min_val=0, max_val=NE - 1)

            def up(t, b, e, between):
                pe.wait_ge(xs_ready, t + 1)
                for q in range(CH // 2):
                    m = (3 * b + q) % 2
                    for w, bank, free, ready in ((0, bk12, silu_ready, h1_ready), (1, bk34, h_ready, h3_ready)):
                        wait(pe, free, 3 * t + q - 1)
                        for ch in range(2):
                            for part in range(2):
                                last = mm(bank[:, m, ch * MT:(ch + 1) * MT],
                                          w13[:, ds(e, 1), w, 2 * q + ch, part, :].rearrange("p o n -> p (o n)"),
                                          xs[:, b, :], start=part == 0, stop=part == 1)
                        last.then_inc(ready, 1)
                    if between is not None and q > 0:
                        between(q - 1)

            def down(t, b, nth, e, h):
                if h == 0:
                    pe.wait_ge(h_ready, 3 * t + 3)
                    wait(pe, yout_ready[b], nth)
                for ch in range(CH):
                    last = mm(bk56[:, b, h * C:(h + 1) * C], hbuf[:, b, ch, h * P:(h + 1) * P],
                              w2s[:, ds(e, 1), ch, :].rearrange("p o n -> p (o n)"),
                              start=ch == 0, stop=ch == CH - 1)
                if h == 1:
                    last.then_inc(e_y_ready, 1)

            turn_rows(0, 0, 0)
            turn_rows(1, 1, 0)
            up(0, 0, expert_of(0), None)

            def two_tiles(k):
                e = [expert_of(2 * k + a) for a in range(3)]
                turn_rows(2 * k + 2, 0, k + 1)
                up(2 * k + 1, 1, e[1], lambda h: down(2 * k, 0, k, e[0], h))
                turn_rows(2 * k + 3, 1, k + 1)
                up(2 * k + 2, 0, e[2], lambda h: down(2 * k + 1, 1, k, e[1], h))

            first_then_loop(pe, (NT - 1) // 2, two_tiles)
            e = expert_of(NT - 1)
            for h in range(2):
                down(NT - 1, 0, (NT - 1) // 2, e, h)

            def turn_output(k):
                for b in range(2):
                    pe.wait_ge(t3_ready, 2 * k + b + 1)
                    wait(pe, og_ready[b], k)
                    for a in range(4):
                        last = turn(bk12[:, b, a * P:(a + 1) * P], t3[:, b, 2 * a:2 * a + 2, :], ident[:, :])
                    last.then_inc(o_turned[b], 1)

            first_then_loop(pe, NG // 2, turn_output)

        @block.scalar
        def _(act):
            f = nc.scalar.activation
            act.wait_ge(consts_ready, 1)
            def store_tokens(a):
                act.wait_ge(t_ready, a + 1)
                wait(act, tok_used, a)
                f(tok[:, :, :], t_ps.rearrange("p (j c) -> p j c", j=NJ), ACT.Copy).then_inc(tok_ready, 1)

            def squares1(a):
                act.wait_ge(cent1_ready, a + 1)
                f(sq_a[:, :, :], cent_a[:, :, :], ACT.Square).then_inc(sq1_ready, 1)

            def store_n1t(a, h):
                act.wait_ge(n1_turned, 2 * a + h + 1)
                f(n1t[:, h * 512:(h + 1) * 512], bk0[0:C + 1, :], ACT.Copy).then_inc(n1t_ready, 1)

            def store_queries(a):
                act.wait_ge(q_ready, a + 1)
                f(qt[:, :], bk34[0:C + 1, :, :].rearrange("c a n -> c (a n)"), ACT.Copy).then_inc(qt_ready, 1)

            def repeat_pooled(b):
                act.wait_ge(pooledt_ready, b + 1)
                for m in range(GB):
                    ins = f(pooled_rep[:, m, :, :],
                            pooled_t[0:C + 1, M * m:M * (m + 1)].unsqueeze(1).broadcast_to([C + 1, 4, M]), ACT.Copy)
                ins.then_inc(rep_ready, 1)

            def exponentials(b, p):
                act.wait_ge(ssub_ready, 4 * b + p + 1)
                wait(act, probt_turned, 4 * b + p - 1)
                f(prob[:, p % 2, :, :].rearrange("p a n -> p (a n)"),
                  ssub[:, p % 2, :, :].rearrange("p h m -> p (h m)"), ACT.Exp, scale=DH ** -0.5)\
                    .then_inc(prob_ready, 1)

            def store_prob(b, p):
                act.wait_ge(probt_turned, 4 * b + p + 1)
                wait(act, av_ready, 4 * b + p - 1)
                f(prob_t[:, p % 2, :, :].rearrange("p a n -> p (a n)"), bk34[:, p % 2, :], ACT.Copy)\
                    .then_inc(probt_ready, 1)

            def squares2(b):
                act.wait_ge(cent2_ready, b + 1)
                f(sq_c[:, :, :], cent_c[:, :, :], ACT.Square).then_inc(sq2_ready, 1)

            def high_n2(c):
                act.wait_ge(n2_ready, c + 1)
                f(n2s[:, :, 0:C], n2[:, :, :], ACT.Copy, scale=XS).then_inc(n2hi_ready, 1)

            def store_n2t(c):
                act.wait_ge(n2_turned, c + 1)
                f(n2t, bk6.bitcast(F16), ACT.Copy).then_inc(n2t_ready, 1)

            def gelus(c):
                back = small_back[:, 0:1].bitcast(F32)
                for q in range(4):
                    h, a = q // 2, q % 2
                    act.wait_ge(fc1_ready, 4 * c + q + 1)
                    f(hid[:, a, h * 512:(h + 1) * 512], fc1_ps[a], ACT.Gelu, bias=fc1_bias[:, a:a + 1], scale=back)\
                        .then_inc(hid_ready, 1)

            def squares3(c):
                act.wait_ge(cent3_ready, c + 1)
                f(sq_c[:, :, :], cent_c[:, :, :], ACT.Square).then_inc(sq3_ready, 1)

            def high_wtok(c):
                act.wait_ge(wtok_ready, c + 1)
                wait(act, scattered, c * 2 * NJ * 16)
                hi = srow[:, 0, :, 0:C // 2].bitcast(F16)
                f(hi, wtok[:, :, :], ACT.Copy, scale=XS).then_inc(whi_ready, 1)

            def store_wtok(c):
                act.wait_ge(wt_turned, c + 1)
                f(wtok_t, bk6.bitcast(F16), ACT.Copy).then_inc(wt_ready, 1)

            def router_exp(c):
                act.wait_ge(lsub_ready, c + 1)
                f(lexp[:, :, :], lsub[:, :, :], ACT.Exp, scale=small_back[:, 1:2].bitcast(F32)).then_inc(lexp_ready, 1)

            def high_weights(c):
                act.wait_ge(w_scale_ready, c + 1)
                wait(act, w_turned, 4 * c)
                for t in range(2):
                    f(w_hi[:, t, :, :].rearrange("p k c -> p (k c)"), wn[:, t, :, :].rearrange("p k c -> p (k c)"),
                      ACT.Copy, scale=wscale[:, t:t + 1].bitcast(F32)).then_inc(w_hi_ready, 1)

            def store_weights(c, part):
                act.wait_ge(w_turned, 4 * c + part + 1)
                act.sem_inc(waited, 1)
                f(w13_q[:, ds(c, 1), 8 * part:8 * part + 8, :].rearrange("p o q n -> p (o q n)"),
                  w_turn_ps[part], ACT.Copy).then_inc(w_stored_act, 1)

            def iteration(a=None, b=None, c=None, d=None):
                run(b, repeat_pooled)
                run(c, high_n2)
                run(c, store_n2t)
                run(c, gelus)
                run(b, exponentials, 0)
                run(a, store_tokens)
                run(b, exponentials, 1)
                run(b, store_prob, 0)
                run(c, squares3)
                run(b, store_prob, 1)
                run(a, squares1)
                run(b, exponentials, 2)
                run(b, exponentials, 3)
                run(b, store_prob, 2)
                run(b, store_prob, 3)
                run(c, high_wtok)
                run(a, store_n1t, 0)
                run(a, store_n1t, 1)
                run(c, store_wtok)
                run(c, router_exp)
                run(b, squares2)
                run(c, high_weights)
                run(a, store_queries)
                run(c, store_weights, 0)
                run(c, store_weights, 1)

            pipeline(act, iteration)

            act.wait_ge(sched_ready, 2)

            def store_xs(t, b):
                act.wait_ge(xt_turned, t + 1)
                wait(act, h3_ready, 3 * t - 3)
                f(xs[:, b, :], bk7[:, :].bitcast(F16)[:, 0:MT], ACT.Copy).then_inc(xs_ready, 1)

            def silus(t, b):
                back = tile_back[:, ds(t, 1), 0:1].rearrange("p o n -> p (o n)")
                for q in range(CH // 2):
                    m = (3 * b + q) % 2
                    act.wait_ge(h1_ready, 3 * t + q + 1)
                    wait(act, h_ready, 3 * t + q - 1)
                    act.sem_inc(waited, 1)
                    f(silu[:, m, :], bk12[:, m, :], ACT.Silu, scale=back).then_inc(silu_ready, 1)

            store_xs(0, 0)
            store_xs(1, 1)
            silus(0, 0)
            with act.Fori(0, (NT - 1) // 2) as k:
                store_xs(2 * k + 2, 0)
                silus(2 * k + 1, 1)
                store_xs(2 * k + 3, 1)
                silus(2 * k + 2, 0)

            out_rows = out.rearrange("b c h w -> (b c) (h w)").rearrange("(g s p) n -> g p s n", g=NG, s=2)

            def store_output(k):
                for b in range(2):
                    act.wait_ge(o_turned[b], k + 1)
                    wait(act, out_stored[b], 16 * k)
                    f(og[:, b, :], bk12[:, b, :], ACT.Copy).then_inc(og_ready[b], 1)
                    act.wait_ge(og_ready[b], k + 1)
                    act.dma_start(out_rows[ds(2 * k + b, 1)].rearrange("g p s n -> (g p) s n"),
                                  og[:, b, :].rearrange("p (s n) -> p s n", s=2)).then_inc(out_stored[b], 16)

            first_then_loop(act, NG // 2, store_output)
            for b in range(2):
                act.wait_ge(out_stored[b], 16 * (NG // 2))

        @block.vector
        def _(dve):
            v = nc.vector
            tt = v.tensor_tensor

            def wide(col, n):
                return col.unsqueeze(2).broadcast_to([col.shape[0], col.shape[1], n])

            setup = [0]

            def setup_done(ins, wait=True):
                setup[0] += 1
                ins.then_inc(dve_setup, 1)
                if wait:
                    dve.wait_ge(dve_setup, setup[0])

            dve.wait_ge(pe_setup, 1)
            setup_done(v.tensor_copy(q_aug[:, 0:C], bk12[0:C + 1, 0, 0:C]), wait=False)
            setup_done(v.tensor_copy(rot_aug[:, :], bk12[0:C + 1, 0, C:C + M]), wait=False)
            setup_done(v.tensor_copy(k_aug[0:C + 1, 0:C], bk12[0:C + 1, 0, C + M:2 * C + M]), wait=False)
            setup_done(v.tensor_copy(v_aug[:, :], bk12[0:C + 1, 0, 2 * C + M:3 * C + M]), wait=False)
            setup_done(v.tensor_copy(router_t[:, :], bk12[:, 1, 8:8 + NE]), wait=False)
            setup_done(v.tensor_scalar(fc1_s[:, :], fc1_n[:, :], g2[:, 0:1], None, ALU.mult), wait=False)
            setup_done(tt(fc1_bias[:, :], bk12[:, 1, 0:2], fc1_bias0[:, :], ALU.add))

            def scales(largest, exponent, scale, back, step_done):
                step_done(v.tensor_scalar(largest, largest, TINY, None, ALU.max))
                step_done(v.tensor_scalar(exponent, largest.bitcast(U32), EXP_MASK, None, ALU.bitwise_and))
                v.tensor_scalar(back, exponent, float(-BACK_EXP << 23), None, ALU.add)
                return v.tensor_scalar(scale, exponent, -1.0, float(SCALE_EXP << 23), ALU.mult, ALU.add)

            biggest = dict(axis=AX.X, op=ALU.max, apply_absolute_value=True)
            v.tensor_reduce(small_max[:, 0:1], fc1_s[:, :], **biggest)
            v.tensor_reduce(small_max[:, 1:2], router_t[:, :], **biggest).then_inc(small_max_ready, 1)
            dve.wait_ge(small_max_all_ready, 1)
            setup_done(scales(small_max_all[:, :], wexp[:, :], small_scale[:, :], small_back[:, :], setup_done))
            for m, (full, parts) in enumerate(((fc1_s, fc1_p), (router_t, router_p))):
                by = small_scale[:, m:m + 1].bitcast(F32)
                setup_done(v.tensor_scalar(parts[:, 0, :], full[:, :], by, None, ALU.mult))
                setup_done(v.scalar_tensor_tensor(out=parts[:, 1, :], in0=full[:, :], scalar=by, in1=parts[:, 0, :],
                                                  op0=ALU.mult, op1=ALU.subtract))
            assert setup[0] == DVE_SETUP

            step_sem = dict(a=a_step, b=b_step, c=c_step, w=w_step)
            count = {}

            def chained(stage, group):
                def done(ins):
                    count[stage] += 1
                    ins.then_inc(step_sem[stage], 1)
                    dve.wait_ge(step_sem[stage], group * STEPS[stage] + count[stage])
                return done

            def channel_statistics(a):
                done = chained("a", a)
                dve.wait_ge(x_loaded, 16 * a + 16)
                xf = xg[:, :, :, :].rearrange("p s h w -> p s (h w)")
                v.bn_stats(bst[:, 0, :], xf[:, 0, :])
                done(v.bn_stats(bst[:, 1, :], xf[:, 1, :]))
                dve.sem_inc(waited, 1)
                v.bn_aggr(mv[:, 0, :], bst[:, 0, :])
                v.bn_aggr(mv[:, 1, :], bst[:, 1, :]).then_inc(mean_ready, 1)

            def channel_variances(a):
                done = chained("a", a)
                dve.wait_ge(mean_ready, a + 1)
                dve.wait_ge(gmean_ready, a + 1)
                done(tt(dmean[:, :], mv[:, :, 0], gmean_ps, ALU.subtract))
                done(tt(dmean2[:, :], dmean[:, :], dmean[:, :], ALU.mult))
                tt(chvar[:, :], dmean2[:, :], mv[:, :, 1], ALU.add).then_inc(chvar_ready, 1)

            def pair_statistics(a):
                done = chained("a", a)
                dve.wait_ge(gvar_done, a + 1)
                v.tensor_scalar(gvar[:, :], gvar_ps, EPS, None, ALU.add).then_inc(gvar_ready, 1)
                done(v.tensor_copy(gmean[:, :], gmean_ps))

            def row_sums(a):
                done = chained("a", a)
                dve.wait_ge(grstd_ready, a + 1)
                for s in range(2):
                    ins = v.tensor_scalar(xpad[:, s, 1:HH + 1, 1:WW + 1], xg[:, s, :, :], gmean[:, s:s + 1],
                                          grstd[:, s:s + 1], ALU.subtract, ALU.mult)
                done(ins)
                inner = xpad[:, :, 1:HH + 1, :]
                hin = hsum[:, :, 1:HH + 1, :]
                tt(hin, inner[:, :, :, 0:WW], inner[:, :, :, 1:WW + 1], ALU.add)
                for s in range(2):
                    ins = v.scalar_tensor_tensor(out=xres[:, s, :, :], in0=xg[:, s, :, :], scalar=bias2[:, 0:1],
                                                 in1=xpad[:, s, 1:HH + 1, 1:WW + 1], op0=ALU.add, op1=ALU.add)
                ins.then_inc(x_used, 1)
                dve.wait_ge(x_used, a + 1)
                tt(hin, hin, inner[:, :, :, 2:WW + 2], ALU.add).then_inc(conv_ready, 1)

            def centre_tokens(done, src, ssum, cent, ready):
                done(v.tensor_reduce(ssum[:, :], src, AX.X, ALU.add))
                v.scalar_tensor_tensor(out=cent[:, :, :], in0=wide(ssum[:, :], C), scalar=-1.0 / C, in1=src,
                                       op0=ALU.mult, op1=ALU.add).then_inc(ready, 1)

            def centre1(a):
                dve.wait_ge(tok_ready, a + 1)
                centre_tokens(chained("a", a), tok[:, :, :], ssum_a, cent_a, cent1_ready)

            def variance1(a):
                done = chained("a", a)
                dve.wait_ge(sq1_ready, a + 1)
                done(v.tensor_reduce(ssq_a[:, :], sq_a[:, :, :], AX.X, ALU.add))
                v.tensor_scalar(v64[:, :], ssq_a[:, :], 1.0 / C, None, ALU.mult)
                v.tensor_scalar(vare_a[:, :], ssq_a[:, :], 1.0 / C, EPS, ALU.mult, ALU.add).then_inc(vare1_ready, 1)

            def normalise1(a):
                dve.wait_ge(r12_ready, a + 1)
                tt(n1[:, :, 0:C], cent_a[:, :, :], wide(r12[:, :], C), ALU.mult).then_inc(n1_ready, 1)

            def normalise0(a):
                wait(dve, ut_ready, a)
                tt(u[:, :, :], cent_a[:, :, :], wide(r1[:, :], C), ALU.mult).then_inc(u_ready, 1)

            def buckets(b):
                done = chained("b", b)
                dve.wait_ge(rot_ready, b + 1)
                rot = rot_ps.rearrange("p (a k) -> p a k", k=BUCKETS)
                done(v.tensor_reduce(bmax[:, :], rot, AX.X, ALU.max))
                done(tt(beq[:, :, :], rot, wide(bmax[:, :], BUCKETS), ALU.is_equal))
                rank = descend[:, :].unsqueeze(1).broadcast_to([P, NJ * HASHES, BUCKETS])
                done(tt(beq[:, :, :], beq[:, :, :], rank, ALU.mult))
                done(v.tensor_reduce(bfirst[:, :], beq[:, :, :], AX.X, ALU.max))
                tt(onehot[:, :, :], beq[:, :, :], wide(bfirst[:, :], BUCKETS), ALU.is_equal).then_inc(onehot_ready, 1)

            def bucket_means(b):
                done = chained("b", b)
                dve.wait_ge(pool_ready, b + 1)
                n_in = pool_ps[:, C:C + 1]
                v.tensor_scalar(pooled[:, C + 1:C + 2], n_in, 1.0, MASKED, ALU.is_lt, ALU.mult)
                done(v.tensor_scalar(cnt[:, :], n_in, 1e-20, None, ALU.add))
                done(v.reciprocal(rcnt[:, :], cnt[:, :]))
                v.tensor_scalar(pooled[:, 0:C + 1], pool_ps, rcnt[:, 0:1], None, ALU.mult).then_inc(pooled_ready, 1)

            def store_pooled(b):
                dve.wait_ge(poolt_ready, b + 1)
                v.tensor_copy(pooled_t[:, :], poolt_ps).then_inc(pooledt_ready, 1)

            def key_value_blocks(b):
                dve.wait_ge(kv_ready, b + 1)
                for m in range(GB):
                    tt(kblk[:, m, :, :], k_ps[:, M * m:M * (m + 1)].unsqueeze(1).broadcast_to([C + 1, HEADS, M]),
                       wide(head_of[:, :], M), ALU.mult)
                for ch in range(2):
                    ins = tt(vblk[:, :, ch, 0:C], v_ps,
                             v_mask[:, ch, :].unsqueeze(1).broadcast_to([P, GB, C]), ALU.mult)
                ins.then_inc(blk_ready, 1)

            def centre_scores(b, p):
                done = chained("b", b)
                dve.wait_ge(s_ready, 4 * b + p + 1)
                s_ps = bk12[:, p % 2, :].rearrange("p (h m) -> p h m", m=M)
                done(v.tensor_reduce(smax[:, p % 2, :], s_ps, AX.X, ALU.max))
                wait(dve, prob_ready, 4 * b + p - 1)
                tt(ssub[:, p % 2, :, :], s_ps, wide(smax[:, p % 2, :], M), ALU.subtract).then_inc(ssub_ready, 1)

            def attended(b, s):
                done = chained("b", b)
                dve.wait_ge(av_ready, 4 * b + 2 * s + 2)
                done(v.reciprocal(rden[:, s, :, :], av_ps[:, :, C:C + HEADS]))
                o = av_ps[:, :, 0:C].rearrange("p j (h d) -> p j h d", d=DH)
                r = rden[:, s, :, :].unsqueeze(3).broadcast_to([P, 4, HEADS, DH])
                if s == 0:
                    wait(dve, x2t_ready, b)
                tt(att[:, s, :, :].rearrange("p j (h d) -> p j h d", d=DH), o, r, ALU.mult).then_inc(att_read, 1)

            def centre2(b):
                done = chained("b", b)
                dve.wait_ge(att_read, 2 * b + 2)
                done(tt(x2[:, :, :].rearrange("p j c -> p (j c)"), u[:, :, :].rearrange("p j c -> p (j c)"),
                        att[:, :, :, :].rearrange("p s j c -> p (s j c)"), ALU.add))
                centre_tokens(done, x2[:, :, :], ssum_c, cent_c, cent2_ready)

            def variance_c(c, k, squares_ready):
                done = chained("c", c)
                dve.wait_ge(squares_ready, c + 1)
                done(v.tensor_reduce(ssq_c[:, :], sq_c[:, :, :], AX.X, ALU.add))
                v.tensor_scalar(vare_c[:, :], ssq_c[:, :], 1.0 / C, EPS, ALU.mult, ALU.add).then_inc(vare_c_ready, 1)

            def normalise2(c):
                dve.wait_ge(rc_ready, 2 * c + 1)
                tt(n2[:, :, :], cent_c[:, :, :], wide(rc[:, :], C), ALU.mult).then_inc(n2_ready, 1)

            def low_n2(c):
                dve.wait_ge(n2_ready, c + 1)
                dve.wait_ge(n2hi_ready, c + 1)
                v.scalar_tensor_tensor(out=n2s[:, :, C:2 * C], in0=n2[:, :, :], scalar=XS, in1=n2s[:, :, 0:C],
                                       op0=ALU.mult, op1=ALU.subtract).then_inc(n2s_ready, 1)

            def centre3(c):
                done = chained("c", c)
                dve.wait_ge(x2t_ready, c + 1)
                dve.wait_ge(y_ready, c + 1)
                tt(t2[:, :, :], x2t[:, :, :], y_ps, ALU.add).then_inc(t2_ready, 1)
                dve.wait_ge(t2_ready, c + 1)
                centre_tokens(done, t2[:, :, :], ssum_c, cent_c, cent3_ready)
                v.tensor_copy(t2_all[:, ds(c, 1), :, :].rearrange("p o j c -> p (o j c)"),
                              t2[:, :, :].rearrange("p j c -> p (j c)"))

            def normalise3(c):
                dve.wait_ge(rc_ready, 2 * c + 2)
                tt(wtok[:, :, :], cent_c[:, :, :], wide(rc[:, :], C), ALU.mult).then_inc(wtok_ready, 1)

            def low_wtok(c):
                dve.wait_ge(wtok_ready, c + 1)
                dve.wait_ge(whi_ready, c + 1)
                hi = srow[:, 0, :, 0:C // 2].bitcast(F16)
                lo = srow[:, 0, :, C // 2:C].bitcast(F16)
                v.scalar_tensor_tensor(out=lo, in0=wtok[:, :, :], scalar=XS, in1=hi, op0=ALU.mult,
                                       op1=ALU.subtract).then_inc(srow_ready, 1)

            def centre_logits(c):
                done = chained("c", c)
                dve.wait_ge(router_ready, c + 1)
                done(v.tensor_reduce(lmax[:, :], l_ps, AX.X, ALU.max))
                tt(lsub[:, :, :], l_ps, wide(lmax[:, :], NE), ALU.subtract).then_inc(lsub_ready, 1)

            def picks(c):
                done = chained("c", c)
                dve.wait_ge(lexp_ready, c + 1)
                done(v.tensor_reduce(lden[:, :], lexp[:, :, :], AX.X, ALU.add))
                done(v.reciprocal(lrec[:, :], lden[:, :]))
                done(tt(pr[:, :, :], lexp[:, :, :], wide(lrec[:, :], NE), ALU.mult))
                order = descend[:, :].unsqueeze(1).broadcast_to([P, NJ, NE])

                def pick(src, k):
                    done(v.tensor_reduce(pk[:, k, :], src, AX.X, ALU.max))
                    done(tt(peq[:, :, :], src, wide(pk[:, k, :], NE), ALU.is_equal))
                    done(tt(peq[:, :, :], peq[:, :, :], order, ALU.mult))
                    done(v.tensor_reduce(pfirst[:, :], peq[:, :, :], AX.X, ALU.max))
                    done(tt(oh[:, k, :, :], peq[:, :, :], wide(pfirst[:, :], NE), ALU.is_equal))

                pick(pr[:, :, :], 0)
                done(v.scalar_tensor_tensor(out=prest[:, :, :], in0=oh[:, 0, :, :], scalar=-2.0, in1=pr[:, :, :],
                                            op0=ALU.mult, op1=ALU.add))
                pick(prest[:, :, :], 1)
                by_e = "p j e -> p e j"
                tt(picked[:, :, 1:NJ + 1], oh[:, 0, :, :].rearrange(by_e), oh[:, 1, :, :].rearrange(by_e), ALU.add)
                done(tt(gsum[:, :], pk[:, 0, :], pk[:, 1, :], ALU.add))
                flat9 = "p e j -> p (e j)"
                v.tensor_tensor_scan(passed[:, :, :].rearrange(flat9), scan_keep[:, :, :].rearrange(flat9),
                                     picked[:, :, :].rearrange(flat9), 0.0, ALU.mult, ALU.add)\
                    .then_inc(passed_ready, 1)
                done(v.tensor_scalar(gsum[:, :], gsum[:, :], 1e-9, None, ALU.add))
                done(v.reciprocal(grec[:, :], gsum[:, :]))
                dve.wait_ge(dst_ready, c + 1)
                for k in range(2):
                    tt(srow[:, k, :, C], pk[:, k, :], grec[:, :], ALU.mult)

            def row_places(c):
                done = chained("c", c)
                by_e = "p j e -> p e j"
                dve.wait_ge(pos_counted, c + 1)
                v.tensor_copy(picked[:, :, 0], passed[:, :, NJ]).then_inc(sums_kept, 1)
                done(tt(posall[:, :, :], pos_ps, region[:, :, :], ALU.add))
                for k in range(2):
                    ins = tt(posk[:, k, :, :], posall[:, :, :], oh[:, k, :, :].rearrange(by_e), ALU.mult)
                done(ins)
                for k in range(2):
                    ins = v.tensor_reduce(posf[:, k, :], posk[:, k, :, :].rearrange("p e j -> p j e"), AX.X, ALU.add)
                done(ins)
                v.tensor_copy(pos[:, :, :], posf[:, :, :]).then_inc(pos_ready, 1)

            def largest_weight(c):
                dve.wait_ge(experts_loaded, 64 * c + 64)
                v.tensor_reduce(wmax[:, :], wn[:, :, :, :].rearrange("p t k c -> p t (k c)"), AX.X, ALU.max,
                                apply_absolute_value=True).then_inc(w_max_ready, 1)

            def weight_scales(c):
                dve.wait_ge(w_max_all, c + 1)
                scales(wmax_all[:, :], wexp[:, :], wscale[:, :], wback[:, ds(c, 1), :].rearrange("p o t -> p (o t)"),
                       chained("w", c)).then_inc(w_scale_ready, 1)

            def low_weights(c):
                for t in range(2):
                    dve.wait_ge(w_hi_ready, 2 * c + t + 1)
                    flat = "p k c -> p (k c)"
                    ins = v.scalar_tensor_tensor(
                        out=w_lo[:, t, :, :].rearrange(flat), in0=wn[:, t, :, :].rearrange(flat),
                        scalar=wscale[:, t:t + 1].bitcast(F32), in1=w_hi[:, t, :, :].rearrange(flat),
                        op0=ALU.mult, op1=ALU.subtract)
                ins.then_inc(w_parts_ready, 1)

            def store_weights(c):
                dve.wait_ge(w_turned, 4 * c + 3)
                dve.sem_inc(waited, 1)
                v.tensor_copy(w13_q[:, ds(c, 1), 16:24, :].rearrange("p o q n -> p (o q n)"), w_turn_ps[2])\
                    .then_inc(w_stored_dve, 1)
                dve.wait_ge(w_turned, 4 * c + 4)
                dve.sem_inc(waited, 1)
                v.tensor_copy(w2s[:, ds(c, 1), :, :].rearrange("p o k c -> p (o k c)"), bk7[:, 0:CH * C])\
                    .then_inc(w_stored_dve, 1)

            def iteration(a=None, b=None, c=None, d=None):
                count.update(dict.fromkeys(STEPS, 0))
                run(b, buckets)
                run(a, channel_statistics)
                run(c, variance_c, 2, sq2_ready)
                run(b, bucket_means)
                run(a, channel_variances)
                run(b, store_pooled)
                run(a, pair_statistics)
                run(c, largest_weight)
                run(c, normalise2)
                run(b, key_value_blocks)
                run(c, low_n2)
                run(a, row_sums)
                run(b, centre_scores, 0)
                run(b, centre_scores, 1)
                run(c, centre3)
                run(a, centre1)
                run(b, centre_scores, 2)
                run(c, variance_c, 3, sq3_ready)
                run(b, centre_scores, 3)
                run(a, variance1)
                run(b, attended, 0)
                run(c, normalise3)
                run(a, normalise1)
                run(c, low_wtok)
                run(b, attended, 1)
                run(c, weight_scales)
                run(b, centre2)
                run(c, centre_logits)
                run(a, normalise0)
                run(c, low_weights)
                run(c, picks)
                run(c, row_places)
                run(c, store_weights)
                done_stages = dict(a=a, b=b, c=c, w=c)
                assert all(done_stages[k] is None or count[k] == STEPS[k] for k in STEPS), count

            pipeline(dve, iteration)

            n = 0

            def step_done(ins):
                nonlocal n
                n += 1
                ins.then_inc(sched_step, 1)
                dve.wait_ge(sched_step, n)

            dve.wait_ge(w_stored_dve, 2 * NG)
            dve.wait_ge(counted, 1)
            step_done(v.tensor_copy(cnt8[:, :], bk7[:, 0:NE]))
            nk = T // MT
            step_done(tt(over[:, :, :], wide(cnt8[:, :], nk), k_rows[:, :].unsqueeze(1).broadcast_to([P, NE, nk]),
                         ALU.is_gt))
            step_done(v.tensor_reduce(tiles[:, :], over[:, :, :], AX.X, ALU.add))
            tt(pad_row[:, :], cnt8[:, :], region[:, :, 0], ALU.add)
            v.tensor_scalar(adjust[:, :], tiles[:, :], -float(MT), float(REG), ALU.mult, ALU.add)
            step_done(v.tensor_tensor_scan(tiles_end[:, :], ones[:, 0:NE], tiles[:, :], 0.0, ALU.mult, ALU.add))
            step_done(tt(past[:, :, :], wide(g_no[:, :], NE), tiles_end[:, :].unsqueeze(1).broadcast_to([P, NS, NE]),
                         ALU.is_ge))
            step_done(v.tensor_reduce(n_past[:, :], past[:, :, :], AX.X, ALU.add))
            v.tensor_scalar(tile_expert[:, :], n_past[:, :], float(NE - 1), None, ALU.min)
            v.tensor_scalar(tile_expert_f[:, :], n_past[:, :], float(NE - 1), None, ALU.min)
            step_done(tt(past_a[:, :, :], past[:, :, :], adjust[:, :].unsqueeze(1).broadcast_to([P, NS, NE]),
                         ALU.mult))
            step_done(v.tensor_reduce(a_past[:, :], past_a[:, :, :], AX.X, ALU.add))
            step_done(tt(a_past[:, :], a_past[:, :], g_row[:, :], ALU.add))
            v.tensor_scalar(tile_row[:, :], a_past[:, :], float(NE * REG), None, ALU.min).then_inc(sched_ready, 1)
            dve.wait_ge(sched_ready, 1)
            step_done(tt(past[:, :, :], wide(tile_expert_f[:, :], NE),
                         e_no[:, :].unsqueeze(1).broadcast_to([P, NS, NE]), ALU.is_equal))
            for w in range(2):
                back = wback[:, :, w].bitcast(F32).unsqueeze(1).broadcast_to([P, NS, NE])
                step_done(tt(past_a[:, :, :], past[:, :, :], back, ALU.mult))
                step_done(v.tensor_reduce(tile_back[:, :, w], past_a[:, :, :], AX.X, ALU.add))
            v.tensor_copy(cnt[:, :], ones[:, 0:1]).then_inc(sched_ready, 1)

            def gated(t, b):
                back = tile_back[:, ds(t, 1), 1:2].rearrange("p o n -> p (o n)")
                for q in range(CH // 2):
                    m = (3 * b + q) % 2
                    dve.wait_ge(silu_ready, 3 * t + q + 1)
                    dve.wait_ge(h3_ready, 3 * t + q + 1)
                    v.scalar_tensor_tensor(out=hbuf[:, b, 2 * q:2 * q + 2, :].rearrange("p k n -> p (k n)"),
                                           in0=bk34[:, m, :], scalar=back, in1=silu[:, m, :],
                                           op0=ALU.mult, op1=ALU.mult).then_inc(h_ready, 1)

            def gate_out(t, b, nth):
                dve.wait_ge(e_y_ready, t + 1)
                dve.wait_ge(route_ready, t + 1)
                wait(dve, y_scattered[b], 32 * nth)
                v.tensor_copy(dest[:, b, :], route[:, b, :, 1])
                tt(yout[:, b, :, :], bk56[:, b, 0:2 * C].rearrange("p (h c) -> p h c", h=2),
                   wide(route[:, b, :, 0], C), ALU.mult).then_inc(yout_ready[b], 1)

            gated(0, 0)

            def two_tiles(k):
                gated(2 * k + 1, 1)
                gate_out(2 * k, 0, k)
                gated(2 * k + 2, 0)
                gate_out(2 * k + 1, 1, k)

            first_then_loop(dve, (NT - 1) // 2, two_tiles)
            gate_out(NT - 1, 0, (NT - 1) // 2)

            def add_results(k):
                for b in range(2):
                    dve.wait_ge(res_loaded[b], 128 * (k + 1))
                    wait(dve, o_turned[b], k)
                    tt(t3[:, b, :, :], res[:, b, 0, :, :], res[:, b, 1, :, :], ALU.add).then_inc(t3_sum, 1)
                    dve.wait_ge(t3_sum, 2 * k + b + 1)
                    tt(t3[:, b, :, :].rearrange("p j c -> p (j c)"), t3[:, b, :, :].rearrange("p j c -> p (j c)"),
                       t2_all[:, ds(2 * k + b, 1), :, :].rearrange("p o j c -> p (o j c)"), ALU.add)\
                        .then_inc(t3_ready, 1)

            first_then_loop(dve, NG // 2, add_results)


DVE_SETUP = 14
STEPS = dict(a=7, b=14, c=24, w=2)


def wait(engine, semaphore, value):
    if not isinstance(value, int) or value > 0:
        engine.wait_ge(semaphore, value)


def run(group, step, *args):
    if group is not None:
        step(group, *args)


def pipeline(engine, iteration):
    iteration(a=0)
    iteration(a=1, b=0)
    iteration(a=2, b=1, c=0)
    with engine.Fori(0, NG - 3) as i:
        iteration(a=i + 3, b=i + 2, c=i + 1, d=i)
    iteration(b=NG - 1, c=NG - 2, d=NG - 3)
    iteration(c=NG - 1, d=NG - 2)
    iteration(d=NG - 1)


def first_then_loop(engine, n, body):
    body(0)
    with engine.Fori(1, n) as k:
        body(k)


def kernel(**inputs):
    import numpy as np
    import concourse.bacc as bacc
    from concourse.bass_utils import run_bass_kernel_spmd

    names = ["x", "L0_conv_bias", "L1_attn_rotations", "L1_attn_norm1_g", "L1_attn_norm1_b", "L1_attn_q_w",
             "L1_attn_kv_w", "L1_attn_norm2_g", "L1_attn_norm2_b", "L1_attn_fc1_w", "L1_attn_fc1_b",
             "L1_attn_fc2_w", "L1_attn_fc2_b", "L1_ffn_router_w", "L1_ffn_w1", "L1_ffn_w2", "L1_ffn_w3"]
    nc = bacc.Bacc("TRN2", target_bir_lowering=False, num_devices=1)
    arrays, args = {}, []
    for name in names:
        a = np.ascontiguousarray(inputs[name])
        arrays[f"in_{name}"] = a
        args.append(nc.dram_tensor(f"in_{name}", a.shape, mybir.dt.from_np(a.dtype), kind="ExternalInput").ap())
    out = nc.dram_tensor("out_0", (B, C, HH, WW), F32, kind="ExternalOutput").ap()
    hybrid_block(nc, *args, out)
    r = run_bass_kernel_spmd(nc, [arrays], core_ids=[0])
    return r.results[0]["out_0"]
```

```python
from contextlib import ExitStack

import concourse.bass as bass
from concourse import mybir
from concourse.bass import ds

P = 128
B, C, HH, WW = 32, 64, 16, 16
N = HH * WW
T = B * N
GB = 4
NG = B // GB
GT = GB * N
NJ = GT // P
HASHES, BUCKETS = 4, 8
M = HASHES * BUCKETS
HEADS = 8
DH = C // HEADS
DFF = 4 * C
NE = 8
HID = 682
CF = 5
CR = HID - CF * P
CH = CF + 1
MT = 256
REG = T + MT
NT = (2 * T + NE * (MT - 1)) // MT
UNROLLED = 3
WINDOW = 2 * UNROLLED + 1
EXPERT_BITS = (NE - 1).bit_length()
NS = NT + 1
ROW = C + 2
DUMP = 2 * T
XS = 2048.0
EPS = 1e-5
TINY = 1e-30
EXP_MASK = 0x7F800000
SCALE_EXP = 127 + 13 + 127
BACK_EXP = 13 + 11
MASKED = -1e30

ALU = mybir.AluOpType
ACT = mybir.ActivationFunctionType
F32 = mybir.dt.float32
F16 = mybir.dt.float16
U32 = mybir.dt.uint32
I32 = mybir.dt.int32
AX = mybir.AxisListType


def hybrid_block(nc, x, conv_bias, rotations, norm1_g, norm1_b, q_w, kv_w, norm2_g, norm2_b,
                 fc1_w, fc1_b, fc2_w, fc2_b, router_w, w1, w2, w3, out):
    with ExitStack() as ctx:
        def sb(name, shape, dt=F32):
            return ctx.enter_context(nc.sbuf_tensor(name, shape, dt))

        def sem(name):
            return ctx.enter_context(nc.semaphore(name))

        rows = nc.dram_tensor("expert_rows", (NE * REG + MT, ROW), F32).ap()
        results = nc.dram_tensor("expert_results", (DUMP, C), F32).ap()

        ident = sb("ident", [P, P])
        ident16 = sb("ident16", [P, P], F16)
        pair_mean = sb("pair_mean", [P, P])
        before = sb("before", [P, P])
        ones = sb("ones", [P, P])
        descend = sb("descend", [P, BUCKETS])
        head_of = sb("head_of", [C + 1, HEADS])
        v_mask = sb("v_mask", [P, 2, C])
        v_heads = sb("v_heads", [P, 2, HEADS])
        region = sb("region", [P, NE, NJ])
        scan_keep = sb("scan_keep", [P, NE, NJ + 1])
        c_mhalf = sb("c_mhalf", [P, NJ])
        c_64th = sb("c_64th", [P, NJ])
        c_eps = sb("c_eps", [P, NJ])
        c_group = sb("c_group", [P, 2, NJ])
        bias2 = sb("bias2", [P, 1])
        g1 = sb("g1", [C, 1])
        g2 = sb("g2", [P, 1])
        b2c = sb("b2c", [C, 1])
        fc1_bias0 = sb("fc1_bias0", [P, 2])
        fc1_bias = sb("fc1_bias", [P, 2])
        diag_g1 = sb("diag_g1", [C, C + 1])
        proj = sb("proj", [C, C + M + 2 * C])
        q_aug = sb("q_aug", [C + 1, C + 1])
        rot_aug = sb("rot_aug", [C + 1, M])
        k_aug = sb("k_aug", [C + 2, C + 1])
        v_aug = sb("v_aug", [C + 1, C])
        fc1_n = sb("fc1_n", [P, DFF])
        fc1_s = sb("fc1_s", [P, DFF])
        fc1_p = sb("fc1_p", [P, 2, DFF], F16)
        fc2_s = sb("fc2_s", [P, 2, C])
        fc2_bias = sb("fc2_bias", [P, C])
        router_n = sb("router_n", [NE, 2 * C])
        router_t = sb("router_t", [P, NE])
        router_p = sb("router_p", [P, 2, NE], F16)
        small_max = sb("small_max", [P, 2])
        small_max_all = sb("small_max_all", [P, 2])
        small_scale = sb("small_scale", [P, 2], U32)
        small_back = sb("small_back", [P, 2], U32)
        wn = sb("wn", [P, 2, CH, C])
        w2n = sb("w2n", [C, CH * P])
        w_hi = sb("w_hi", [P, 2, CH, C], F16)
        w_lo = sb("w_lo", [P, 2, CH, C], F16)
        w2_parts = sb("w2_parts", [C, 2, CH * P], F16)
        w13 = sb("w13", [P, NE, 2, CH, 2, P], F16)
        w2s = sb("w2s", [P, NE, CH, 2, C], F16)
        wmax = sb("wmax", [P, 3])
        wmax_all = sb("wmax_all", [P, 3])
        wexp = sb("wexp", [P, 3], U32)
        wscale = sb("wscale", [P, 3], U32)
        wpow = sb("wpow", [P, 3], U32)
        wprod = sb("wprod", [P, 1])
        wfactor = sb("wfactor", [P, 3])
        wback = sb("wback", [P, NE, 3])
        xg = sb("xg", [P, 2, HH, WW])
        xpad = sb("xpad", [P, 2, HH + 2, WW + 2])
        hsum = sb("hsum", [P, 2, HH + 2, WW])
        xres = sb("xres", [P, 2, HH, WW])
        bst = sb("bst", [P, 2, 6])
        mv = sb("mv", [P, 2, 2])
        dmean = sb("dmean", [P, 2])
        dmean2 = sb("dmean2", [P, 2])
        chvar = sb("chvar", [P, 2])
        gmean = sb("gmean", [P, 2])
        gvar = sb("gvar", [P, 2])
        grstd = sb("grstd", [P, 2])
        tok = sb("tok", [P, NJ, C])
        cent_a, cent_c = sb("cent_a", [P, NJ, C]), sb("cent_c", [P, NJ, C])
        sq_a, sq_c = sb("sq_a", [P, NJ, C]), sb("sq_c", [P, NJ, C])
        ssum_a, ssum_c = sb("ssum_a", [P, NJ]), sb("ssum_c", [P, NJ])
        ssq_a, ssq_c = sb("ssq_a", [P, NJ]), sb("ssq_c", [P, NJ])
        vare_a, vare_c = sb("vare_a", [P, NJ]), sb("vare_c", [P, NJ])
        r1, rc = sb("r1", [P, NJ]), sb("rc", [P, NJ])
        r1sq = sb("r1sq", [P, NJ])
        v64 = sb("v64", [P, NJ])
        uvar = sb("uvar", [P, NJ])
        uvare = sb("uvare", [P, NJ])
        r2 = sb("r2", [P, NJ])
        r12 = sb("r12", [P, NJ])
        u = sb("u", [P, NJ, C])
        n1 = sb("n1", [P, NJ, C + 1])
        res = sb("res", [P, 2, 2, NJ, C])
        n1t = res[0:C + 1, 0, :, :, :].rearrange("p k j c -> p (k j c)")
        qt = res[0:C + 1, 1, :, :, :].rearrange("p k j c -> p (k j c)")
        bmax = sb("bmax", [P, NJ * HASHES])
        beq = sb("beq", [P, NJ * HASHES, BUCKETS])
        bfirst = sb("bfirst", [P, NJ * HASHES])
        onehot = sb("onehot", [P, NJ * HASHES, BUCKETS])
        cnt = sb("cnt", [P, 1])
        rcnt = sb("rcnt", [P, 1])
        pooled = sb("pooled", [P, C + 2])
        pooled_t = sb("pooled_t", [C + 2, P])
        pooled_rep = sb("pooled_rep", [C + 1, GB, 4, M])
        kblk = sb("kblk", [C + 1, GB, HEADS, M])
        vblk = sb("vblk", [P, GB, 2, C + HEADS])
        smax = sb("smax", [P, 2, 2 * HEADS])
        ssub = sb("ssub", [P, 2, 2 * HEADS, M])
        silu = ssub[:, :, :, :].rearrange("p b h m -> p b (h m)")
        prob = sb("prob", [P, 2, 4, P])
        prob_t = sb("prob_t", [P, 2, 4, P])
        rden = sb("rden", [P, 2, 4, HEADS])
        att = sb("att", [P, 2, 4, C])
        x2 = sb("x2", [P, NJ, C])
        u_tok = sb("u_tok", [P, NJ, C])
        x2t = sb("x2t", [P, NJ, C])
        n2s = sb("n2s", [P, NJ, 2 * C], F16)
        n2 = sb("n2", [P, NJ, C])
        hbuf = sb("hbuf", [P, 2, CH, MT])
        hparts = hbuf[:, :, :, :].rearrange("p b k n -> p b (k n)").bitcast(F16)\
            .rearrange("p b (k a n) -> p b k a n", k=CH, a=2)
        hid = hbuf[:, :, :, :].rearrange("p b k n -> p (b k n)")[:, 0:2 * GT].rearrange("p (a n) -> p a n", a=2)
        t3 = sb("t3", [P, 2, NJ, C])
        og = sb("og", [P, 2, 2 * N])
        n2t = t3[:, 0, :, :].rearrange("p j c -> p (j c)").bitcast(F16)
        wtok_t = t3[:, 1, :, :].rearrange("p j c -> p (j c)").bitcast(F16)
        t2 = sb("t2", [P, NJ, C])
        t2_all = sb("t2_all", [P, NG, NJ, C])
        wtok = sb("wtok", [P, NJ, C])
        wparts = sb("wparts", [P, NJ, 2 * C], F16)
        lmax = sb("lmax", [P, NJ])
        lsub = sb("lsub", [P, NJ, NE])
        lexp = sb("lexp", [P, NJ, NE])
        lden = sb("lden", [P, NJ])
        lrec = sb("lrec", [P, NJ])
        pr = sb("pr", [P, NJ, NE])
        pk = sb("pk", [P, 2, NJ])
        peq = sb("peq", [P, NJ, NE])
        pfirst = sb("pfirst", [P, NJ])
        oh = sb("oh", [P, 2, NJ, NE])
        prest = sb("prest", [P, NJ, NE])
        gsum = sb("gsum", [P, NJ])
        grec = sb("grec", [P, NJ])
        picked = sb("picked", [P, NE, NJ + 1])
        passed = sb("passed", [P, NE, NJ + 1])
        posall = sb("posall", [P, NE, NJ])
        posk = sb("posk", [P, 2, NE, NJ])
        posf = sb("posf", [P, 2, NJ])
        pos = sb("pos", [P, 2, NJ], U32)
        srow = sb("srow", [P, 2, NJ, ROW])

        cnt8 = sb("cnt8", [P, NE])
        k_rows = sb("k_rows", [P, T // MT])
        over = beq[:, :, :].rearrange("p a k -> p (a k)").rearrange("p (e n) -> p e n", e=NE)
        tiles = sb("tiles", [P, NE])
        tiles_end = sb("tiles_end", [P, NE])
        adjust = sb("adjust", [P, NE])
        g_no = sb("g_no", [P, NS])
        g_row = sb("g_row", [P, NS])
        past = prob[:, :, :, :].rearrange("p b a n -> p (b a n)")[:, 0:NS * NE].rearrange("p (t e) -> p t e", e=NE)
        past_a = prob_t[:, :, :, :].rearrange("p b a n -> p (b a n)")[:, 0:NS * NE].rearrange("p (t e) -> p t e", e=NE)
        n_past = sb("n_past", [P, NS])
        a_past = sb("a_past", [P, NS])
        packed = sb("packed", [1, 2, NS + 1])
        window_experts = sb("window_experts", [1, NS], U32)
        tile_expert_f = sb("tile_expert_f", [P, NS])
        e_no = sb("e_no", [P, NE])
        tile_back = sb("tile_back", [P, NS, 3])
        tile_row = sb("tile_row", [P, NS], U32)
        pad_row = sb("pad_row", [P, NE], U32)
        pad = sb("pad", [P, 2, ROW])
        xin = sb("xin", [P, 2, 2, ROW])
        xs = onehot[:, :, :].rearrange("p a k -> p (a k)").bitcast(F16).rearrange("p (b n) -> p b n", b=2)
        route = sb("route", [P, NS, 2, 2])
        dest = sb("dest", [P, 2, 2], U32)
        yout = att[:, :, 0:2, :]
        units = [prob[:, 0, :, :].rearrange("p a n -> p (a n)"), prob[:, 1, :, :].rearrange("p a n -> p (a n)"),
                 prob_t[:, 0, :, :].rearrange("p a n -> p (a n)")]
        ylow = sb("ylow", [P, 2, 2, C])

        def ps(name, shape, dt=F32):
            return ctx.enter_context(nc.psum_tensor(name, shape, dt))

        bk0 = ps("bk0", [P, 512])
        bk12 = ps("bk12", [P, 2, 512])
        bk34 = ps("bk34", [P, 2, 512])
        bk56 = ps("bk56", [P, 2, 512])
        bk7 = ps("bk7", [P, 512])

        bk5, bk6 = bk56[:, 0, :], bk56[:, 1, :]
        t_ps = bk0[:, :]
        gmean_ps = bk0[:, 0:2]
        gvar_ps = bk0[:, 8:10]
        rot_ps = bk5[:, 0:256]
        pool_ps = bk5[:, 256:256 + C + 1]
        poolt_ps = bk5[0:C + 2, 384:512]
        av_ps = bk5[:, 0:4 * (C + HEADS)].rearrange("p (j c) -> p j c", j=4)
        k_ps = bk34[0:C + 1, 0, 0:P]
        v_ps = bk34[:, 0, 256:512].rearrange("p (b c) -> p b c", b=GB)
        fc1_ps = [bk7[:, :], bk6]
        y_ps = bk7[:, :].rearrange("p (j c) -> p j c", j=NJ)
        l_ps = bk12[:, 0, 0:NJ * NE].rearrange("p (j e) -> p j e", j=NJ)
        pos_ps = bk12[:, 1, 0:NE * NJ].rearrange("p (e j) -> p e j", e=NE)
        w13_q = w13[:, :, :, :, :, :].rearrange("p e t k a n -> p e (t k a) n")
        w_turn_ps = bk0[:, :].bitcast(F16)

        waited = sem("waited")
        small_loaded = sem("small_loaded")
        experts_loaded = sem("experts_loaded")
        w2_loaded = sem("w2_loaded")
        sched_ready = sem("sched_ready")
        counted = sem("counted")
        pads_written = sem("pads_written")
        xin_loaded = [sem(f"xin_loaded{b}") for b in range(2)]
        xt_turned = sem("xt_turned")
        xs_ready = sem("xs_ready")
        h1_ready = sem("h1_ready")
        h3_ready = sem("h3_ready")
        silu_ready = sem("silu_ready")
        h_ready = sem("h_ready")
        h_hi_ready = sem("h_hi_ready")
        h_lo_dve = sem("h_lo_dve")
        h_lo_pool = sem("h_lo_pool")
        ylow_ready = sem("ylow_ready")
        experts_packed = sem("experts_packed")
        ysum_ready = sem("ysum_ready")
        e_y_ready = sem("e_y_ready")
        route_ready = sem("route_ready")
        yout_ready = [sem(f"yout_ready{b}") for b in range(2)]
        y_scattered = [sem(f"y_scattered{b}") for b in range(2)]
        res_loaded = [sem(f"res_loaded{b}") for b in range(2)]
        t3_ready = sem("t3_ready")
        t3_sum = sem("t3_sum")
        sched_step = sem("sched_step")
        o_turned = [sem(f"o_turned{b}") for b in range(2)]
        og_ready = [sem(f"og_ready{b}") for b in range(2)]
        out_stored = [sem(f"out_stored{b}") for b in range(2)]
        consts_step = sem("consts_step")
        consts_ready = sem("consts_ready")
        pe_setup = sem("pe_setup")
        dve_setup = sem("dve_setup")
        w_max_ready = sem("w_max_ready")
        w_scale_ready = sem("w_scale_ready")
        w_max_all = sem("w_max_all")
        w_hi_ready = sem("w_hi_ready")
        w_parts_ready = sem("w_parts_ready")
        w_turned = sem("w_turned")
        w_stored = sem("w_stored")
        x_loaded = sem("x_loaded")
        x_used = sem("x_used")
        mean_ready = sem("mean_ready")
        gmean_ready = sem("gmean_ready")
        chvar_ready = sem("chvar_ready")
        gvar_done = sem("gvar_done")
        gvar_ready = sem("gvar_ready")
        grstd_ready = sem("grstd_ready")
        conv_ready = sem("conv_ready")
        t_ready = sem("t_ready")
        tok_ready = sem("tok_ready")
        rot_ready = sem("rot_ready")
        q_ready = sem("q_ready")
        qt_ready = sem("qt_ready")
        onehot_ready = sem("onehot_ready")
        pool_ready = sem("pool_ready")
        pooled_ready = sem("pooled_ready")
        poolt_ready = sem("poolt_ready")
        pooledt_ready = sem("pooledt_ready")
        rep_ready = sem("rep_ready")
        kv_ready = sem("kv_ready")
        blk_ready = sem("blk_ready")
        s_ready = sem("s_ready")
        ssub_ready = sem("ssub_ready")
        prob_ready = sem("prob_ready")
        probt_turned = sem("probt_turned")
        probt_ready = sem("probt_ready")
        av_ready = sem("av_ready")
        x2t_ready = sem("x2t_ready")
        fc1_ready = sem("fc1_ready")
        hid_ready = sem("hid_ready")
        y_ready = sem("y_ready")
        router_ready = sem("router_ready")
        lsub_ready = sem("lsub_ready")
        lexp_ready = sem("lexp_ready")
        passed_ready = sem("passed_ready")
        pos_ready = sem("pos_ready")
        pos_counted = sem("pos_counted")
        wtok_ready = sem("wtok_ready")
        whi_ready = sem("whi_ready")
        dst_ready = sem("dst_ready")
        wparts_ready = sem("wparts_ready")
        rows_ready = sem("rows_ready")
        scattered = sem("scattered")

        small_max_ready = sem("small_max_ready")
        small_max_all_ready = sem("small_max_all_ready")
        cent1_ready = sem("cent1_ready")
        sq1_ready = sem("sq1_ready")
        vare1_ready = sem("vare1_ready")
        r12_step = sem("r12_step")
        r12_ready = sem("r12_ready")
        n1_ready = sem("n1_ready")
        n1_turned = sem("n1_turned")
        n1t_ready = sem("n1t_ready")
        u_ready = sem("u_ready")
        tok_used = sem("tok_used")
        ut_ready = sem("ut_ready")
        cent2_ready = sem("cent2_ready")
        sq2_ready = sem("sq2_ready")
        vare_c_ready = sem("vare_c_ready")
        rc_ready = sem("rc_ready")
        n2_ready = sem("n2_ready")
        n2hi_ready = sem("n2hi_ready")
        n2s_ready = sem("n2s_ready")
        n2_turned = sem("n2_turned")
        n2t_ready = sem("n2t_ready")
        t2_ready = sem("t2_ready")
        cent3_ready = sem("cent3_ready")
        sq3_ready = sem("sq3_ready")
        wt_turned = sem("wt_turned")
        wt_ready = sem("wt_ready")
        att_read = sem("att_read")
        sums_kept = sem("sums_kept")
        a_step, b_step, c_step, d_step = sem("a_step"), sem("b_step"), sem("c_step"), sem("d_step")
        w_step = sem("w_step")

        x_rows = x.rearrange("b c h w -> (b c) (h w)")
        x_groups = x_rows.rearrange("(g s p) n -> g p s n", g=NG, s=2)

        block = ctx.enter_context(nc.Block())

        def write_pad(queue, row):
            queue.dma_start(rows[ds(row, MT), :].rearrange("(h p) w -> p h w", h=2), pad[:, :, :])\
                .then_inc(pads_written, 16)

        NSMALL = 18

        @block.sync
        def _(sp):
            flat = xg[:, :, :, :].rearrange("p s h w -> p s (h w)")
            sp.dma_start(bias2[0:C, :], conv_bias.rearrange("(c o) -> c o", o=1)).then_inc(small_loaded, 16)
            sp.dma_start(bias2[C:P, :], conv_bias.rearrange("(c o) -> c o", o=1)).then_inc(small_loaded, 16)
            sp.dma_start(g1[:, :], norm1_g.rearrange("(c o) -> c o", o=1)).then_inc(small_loaded, 16)
            sp.dma_start(diag_g1[:, C:C + 1], norm1_b.rearrange("(c o) -> c o", o=1)).then_inc(small_loaded, 16)
            for h in range(2):
                sp.dma_start(g2[h * C:(h + 1) * C, :], norm2_g.rearrange("(c o) -> c o", o=1))\
                    .then_inc(small_loaded, 16)
                sp.dma_start(fc1_n[h * C:(h + 1) * C, :], fc1_w).then_inc(small_loaded, 16)
            sp.dma_start(b2c[:, :], norm2_b.rearrange("(c o) -> c o", o=1)).then_inc(small_loaded, 16)
            sp.dma_start(proj[:, 0:C], q_w).then_inc(small_loaded, 16)
            rot_dst = proj[:, C:C + M].rearrange("c (h n) -> c h n", h=HASHES)
            sp.dma_start(rot_dst[:, :, 0:BUCKETS // 2], rotations.rearrange("o c h n -> (o c) h n")).then_inc(small_loaded, 16)
            sp.dma_start(proj[:, C + M:], kv_w).then_inc(small_loaded, 16)
            for a in range(2):
                sp.dma_start(fc1_bias0[:, a:a + 1], fc1_b[a * P:(a + 1) * P].rearrange("(p o) -> p o", o=1))\
                    .then_inc(small_loaded, 16)
            sp.dma_start(fc2_s[:, :, :], fc2_w.rearrange("(a p) c -> p a c", a=2)).then_inc(small_loaded, 16)
            for h in range(2):
                sp.dma_start(router_n[:, h * C:(h + 1) * C], router_w).then_inc(small_loaded, 16)
            sp.dma_start(fc2_bias[:, :], fc2_b.rearrange("(o c) -> o c", o=1).broadcast_to([P, C]))\
                .then_inc(small_loaded, 16)
            sp.wait_ge(consts_ready, 2)

            def iteration(a=None, b=None, c=None, d=None):
                if a is not None:
                    wait(sp, x_used, a)
                    sp.dma_start(flat, x_groups[ds(a, 1)].rearrange("g p s n -> (g p) s n")).then_inc(x_loaded, 16)
                if c is not None:
                    wait(sp, w_parts_ready, c)
                    for t, w in enumerate((w1, w3)):
                        we = w[ds(c, 1)].rearrange("e h c -> (e h) c")
                        sp.dma_start(wn[:, t, 0:CF, :], we[0:CF * P, :].rearrange("(p k) c -> p k c", k=CF))\
                            .then_inc(experts_loaded, 16)
                        sp.dma_start(wn[0:CR, t, CF, :], we[CF * P:HID, :]).then_inc(experts_loaded, 16)
                    w2e = w2[ds(c, 1)].rearrange("e c h -> (e c) h")
                    sp.dma_start(w2n[:, 0:HID], w2e).then_inc(w2_loaded, 16)

            pipeline(sp, iteration)
            sp.wait_ge(sched_ready, 1)
            write_pad(sp, NE * REG)
            for e in range(NE // 2):
                write_pad(sp, sp.value_load(pad_row[0:1, e:e + 1], min_val=0, max_val=NE * REG - MT))
            sp.wait_ge(pads_written, 16 * (NE + 1))
            sp.wait_ge(scattered, NG * 2 * NJ * 16)

            def load(t, b):
                row = sp.value_load(tile_row[0:1, ds(t, 1)], min_val=0, max_val=NE * REG)
                sp.dma_start(xin[:, b, :, :], rows[ds(row, MT), :].rearrange("(h p) w -> p h w", h=2))\
                    .then_inc(xin_loaded[b], 16)

            load(0, 0)
            load(1, 1)
            with sp.Fori(0, (NT - 1) // 2) as k:
                for b in range(2):
                    sp.wait_ge(xt_turned, 2 * k + b + 1)
                    sp.wait_ge(route_ready, 2 * k + b + 1)
                    load(2 * k + b + 2, b)

            sp.wait_ge(y_scattered[0], 32 * ((NT + 1) // 2))
            sp.wait_ge(y_scattered[1], 32 * (NT // 2))
            res_v = results.rearrange("(k i j p) c -> i k p j c", k=2, i=NG, p=P)

            def load_results(i, b):
                for k in range(2):
                    sp.dma_start(res[:, b, k, :, :], res_v[ds(i, 1), k].rearrange("i p j c -> (i p) j c"))\
                        .then_inc(res_loaded[b], 16)

            load_results(0, 0)
            load_results(1, 1)
            with sp.Fori(0, NG // 2 - 1) as k:
                for b in range(2):
                    sp.wait_ge(t3_sum, 2 * k + b + 1)
                    load_results(2 * k + b + 2, b)

        @block.gpsimd
        def _(pool):
            step = [0]

            def then(ins):
                step[0] += 1
                ins.then_inc(consts_step, 1)
                pool.wait_ge(consts_step, step[0])

            g = nc.gpsimd
            g.memset(ones[:, :], 1.0).then_inc(consts_ready, 1)
            g.memset(ident[:, :], 0.0)
            g.memset(ident16[:, :], 0.0)
            g.memset(diag_g1[:, 0:C], 0.0)
            g.memset(packed[:, :, :], 0.0)
            g.memset(pair_mean[:, :], 0.5)
            g.memset(before[:, :], 1.0)
            g.memset(head_of[:, :], 1.0)
            g.memset(v_mask[:, :, :], 1.0)
            g.memset(v_heads[:, :, :], 1.0)
            g.memset(scan_keep[:, :, :], 1.0)
            g.memset(q_aug[:, :], 0.0)
            g.memset(k_aug[:, :], 0.0)
            g.memset(c_mhalf[:, :], -0.5)
            g.memset(c_64th[:, :], 1.0 / C)
            g.memset(c_eps[:, :], EPS)
            g.memset(c_group[:, :, :], float(GT))
            g.memset(xpad[:, :, :, :], 0.0)
            g.memset(hsum[:, :, :, :], 0.0)
            g.memset(n1[:, :, C:C + 1], 1.0)
            then(g.memset(picked[:, :, 0:1], 0.0))
            for m in (ident, ident16):
                g.affine_select(out=m[:, :], in_=m[:, :], compare_op=ALU.not_equal, fill=1.0, base=0,
                                pattern=[[-1, P]], channel_multiplier=1)
            pm = pair_mean[:, :].rearrange("p (a b) -> p a b", b=2)
            then(g.affine_select(out=pm, in_=pm, compare_op=ALU.is_ge, fill=0.0, base=0,
                                 pattern=[[-2, C], [0, 2]], channel_multiplier=1))
            g.affine_select(out=pm, in_=pm, compare_op=ALU.is_ge, fill=0.0, base=1,
                            pattern=[[2, C], [0, 2]], channel_multiplier=-1)
            g.affine_select(out=before[:, :], in_=before[:, :], compare_op=ALU.is_gt, fill=0.0, base=0,
                            pattern=[[1, P]], channel_multiplier=-1)
            hc = head_of[0:C, :]
            g.affine_select(out=hc, in_=hc, compare_op=ALU.is_ge, fill=0.0, base=0,
                            pattern=[[-DH, HEADS]], channel_multiplier=1)
            vm = v_mask[:, :, :].rearrange("p a (h d) -> p a h d", h=HEADS)
            g.affine_select(out=vm, in_=vm, compare_op=ALU.is_ge, fill=0.0, base=0,
                            pattern=[[P, 2], [-M, HEADS], [0, DH]], channel_multiplier=1)
            then(g.affine_select(out=v_heads[:, :, :], in_=v_heads[:, :, :], compare_op=ALU.is_ge, fill=0.0,
                                 base=0, pattern=[[P, 2], [-M, HEADS]], channel_multiplier=1))
            g.affine_select(out=hc, in_=hc, compare_op=ALU.is_ge, fill=0.0, base=DH - 1,
                            pattern=[[DH, HEADS]], channel_multiplier=-1)
            g.affine_select(out=vm, in_=vm, compare_op=ALU.is_ge, fill=0.0, base=M - 1,
                            pattern=[[-P, 2], [M, HEADS], [0, DH]], channel_multiplier=-1)
            then(g.affine_select(out=v_heads[:, :, :], in_=v_heads[:, :, :], compare_op=ALU.is_ge, fill=0.0,
                                 base=M - 1, pattern=[[-P, 2], [M, HEADS]], channel_multiplier=-1))
            for b in range(GB):
                g.tensor_copy(vblk[:, b, :, C:C + HEADS], v_heads[:, :, :])
            g.affine_select(out=scan_keep[:, :, :], in_=scan_keep[:, :, :], compare_op=ALU.not_equal, fill=0.0,
                            base=0, pattern=[[0, NE], [1, NJ + 1]], channel_multiplier=0)
            g.affine_select(out=q_aug[:, C:C + 1], in_=q_aug[:, C:C + 1], compare_op=ALU.not_equal, fill=1.0,
                            base=-C, pattern=[[0, 1]], channel_multiplier=1)
            g.affine_select(out=k_aug[:, C:C + 1], in_=k_aug[:, C:C + 1], compare_op=ALU.not_equal, fill=1.0,
                            base=-(C + 1), pattern=[[0, 1]], channel_multiplier=1)
            g.iota(descend[:, :], [[-1, BUCKETS]], base=BUCKETS, channel_multiplier=0,
                   allow_small_or_imprecise_dtypes=True)
            g.iota(region[:, :, :], [[REG // MT, NE], [0, NJ]], base=0, channel_multiplier=0,
                   allow_small_or_imprecise_dtypes=True)
            for k in range(2):
                g.iota(srow[:, k, :, ROW - 1], [[P, NJ]], base=k * T - GT, channel_multiplier=1,
                       allow_small_or_imprecise_dtypes=True)
            g.memset(wn[:, :, CF, :], 0.0)
            g.memset(w2n[:, HID:CH * P], 0.0)
            g.memset(wmax[:, 2:3], 0.0)
            g.memset(pad[:, :, :], 0.0)
            for m, n in ((k_rows, T // MT), (g_no, NS), (e_no, NE)):
                g.iota(m[:, :], [[1, n]], base=0, channel_multiplier=0, allow_small_or_imprecise_dtypes=True)
            then(g.memset(r1[:, :], 0.0))
            g.memset(pad[:, :, ROW - 1:ROW], float(DUMP))
            g.tensor_scalar(g_row[:, :], g_no[:, :], float(MT), None, ALU.mult)
            g.tensor_scalar(k_rows[:, :], k_rows[:, :], float(MT), None, ALU.mult)
            g.tensor_scalar(region[:, :, :], region[:, :, :], float(MT), None, ALU.mult)
            pool.wait_ge(small_loaded, 16 * NSMALL)
            g.tensor_tensor(diag_g1[:, 0:C], ident[0:C, 0:C], g1[:, 0:1].broadcast_to([C, C]), ALU.mult)
            rot = proj[:, C:C + M].rearrange("c (h n) -> c h n", h=HASHES)
            g.tensor_scalar(rot[:, :, BUCKETS // 2:], rot[:, :, 0:BUCKETS // 2], -1.0, None, ALU.mult)\
                .then_inc(consts_ready, 1)

            pool.wait_ge(small_max_ready, 1)
            pool.sem_inc(waited, 1)
            g.partition_all_reduce(small_max_all[:, :], small_max[:, :], P, bass.bass_isa.ReduceOp.max)\
                .then_inc(small_max_all_ready, 1)

            def group_rstd(a):
                pool.wait_ge(gvar_ready, a + 1)
                g.tensor_tensor(grstd[:, :], gvar[:, :], c_mhalf[:, 0:2], ALU.pow).then_inc(grstd_ready, 1)

            def token_rstd(a):
                n = 0

                def step_done(ins):
                    nonlocal n
                    n += 1
                    ins.then_inc(r12_step, 1)
                    pool.wait_ge(r12_step, a * 5 + n)

                pool.wait_ge(vare1_ready, a + 1)
                step_done(g.tensor_tensor(r1[:, :], vare_a[:, :], c_mhalf[:, :], ALU.pow))
                step_done(g.tensor_tensor(r1sq[:, :], r1[:, :], r1[:, :], ALU.mult))
                step_done(g.tensor_tensor(uvar[:, :], r1sq[:, :], v64[:, :], ALU.mult))
                step_done(g.tensor_tensor(uvare[:, :], uvar[:, :], c_eps[:, :], ALU.add))
                step_done(g.tensor_tensor(r2[:, :], uvare[:, :], c_mhalf[:, :], ALU.pow))
                g.tensor_tensor(r12[:, :], r1[:, :], r2[:, :], ALU.mult).then_inc(r12_ready, 1)

            def late_rstd(c, k):
                pool.wait_ge(vare_c_ready, 2 * c + k)
                g.tensor_tensor(rc[:, :], vare_c[:, :], c_mhalf[:, :], ALU.pow).then_inc(rc_ready, 1)

            def residual(b):
                pool.wait_ge(att_read, 2 * b + 2)
                wait(pool, t2_ready, b)
                g.tensor_tensor(x2t[:, :, :].rearrange("p j c -> p (j c)"),
                                u_tok[:, :, :].rearrange("p j c -> p (j c)"),
                                att[:, :, :, :].rearrange("p s j c -> p (s j c)"), ALU.add).then_inc(x2t_ready, 1)

            def token_sum(b):
                pool.wait_ge(tok_ready, b + 1)
                wait(pool, x2t_ready, b)
                g.tensor_tensor(u_tok[:, :, :], tok[:, :, :],
                                fc2_bias[:, :].unsqueeze(1).broadcast_to([P, NJ, C]), ALU.add).then_inc(tok_used, 1)
                pool.wait_ge(tok_used, b + 1)
                pool.wait_ge(u_ready, b + 1)
                g.tensor_tensor(u_tok[:, :, :], u_tok[:, :, :], u[:, :, :], ALU.add).then_inc(ut_ready, 1)

            def complete_rows(d):
                wait(pool, scattered, d * 2 * NJ * 16)
                dst = srow[:, :, :, ROW - 1]
                g.tensor_tensor(dst, dst, c_group[:, :, :], ALU.add).then_inc(dst_ready, 1)
                pool.wait_ge(wparts_ready, d + 1)
                pool.sem_inc(waited, 1)
                for k in range(2):
                    ins = g.tensor_copy(srow[:, k, :, 0:C], wparts[:, :, :].bitcast(F32))
                ins.then_inc(rows_ready, 1)

            def scatter(d, tiles_):
                pool.wait_ge(rows_ready, d + 1)
                pool.wait_ge(pos_ready, d + 1)
                pool.sem_inc(waited, 1)
                for j in tiles_:
                    for k in range(2):
                        g.indirect_dma_start(
                            rows[0:NE * REG, :], bass.IndirectOffsetOnAxis(ap=pos[:, k, j:j + 1], axis=0),
                            srow[:, k, j, :], None).then_inc(scattered, 16)

            def largest_weight(c):
                pool.wait_ge(w_max_ready, c + 1)
                pool.sem_inc(waited, 1)
                g.partition_all_reduce(wmax_all[:, :], wmax[:, :], P, bass.bass_isa.ReduceOp.max)\
                    .then_inc(w_max_all, 1)

            def iteration(a=None, b=None, c=None, d=None):
                run(c, late_rstd, 1)
                run(d, complete_rows)
                run(b, token_sum)
                run(a, group_rstd)
                run(c, largest_weight)
                run(d, scatter, (0, 1, 2, 3))
                run(c, late_rstd, 2)
                run(a, token_rstd)
                run(d, scatter, (4, 5, 6, 7))
                run(b, residual)

            pipeline(pool, iteration)

            def take_route(t, b, nth):
                pool.wait_ge(xin_loaded[b], 16 * (nth + 1))
                pool.sem_inc(waited, 1)
                g.tensor_copy(route[:, ds(t, 1), :, :], xin[:, b, :, C:C + 2].unsqueeze(1)).then_inc(route_ready, 1)

            def store(nth, b):
                pool.wait_ge(yout_ready[b], nth + 1)
                pool.sem_inc(waited, 1)
                for h in range(2):
                    g.indirect_dma_start(
                        results[:, :], bass.IndirectOffsetOnAxis(ap=dest[:, b, h:h + 1], axis=0),
                        yout[:, b, h, :], None, bounds_check=DUMP - 1, oob_is_err=False)\
                        .then_inc(y_scattered[b], 16)

            def low_units(t, b):
                pool.wait_ge(h_hi_ready, 3 * t + 1)
                g.tensor_tensor(hparts[:, b, 0:2, 1, :], units[0].rearrange("p (k n) -> p k n", k=2),
                                hparts[:, b, 0:2, 0, :], ALU.subtract).then_inc(h_lo_pool, 1)

            def two_tiles(k):
                take_route(2 * k + 2, 0, k + 1)
                low_units(2 * k + 1, 1)
                if not (isinstance(k, int) and k == 0):
                    store(k - 1, 1)
                take_route(2 * k + 3, 1, k + 1)
                low_units(2 * k + 2, 0)
                store(k, 0)

            take_route(0, 0, 0)
            take_route(1, 1, 0)
            low_units(0, 0)
            first_then_loop(pool, (NT - 1) // 2, two_tiles)
            store((NT - 3) // 2, 1)
            store((NT - 1) // 2, 0)

        @block.tensor
        def _(pe):
            mm = nc.tensor.matmul
            turn = nc.tensor.transpose
            pe.wait_ge(consts_ready, 2)
            mm(bk12[0:C + 1, 0, 0:C + M + 2 * C], diag_g1[:, :], proj[:, :], start=True, stop=True)
            for a in range(2):
                mm(bk12[:, 1, a:a + 1], fc1_n[0:C, a * P:(a + 1) * P], b2c[:, :], start=True, stop=True)
            turn(bk12[:, 1, 8:8 + NE], router_n[:, :], ident[0:NE, 0:NE]).then_inc(pe_setup, 1)
            pe.wait_ge(dve_setup, DVE_SETUP)

            def pair_means(a):
                wait(pe, n1t_ready, 2 * a)
                pe.wait_ge(mean_ready, a + 1)
                mm(gmean_ps, pair_mean[:, :], mv[:, :, 0], start=True, stop=True).then_inc(gmean_ready, 1)

            def pair_variances(a):
                pe.wait_ge(chvar_ready, a + 1)
                mm(gvar_ps, pair_mean[:, :], chvar[:, :], start=True, stop=True).then_inc(gvar_done, 1)

            def convolution(a, s):
                pe.wait_ge(conv_ready, a + 1)
                for f in range(2):
                    o = t_ps[:, (2 * s + f) * P:(2 * s + f + 1) * P]
                    h0 = f * HH // 2
                    mm(o, xres[:, s, h0:h0 + 8, :], ident[:, :], start=True, stop=False)
                    for dy in range(3):
                        last = mm(o, hsum[:, s, h0 + dy:h0 + dy + 8, :], ident[:, :], start=False, stop=dy == 2)
                if s == 1:
                    last.then_inc(t_ready, 1)

            def turn_n1(a):
                pe.wait_ge(n1_ready, a + 1)
                wait(pe, w_stored, 4 * (a - 1))
                for h in range(2):
                    if h == 1:
                        pe.wait_ge(n1t_ready, 2 * a + 1)
                    for j in range(4):
                        last = turn(bk0[0:C + 1, j * P:(j + 1) * P], n1[:, 4 * h + j, :], ident[:, :])
                    last.then_inc(n1_turned, 1)

            def rotate(b):
                pe.wait_ge(n1t_ready, 2 * b + 2)
                wait(pe, att_read, 2 * b)
                for j in range(NJ):
                    last = mm(rot_ps[:, j * M:(j + 1) * M], n1t[:, j * P:(j + 1) * P], rot_aug[:, :],
                              start=True, stop=True)
                last.then_inc(rot_ready, 1)

            def queries(b):
                wait(pe, probt_ready, 4 * b)
                for h in range(2):
                    last = mm(bk34[0:C + 1, h, :], q_aug[:, :], n1t[:, h * 512:(h + 1) * 512], start=True, stop=True)
                last.then_inc(q_ready, 1)

            def bucket_sums(b):
                pe.wait_ge(onehot_ready, b + 1)
                oh_v = onehot[:, :, :].rearrange("p (j h) k -> p j (h k)", j=NJ)
                for m in range(GB):
                    for f in range(2):
                        j = 4 * (m // 2) + 2 * f + m % 2
                        last = mm(pool_ps[M * m:M * (m + 1), :], oh_v[:, j, :], n1[:, j, :],
                                  start=f == 0, stop=f == 1)
                last.then_inc(pool_ready, 1)

            def turn_pooled(b):
                pe.wait_ge(pooled_ready, b + 1)
                turn(poolt_ps, pooled[:, :], ident[:, :]).then_inc(poolt_ready, 1)

            def keys_values(b):
                pe.wait_ge(pooledt_ready, b + 1)
                pe.wait_ge(qt_ready, b + 1)
                mm(k_ps, k_aug[:, :], pooled_t[:, :], start=True, stop=True)
                pe.wait_ge(rep_ready, b + 1)
                for m in range(GB):
                    last = mm(v_ps[:, m, :], pooled_rep[:, m, :, :].rearrange("c h m -> c (h m)"), v_aug[:, :],
                              start=True, stop=True)
                last.then_inc(kv_ready, 1)

            def scores(b, p):
                if p == 0:
                    pe.wait_ge(blk_ready, b + 1)
                if p == 1:
                    wait(pe, pos_ready, b - 1)
                if p >= 2:
                    pe.wait_ge(ssub_ready, 4 * b + p - 1)
                for bp in range(2):
                    j, m = 2 * p + bp, 2 * (p // 2) + bp
                    last = mm(bk12[:, p % 2, bp * 256:(bp + 1) * 256], qt[:, j * P:(j + 1) * P],
                              kblk[:, m, :, :].rearrange("c h m -> c (h m)"), start=True, stop=True)
                last.then_inc(s_ready, 1)

            def turn_prob(b, p):
                pe.wait_ge(prob_ready, 4 * b + p + 1)
                wait(pe, probt_ready, 4 * b + p - 1)
                for a in range(4):
                    last = turn(bk34[:, p % 2, a * P:(a + 1) * P], prob[:, p % 2, a, :], ident[:, :])
                last.then_inc(probt_turned, 1)

            def attend(b, p):
                pe.wait_ge(probt_ready, 4 * b + p + 1)
                if p == 2:
                    pe.wait_ge(att_read, 2 * b + 1)
                for bp in range(2):
                    m = 2 * (p // 2) + bp
                    for ch in range(2):
                        last = mm(av_ps[:, 2 * (p % 2) + bp, :], prob_t[:, p % 2, 2 * bp + ch, :],
                                  vblk[:, m, ch, :], start=ch == 0, stop=ch == 1)
                last.then_inc(av_ready, 1)

            def turn_n2(c):
                pe.wait_ge(n2s_ready, c + 1)
                for j in range(NJ):
                    last = turn(bk6.bitcast(F16)[:, j * P:(j + 1) * P], n2s[:, j, :], ident16[:, :])
                last.then_inc(n2_turned, 1)

            def fc1(c, h):
                pe.wait_ge(n2t_ready, c + 1)
                for a in range(2):
                    q = 2 * h + a
                    if h == 1:
                        pe.wait_ge(hid_ready, 4 * c + q - 1)
                    for part in range(2):
                        last = mm(fc1_ps[a], fc1_p[:, part, a * P:(a + 1) * P], n2t[:, h * 512:(h + 1) * 512],
                                  start=part == 0, stop=part == 1)
                    last.then_inc(fc1_ready, 1)

            def fc2(c):
                for j in range(NJ):
                    if j % 4 == 0:
                        pe.wait_ge(hid_ready, 4 * c + 3 + j // 4)
                    for a in range(2):
                        last = mm(y_ps[:, j, :], hid[:, a, j * P:(j + 1) * P], fc2_s[:, a, :],
                                  start=a == 0, stop=a == 1)
                last.then_inc(y_ready, 1)

            def turn_wtok(c):
                pe.wait_ge(wparts_ready, c + 1)
                for j in range(NJ):
                    last = turn(bk6.bitcast(F16)[:, j * P:(j + 1) * P], wparts[:, j, :], ident16[:, :])
                last.then_inc(wt_turned, 1)

            def router(d):
                pe.wait_ge(wt_ready, d + 1)
                for j in range(NJ):
                    for part in range(2):
                        last = mm(l_ps[:, j, :], wtok_t[:, j * P:(j + 1) * P], router_p[:, part, :],
                                  start=part == 0, stop=part == 1)
                last.then_inc(router_ready, 1)

            def places(d):
                pe.wait_ge(passed_ready, d + 1)
                mm(pos_ps, before[:, :], picked[:, :, 1:NJ + 1], start=True, stop=False)
                mm(pos_ps, ones[:, :], passed[:, :, 0:NJ], start=False, stop=True).then_inc(pos_counted, 1)

            def turn_weights(c, part):
                wait(pe, w_stored, 4 * c + part)
                if part == 0:
                    pe.wait_ge(w_parts_ready, c + 1)
                if part == 3:
                    pe.sem_inc(waited, 1)
                    for ch in range(CH):
                        for low in range(2):
                            src = w2_parts[:, low, ch:CF * P:CF] if ch < CF else w2_parts[:, low, CF * P:CH * P]
                            last = turn(bk0[:, :].bitcast(F16)[:, (2 * ch + low) * C:(2 * ch + low + 1) * C], src,
                                        ident16[0:C, 0:C])
                else:
                    pe.sem_inc(waited, 1)
                    for q in range(8 * part, 8 * part + 8):
                        t, ch, low = q // (2 * CH), q // 2 % CH, q % 2
                        for copy in range(2):
                            last = turn(w_turn_ps[copy * C:(copy + 1) * C, (q % 8) * P:(q % 8 + 1) * P],
                                        (w_hi, w_lo)[low][:, t, ch, :], ident16[:, :])
                last.then_inc(w_turned, 1)

            def iteration(a=None, b=None, c=None, d=None):
                run(d, router)
                run(a, pair_means)
                run(b, rotate)
                run(b, queries)
                run(a, pair_variances)
                run(b, bucket_sums)
                run(b, turn_pooled)
                run(c, turn_n2)
                run(b, keys_values)
                run(d, places)
                run(c, fc1, 0)
                run(a, convolution, 0)
                run(c, fc1, 1)
                run(b, scores, 0)
                run(b, scores, 1)
                run(a, convolution, 1)
                run(c, fc2)
                run(b, scores, 2)
                run(b, turn_prob, 0)
                run(b, turn_prob, 1)
                run(b, attend, 1)
                run(b, attend, 0)
                run(b, scores, 3)
                run(b, turn_prob, 2)
                run(c, turn_weights, 0)
                run(b, attend, 2)
                run(b, turn_prob, 3)
                run(c, turn_weights, 1)
                run(b, attend, 3)
                run(c, turn_weights, 2)
                run(c, turn_wtok)
                run(c, turn_weights, 3)
                run(a, turn_n1)

            pipeline(pe, iteration)

            pe.wait_ge(sums_kept, NG)
            pe.wait_ge(w_stored, 4 * NG)
            mm(bk7[:, 0:NE], ones[:, :], picked[:, :, 0], start=True, stop=True).then_inc(counted, 1)
            pe.wait_ge(sched_ready, 1)
            xt_ps = bk7[:, :].bitcast(F16)

            def turn_rows(t, b, nth):
                pe.wait_ge(xin_loaded[b], 16 * (nth + 1))
                wait(pe, xs_ready, t)
                for h in range(2):
                    last = turn(xt_ps[:, h * P:(h + 1) * P], xin[:, b, h, 0:C].bitcast(F16), ident16[:, :])
                last.then_inc(xt_turned, 1)

            def experts_from(t):
                number = pe.value_load(window_experts[0:1, ds(t, 1)], min_val=0,
                                       max_val=(1 << (WINDOW * EXPERT_BITS)) - 1)
                return [(number >> (EXPERT_BITS * m)) & ((1 << EXPERT_BITS) - 1) for m in range(WINDOW)]

            def up(t, b, e, between):
                pe.wait_ge(xs_ready, t + 1)
                for q in range(CH // 2):
                    m = (3 * b + q) % 2
                    for w, bank, free, ready in ((0, bk12, silu_ready, h1_ready), (1, bk34, h_ready, h3_ready)):
                        wait(pe, free, 3 * t + q - 1)
                        for ch in range(2):
                            for part in range(2):
                                last = mm(bank[:, m, ch * MT:(ch + 1) * MT],
                                          w13[:, ds(e, 1), w, 2 * q + ch, part, :].rearrange("p o n -> p (o n)"),
                                          xs[:, b, :], start=part == 0, stop=part == 1)
                        last.then_inc(ready, 1)
                    if between is not None:
                        between(q)

            def down(t, b, nth, e, q):
                if q == 0:
                    wait(pe, yout_ready[b], nth)
                    pe.wait_ge(h_lo_pool, t + 1)
                else:
                    pe.wait_ge(h_lo_dve, 2 * t + q)
                for ch in (2 * q, 2 * q + 1):
                    for h in range(2):
                        o = bk56[:, b, h * 2 * C:(h + 1) * 2 * C]
                        mm(o, hparts[:, b, ch, 0, h * P:(h + 1) * P],
                           w2s[:, ds(e, 1), ch, :, :].rearrange("p o a n -> p (o a n)"), start=ch == 0 and h == 0, stop=False)
                        last = mm(o[:, 0:C], hparts[:, b, ch, 1, h * P:(h + 1) * P],
                                  w2s[:, ds(e, 1), ch, 0, :].rearrange("p o n -> p (o n)"),
                                  start=False, stop=ch == CH - 1 and h == 1)
                if q == 2:
                    last.then_inc(e_y_ready, 1)

            turn_rows(0, 0, 0)
            turn_rows(1, 1, 0)
            pe.wait_ge(experts_packed, 1)
            up(0, 0, experts_from(0)[0], None)

            def two_tiles(k, experts=None):
                turn_rows(2 * k + 2, 0, k + 1)
                experts = experts or experts_from(2 * k)
                up(2 * k + 1, 1, experts[1], lambda q: down(2 * k, 0, k, experts[0], q))
                turn_rows(2 * k + 3, 1, k + 1)
                up(2 * k + 2, 0, experts[2], lambda q: down(2 * k + 1, 1, k, experts[1], q))
                return experts[2:]

            first_then_loop(pe, (NT - 1) // 2, two_tiles, first=2, unrolled=UNROLLED)
            e = experts_from(NT - 1)[0]
            for q in range(CH // 2):
                down(NT - 1, 0, (NT - 1) // 2, e, q)

            def turn_output(k):
                for b in range(2):
                    pe.wait_ge(t3_ready, 2 * k + b + 1)
                    wait(pe, og_ready[b], k)
                    for a in range(4):
                        last = turn(bk12[:, b, a * P:(a + 1) * P], t3[:, b, 2 * a:2 * a + 2, :], ident[:, :])
                    last.then_inc(o_turned[b], 1)

            first_then_loop(pe, NG // 2, turn_output)

        @block.scalar
        def _(act):
            f = nc.scalar.activation
            act.wait_ge(consts_ready, 1)
            def store_tokens(a):
                act.wait_ge(t_ready, a + 1)
                wait(act, tok_used, a)
                f(tok[:, :, :], t_ps.rearrange("p (j c) -> p j c", j=NJ), ACT.Copy).then_inc(tok_ready, 1)

            def squares1(a):
                act.wait_ge(cent1_ready, a + 1)
                f(sq_a[:, :, :], cent_a[:, :, :], ACT.Square).then_inc(sq1_ready, 1)

            def store_n1t(a, h):
                act.wait_ge(n1_turned, 2 * a + h + 1)
                f(n1t[:, h * 512:(h + 1) * 512], bk0[0:C + 1, :], ACT.Copy).then_inc(n1t_ready, 1)

            def store_queries(b):
                act.wait_ge(q_ready, b + 1)
                f(qt[:, :], bk34[0:C + 1, :, :].rearrange("c a n -> c (a n)"), ACT.Copy).then_inc(qt_ready, 1)

            def repeat_pooled(b):
                act.wait_ge(pooledt_ready, b + 1)
                for m in range(GB):
                    ins = f(pooled_rep[:, m, :, :],
                            pooled_t[0:C + 1, M * m:M * (m + 1)].unsqueeze(1).broadcast_to([C + 1, 4, M]), ACT.Copy)
                ins.then_inc(rep_ready, 1)

            def exponentials(b, p):
                act.wait_ge(ssub_ready, 4 * b + p + 1)
                wait(act, probt_turned, 4 * b + p - 1)
                f(prob[:, p % 2, :, :].rearrange("p a n -> p (a n)"),
                  ssub[:, p % 2, :, :].rearrange("p h m -> p (h m)"), ACT.Exp, scale=DH ** -0.5)\
                    .then_inc(prob_ready, 1)

            def store_prob(b, p):
                act.wait_ge(probt_turned, 4 * b + p + 1)
                wait(act, av_ready, 4 * b + p - 1)
                f(prob_t[:, p % 2, :, :].rearrange("p a n -> p (a n)"), bk34[:, p % 2, :], ACT.Copy)\
                    .then_inc(probt_ready, 1)

            def squares2(b):
                act.wait_ge(cent2_ready, b + 1)
                f(sq_c[:, :, :], cent_c[:, :, :], ACT.Square).then_inc(sq2_ready, 1)

            def high_n2(c):
                act.wait_ge(n2_ready, c + 1)
                f(n2s[:, :, 0:C], n2[:, :, :], ACT.Copy, scale=XS).then_inc(n2hi_ready, 1)

            def store_n2t(c):
                act.wait_ge(n2_turned, c + 1)
                f(n2t, bk6.bitcast(F16), ACT.Copy).then_inc(n2t_ready, 1)

            def gelus(c, h):
                back = small_back[:, 0:1].bitcast(F32)
                for a in range(2):
                    act.wait_ge(fc1_ready, 4 * c + 2 * h + a + 1)
                    f(hid[:, a, h * 512:(h + 1) * 512], fc1_ps[a], ACT.Gelu, bias=fc1_bias[:, a:a + 1], scale=back)\
                        .then_inc(hid_ready, 1)

            def squares3(c):
                act.wait_ge(cent3_ready, c + 1)
                f(sq_c[:, :, :], cent_c[:, :, :], ACT.Square).then_inc(sq3_ready, 1)

            def high_wtok(c):
                act.wait_ge(wtok_ready, c + 1)
                wait(act, rows_ready, c)
                f(wparts[:, :, 0:C], wtok[:, :, :], ACT.Copy, scale=XS).then_inc(whi_ready, 1)

            def store_wtok(c):
                act.wait_ge(wt_turned, c + 1)
                f(wtok_t, bk6.bitcast(F16), ACT.Copy).then_inc(wt_ready, 1)

            def router_exp(d):
                act.wait_ge(lsub_ready, d + 1)
                f(lexp[:, :, :], lsub[:, :, :], ACT.Exp, scale=small_back[:, 1:2].bitcast(F32)).then_inc(lexp_ready, 1)

            def high_weights(c):
                act.wait_ge(w_scale_ready, c + 1)
                wait(act, w_turned, 4 * c)
                for t in range(2):
                    f(w_hi[:, t, :, :].rearrange("p k c -> p (k c)"), wn[:, t, :, :].rearrange("p k c -> p (k c)"),
                      ACT.Copy, scale=wscale[:, t:t + 1].bitcast(F32)).then_inc(w_hi_ready, 1)
                f(w2_parts[:, 0, :], w2n[:, :], ACT.Copy, scale=wscale[0:C, 2:3].bitcast(F32)).then_inc(w_hi_ready, 1)

            def store_weights(c, part):
                act.wait_ge(w_turned, 4 * c + part + 1)
                act.sem_inc(waited, 1)
                f(w13_q[:, ds(c, 1), 8 * part:8 * part + 8, :].rearrange("p o q n -> p (o q n)"),
                  w_turn_ps, ACT.Copy).then_inc(w_stored, 1)

            def iteration(a=None, b=None, c=None, d=None):
                run(d, router_exp)
                run(c, high_n2)
                run(b, store_queries)
                run(b, repeat_pooled)
                run(c, store_n2t)
                run(c, gelus, 0)
                run(c, gelus, 1)
                run(a, store_tokens)
                run(b, exponentials, 0)
                run(b, exponentials, 1)
                run(c, high_weights)
                run(a, squares1)
                run(b, store_prob, 0)
                run(b, store_prob, 1)
                run(b, exponentials, 2)
                run(c, squares3)
                run(b, store_prob, 2)
                run(c, store_weights, 0)
                run(b, exponentials, 3)
                run(b, store_prob, 3)
                run(c, high_wtok)
                run(c, store_weights, 1)
                run(c, store_wtok)
                run(a, store_n1t, 0)
                run(b, squares2)
                run(a, store_n1t, 1)

            pipeline(act, iteration)

            act.wait_ge(sched_ready, 1)
            for e in range(NE // 2, NE):
                write_pad(act, act.value_load(pad_row[0:1, e:e + 1], min_val=0, max_val=NE * REG - MT))
            act.wait_ge(sched_ready, 2)

            def store_xs(t, b):
                act.wait_ge(xt_turned, t + 1)
                wait(act, h3_ready, 3 * t - 3)
                f(xs[:, b, :], bk7[:, :].bitcast(F16)[:, 0:MT], ACT.Copy).then_inc(xs_ready, 1)

            def silu_of(t, b, q):
                back = tile_back[:, ds(t, 1), 0:1].rearrange("p o n -> p (o n)")
                m = (3 * b + q) % 2
                act.wait_ge(h1_ready, 3 * t + q + 1)
                wait(act, h_ready, 3 * t + q - 1)
                act.sem_inc(waited, 1)
                f(silu[:, m, :], bk12[:, m, :], ACT.Silu, scale=back).then_inc(silu_ready, 1)

            def high_units(t, b, q):
                act.wait_ge(h_ready, 3 * t + q + 1)
                wait(act, e_y_ready, t - 1)
                f(hparts[:, b, 2 * q:2 * q + 2, 0, :], units[q].rearrange("p (k n) -> p k n", k=2), ACT.Copy)\
                    .then_inc(h_hi_ready, 1)

            def low_result(t, b, nth):
                factor = tile_back[:, ds(t, 1), 2:3].rearrange("p o n -> p (o n)")
                y_low = bk56[:, b, 0:4 * C].rearrange("p (h a c) -> p h a c", h=2, a=2)[:, :, 1, :]
                act.wait_ge(e_y_ready, t + 1)
                wait(act, yout_ready[b], nth)
                act.sem_inc(waited, 1)
                f(ylow[:, b, :, :], y_low, ACT.Copy, scale=factor).then_inc(ylow_ready, 1)

            def one_tile(t, b, nth):
                if not (isinstance(t, int) and t == 0):
                    high_units(t - 1, 1 - b, 2)
                if not (isinstance(t, int) and t < 2):
                    low_result(t - 2, b, nth)
                silu_of(t, b, 0)
                if not (isinstance(t, int) and t == NT - 1):
                    store_xs(t + 1, 1 - b)
                silu_of(t, b, 1)
                high_units(t, b, 0)
                silu_of(t, b, 2)
                high_units(t, b, 1)

            def two_tiles(k):
                one_tile(2 * k + 1, 1, k - 1)
                one_tile(2 * k + 2, 0, k)

            store_xs(0, 0)
            one_tile(0, 0, 0)
            first_then_loop(act, (NT - 1) // 2, two_tiles, first=2, unrolled=UNROLLED)
            high_units(NT - 1, 0, 2)
            low_result(NT - 2, 1, (NT - 2) // 2)
            low_result(NT - 1, 0, (NT - 1) // 2)

            out_rows = out.rearrange("b c h w -> (b c) (h w)").rearrange("(g s p) n -> g p s n", g=NG, s=2)

            def store_output(k):
                for b in range(2):
                    act.wait_ge(o_turned[b], k + 1)
                    wait(act, out_stored[b], 16 * k)
                    f(og[:, b, :], bk12[:, b, :], ACT.Copy).then_inc(og_ready[b], 1)
                    act.wait_ge(og_ready[b], k + 1)
                    act.dma_start(out_rows[ds(2 * k + b, 1)].rearrange("g p s n -> (g p) s n"),
                                  og[:, b, :].rearrange("p (s n) -> p s n", s=2)).then_inc(out_stored[b], 16)

            first_then_loop(act, NG // 2, store_output)
            for b in range(2):
                act.wait_ge(out_stored[b], 16 * (NG // 2))

        @block.vector
        def _(dve):
            v = nc.vector
            tt = v.tensor_tensor

            def wide(col, n):
                return col.unsqueeze(2).broadcast_to([col.shape[0], col.shape[1], n])

            setup = [0]

            def setup_done(ins, wait=True):
                setup[0] += 1
                ins.then_inc(dve_setup, 1)
                if wait:
                    dve.wait_ge(dve_setup, setup[0])

            dve.wait_ge(pe_setup, 1)
            setup_done(v.tensor_copy(q_aug[:, 0:C], bk12[0:C + 1, 0, 0:C]), wait=False)
            setup_done(v.tensor_copy(rot_aug[:, :], bk12[0:C + 1, 0, C:C + M]), wait=False)
            setup_done(v.tensor_copy(k_aug[0:C + 1, 0:C], bk12[0:C + 1, 0, C + M:2 * C + M]), wait=False)
            setup_done(v.tensor_copy(v_aug[:, :], bk12[0:C + 1, 0, 2 * C + M:3 * C + M]), wait=False)
            setup_done(v.tensor_copy(router_t[:, :], bk12[:, 1, 8:8 + NE]), wait=False)
            setup_done(v.tensor_scalar(fc1_s[:, :], fc1_n[:, :], g2[:, 0:1], None, ALU.mult), wait=False)
            setup_done(tt(fc1_bias[:, :], bk12[:, 1, 0:2], fc1_bias0[:, :], ALU.add))

            def scales(largest, exponent, scale, back, step_done):
                step_done(v.tensor_scalar(largest, largest, TINY, None, ALU.max))
                step_done(v.tensor_scalar(exponent, largest.bitcast(U32), EXP_MASK, None, ALU.bitwise_and))
                v.tensor_scalar(back, exponent, float(-BACK_EXP << 23), None, ALU.add)
                return v.tensor_scalar(scale, exponent, -1.0, float(SCALE_EXP << 23), ALU.mult, ALU.add)

            biggest = dict(axis=AX.X, op=ALU.max, apply_absolute_value=True)
            v.tensor_reduce(small_max[:, 0:1], fc1_s[:, :], **biggest)
            v.tensor_reduce(small_max[:, 1:2], router_t[:, :], **biggest).then_inc(small_max_ready, 1)
            dve.wait_ge(small_max_all_ready, 1)
            setup_done(scales(small_max_all[:, :], wexp[:, 0:2], small_scale[:, :], small_back[:, :], setup_done))
            for m, (full, parts) in enumerate(((fc1_s, fc1_p), (router_t, router_p))):
                by = small_scale[:, m:m + 1].bitcast(F32)
                setup_done(v.tensor_scalar(parts[:, 0, :], full[:, :], by, None, ALU.mult))
                setup_done(v.scalar_tensor_tensor(out=parts[:, 1, :], in0=full[:, :], scalar=by, in1=parts[:, 0, :],
                                                  op0=ALU.mult, op1=ALU.subtract))
            assert setup[0] == DVE_SETUP

            step_sem = dict(a=a_step, b=b_step, c=c_step, d=d_step, w=w_step)
            count = {}

            def chained(stage, group):
                def done(ins):
                    count[stage] += 1
                    ins.then_inc(step_sem[stage], 1)
                    dve.wait_ge(step_sem[stage], group * STEPS[stage] + count[stage])
                return done

            def channel_statistics(a):
                done = chained("a", a)
                dve.wait_ge(x_loaded, 16 * a + 16)
                xf = xg[:, :, :, :].rearrange("p s h w -> p s (h w)")
                v.bn_stats(bst[:, 0, :], xf[:, 0, :])
                done(v.bn_stats(bst[:, 1, :], xf[:, 1, :]))
                dve.sem_inc(waited, 1)
                v.bn_aggr(mv[:, 0, :], bst[:, 0, :])
                v.bn_aggr(mv[:, 1, :], bst[:, 1, :]).then_inc(mean_ready, 1)

            def channel_variances(a):
                done = chained("a", a)
                dve.wait_ge(mean_ready, a + 1)
                dve.wait_ge(gmean_ready, a + 1)
                done(tt(dmean[:, :], mv[:, :, 0], gmean_ps, ALU.subtract))
                done(tt(dmean2[:, :], dmean[:, :], dmean[:, :], ALU.mult))
                tt(chvar[:, :], dmean2[:, :], mv[:, :, 1], ALU.add).then_inc(chvar_ready, 1)

            def pair_statistics(a):
                done = chained("a", a)
                dve.wait_ge(gvar_done, a + 1)
                v.tensor_scalar(gvar[:, :], gvar_ps, EPS, None, ALU.add).then_inc(gvar_ready, 1)
                done(v.tensor_copy(gmean[:, :], gmean_ps))

            def row_sums(a):
                done = chained("a", a)
                dve.wait_ge(grstd_ready, a + 1)
                for s in range(2):
                    ins = v.tensor_scalar(xpad[:, s, 1:HH + 1, 1:WW + 1], xg[:, s, :, :], gmean[:, s:s + 1],
                                          grstd[:, s:s + 1], ALU.subtract, ALU.mult)
                done(ins)
                inner = xpad[:, :, 1:HH + 1, :]
                hin = hsum[:, :, 1:HH + 1, :]
                tt(hin, inner[:, :, :, 0:WW], inner[:, :, :, 1:WW + 1], ALU.add)
                for s in range(2):
                    ins = v.scalar_tensor_tensor(out=xres[:, s, :, :], in0=xg[:, s, :, :], scalar=bias2[:, 0:1],
                                                 in1=xpad[:, s, 1:HH + 1, 1:WW + 1], op0=ALU.add, op1=ALU.add)
                ins.then_inc(x_used, 1)
                dve.wait_ge(x_used, a + 1)
                tt(hin, hin, inner[:, :, :, 2:WW + 2], ALU.add).then_inc(conv_ready, 1)

            def centre_tokens(done, src, ssum, cent, ready):
                done(v.tensor_reduce(ssum[:, :], src, AX.X, ALU.add))
                v.scalar_tensor_tensor(out=cent[:, :, :], in0=wide(ssum[:, :], C), scalar=-1.0 / C, in1=src,
                                       op0=ALU.mult, op1=ALU.add).then_inc(ready, 1)

            def centre1(a):
                dve.wait_ge(tok_ready, a + 1)
                centre_tokens(chained("a", a), tok[:, :, :], ssum_a, cent_a, cent1_ready)

            def variance1(a):
                done = chained("a", a)
                dve.wait_ge(sq1_ready, a + 1)
                done(v.tensor_reduce(ssq_a[:, :], sq_a[:, :, :], AX.X, ALU.add))
                v.tensor_scalar(v64[:, :], ssq_a[:, :], 1.0 / C, None, ALU.mult)
                v.tensor_scalar(vare_a[:, :], ssq_a[:, :], 1.0 / C, EPS, ALU.mult, ALU.add).then_inc(vare1_ready, 1)

            def normalise1(a):
                dve.wait_ge(r12_ready, a + 1)
                tt(n1[:, :, 0:C], cent_a[:, :, :], wide(r12[:, :], C), ALU.mult).then_inc(n1_ready, 1)

            def normalise0(b):
                wait(dve, ut_ready, b)
                tt(u[:, :, :], cent_a[:, :, :], wide(r1[:, :], C), ALU.mult).then_inc(u_ready, 1)

            def buckets(b):
                done = chained("b", b)
                dve.wait_ge(rot_ready, b + 1)
                rot = rot_ps.rearrange("p (a k) -> p a k", k=BUCKETS)
                done(v.tensor_reduce(bmax[:, :], rot, AX.X, ALU.max))
                done(tt(beq[:, :, :], rot, wide(bmax[:, :], BUCKETS), ALU.is_equal))
                rank = descend[:, :].unsqueeze(1).broadcast_to([P, NJ * HASHES, BUCKETS])
                done(tt(beq[:, :, :], beq[:, :, :], rank, ALU.mult))
                done(v.tensor_reduce(bfirst[:, :], beq[:, :, :], AX.X, ALU.max))
                tt(onehot[:, :, :], beq[:, :, :], wide(bfirst[:, :], BUCKETS), ALU.is_equal).then_inc(onehot_ready, 1)

            def bucket_means(b):
                done = chained("b", b)
                dve.wait_ge(pool_ready, b + 1)
                n_in = pool_ps[:, C:C + 1]
                v.tensor_scalar(pooled[:, C + 1:C + 2], n_in, 1.0, MASKED, ALU.is_lt, ALU.mult)
                done(v.tensor_scalar(cnt[:, :], n_in, 1e-20, None, ALU.add))
                done(v.reciprocal(rcnt[:, :], cnt[:, :]))
                v.tensor_scalar(pooled[:, 0:C + 1], pool_ps, rcnt[:, 0:1], None, ALU.mult).then_inc(pooled_ready, 1)

            def store_pooled(b):
                dve.wait_ge(poolt_ready, b + 1)
                v.tensor_copy(pooled_t[:, :], poolt_ps).then_inc(pooledt_ready, 1)

            def key_value_blocks(b):
                dve.wait_ge(kv_ready, b + 1)
                for m in range(GB):
                    tt(kblk[:, m, :, :], k_ps[:, M * m:M * (m + 1)].unsqueeze(1).broadcast_to([C + 1, HEADS, M]),
                       wide(head_of[:, :], M), ALU.mult)
                for ch in range(2):
                    ins = tt(vblk[:, :, ch, 0:C], v_ps,
                             v_mask[:, ch, :].unsqueeze(1).broadcast_to([P, GB, C]), ALU.mult)
                ins.then_inc(blk_ready, 1)

            def centre_scores(b, p):
                done = chained("b", b)
                dve.wait_ge(s_ready, 4 * b + p + 1)
                s_ps = bk12[:, p % 2, :].rearrange("p (h m) -> p h m", m=M)
                done(v.tensor_reduce(smax[:, p % 2, :], s_ps, AX.X, ALU.max))
                wait(dve, prob_ready, 4 * b + p - 1)
                tt(ssub[:, p % 2, :, :], s_ps, wide(smax[:, p % 2, :], M), ALU.subtract).then_inc(ssub_ready, 1)

            def attended(b, s):
                done = chained("b", b)
                dve.wait_ge(av_ready, 4 * b + 2 * s + 2)
                done(v.reciprocal(rden[:, s, :, :], av_ps[:, :, C:C + HEADS]))
                o = av_ps[:, :, 0:C].rearrange("p j (h d) -> p j h d", d=DH)
                r = rden[:, s, :, :].unsqueeze(3).broadcast_to([P, 4, HEADS, DH])
                if s == 0:
                    wait(dve, x2t_ready, b)
                tt(att[:, s, :, :].rearrange("p j (h d) -> p j h d", d=DH), o, r, ALU.mult).then_inc(att_read, 1)

            def centre2(b):
                done = chained("b", b)
                dve.wait_ge(att_read, 2 * b + 2)
                done(tt(x2[:, :, :].rearrange("p j c -> p (j c)"), u[:, :, :].rearrange("p j c -> p (j c)"),
                        att[:, :, :, :].rearrange("p s j c -> p (s j c)"), ALU.add))
                centre_tokens(done, x2[:, :, :], ssum_c, cent_c, cent2_ready)

            def variance_c(c, k, squares_ready):
                done = chained("c", c)
                dve.wait_ge(squares_ready, c + 1)
                done(v.tensor_reduce(ssq_c[:, :], sq_c[:, :, :], AX.X, ALU.add))
                v.tensor_scalar(vare_c[:, :], ssq_c[:, :], 1.0 / C, EPS, ALU.mult, ALU.add).then_inc(vare_c_ready, 1)

            def normalise2(c):
                dve.wait_ge(rc_ready, 2 * c + 1)
                tt(n2[:, :, :], cent_c[:, :, :], wide(rc[:, :], C), ALU.mult).then_inc(n2_ready, 1)

            def low_n2(c):
                dve.wait_ge(n2_ready, c + 1)
                dve.wait_ge(n2hi_ready, c + 1)
                v.scalar_tensor_tensor(out=n2s[:, :, C:2 * C], in0=n2[:, :, :], scalar=XS, in1=n2s[:, :, 0:C],
                                       op0=ALU.mult, op1=ALU.subtract).then_inc(n2s_ready, 1)

            def centre3(c):
                done = chained("c", c)
                dve.wait_ge(x2t_ready, c + 1)
                dve.wait_ge(y_ready, c + 1)
                tt(t2[:, :, :], x2t[:, :, :], y_ps, ALU.add).then_inc(t2_ready, 1)
                dve.wait_ge(t2_ready, c + 1)
                centre_tokens(done, t2[:, :, :], ssum_c, cent_c, cent3_ready)
                v.tensor_copy(t2_all[:, ds(c, 1), :, :].rearrange("p o j c -> p (o j c)"),
                              t2[:, :, :].rearrange("p j c -> p (j c)"))

            def normalise3(c):
                dve.wait_ge(rc_ready, 2 * c + 2)
                tt(wtok[:, :, :], cent_c[:, :, :], wide(rc[:, :], C), ALU.mult).then_inc(wtok_ready, 1)

            def low_wtok(c):
                dve.wait_ge(wtok_ready, c + 1)
                dve.wait_ge(whi_ready, c + 1)
                v.scalar_tensor_tensor(out=wparts[:, :, C:2 * C], in0=wtok[:, :, :], scalar=XS,
                                       in1=wparts[:, :, 0:C], op0=ALU.mult, op1=ALU.subtract).then_inc(wparts_ready, 1)

            def centre_logits(d):
                done = chained("d", d)
                dve.wait_ge(router_ready, d + 1)
                done(v.tensor_reduce(lmax[:, :], l_ps, AX.X, ALU.max))
                tt(lsub[:, :, :], l_ps, wide(lmax[:, :], NE), ALU.subtract).then_inc(lsub_ready, 1)

            def picks(d, half):
                done = chained("d", d)
                order = descend[:, :].unsqueeze(1).broadcast_to([P, NJ, NE])

                def pick(src, k):
                    done(v.tensor_reduce(pk[:, k, :], src, AX.X, ALU.max))
                    done(tt(peq[:, :, :], src, wide(pk[:, k, :], NE), ALU.is_equal))
                    done(tt(peq[:, :, :], peq[:, :, :], order, ALU.mult))
                    done(v.tensor_reduce(pfirst[:, :], peq[:, :, :], AX.X, ALU.max))
                    done(tt(oh[:, k, :, :], peq[:, :, :], wide(pfirst[:, :], NE), ALU.is_equal))

                if half == 0:
                    dve.wait_ge(lexp_ready, d + 1)
                    done(v.tensor_reduce(lden[:, :], lexp[:, :, :], AX.X, ALU.add))
                    done(v.reciprocal(lrec[:, :], lden[:, :]))
                    done(tt(pr[:, :, :], lexp[:, :, :], wide(lrec[:, :], NE), ALU.mult))
                    pick(pr[:, :, :], 0)
                    done(v.scalar_tensor_tensor(out=prest[:, :, :], in0=oh[:, 0, :, :], scalar=-2.0,
                                                in1=pr[:, :, :], op0=ALU.mult, op1=ALU.add))
                    return
                pick(prest[:, :, :], 1)
                by_e = "p j e -> p e j"
                tt(picked[:, :, 1:NJ + 1], oh[:, 0, :, :].rearrange(by_e), oh[:, 1, :, :].rearrange(by_e), ALU.add)
                done(tt(gsum[:, :], pk[:, 0, :], pk[:, 1, :], ALU.add))
                flat9 = "p e j -> p (e j)"
                v.tensor_tensor_scan(passed[:, :, :].rearrange(flat9), scan_keep[:, :, :].rearrange(flat9),
                                     picked[:, :, :].rearrange(flat9), 0.0, ALU.mult, ALU.add)\
                    .then_inc(passed_ready, 1)
                done(v.tensor_scalar(gsum[:, :], gsum[:, :], 1e-9, None, ALU.add))
                done(v.reciprocal(grec[:, :], gsum[:, :]))
                dve.wait_ge(dst_ready, d + 1)
                for k in range(2):
                    tt(srow[:, k, :, C], pk[:, k, :], grec[:, :], ALU.mult)

            def row_places(d):
                done = chained("d", d)
                by_e = "p j e -> p e j"
                dve.wait_ge(pos_counted, d + 1)
                v.tensor_copy(picked[:, :, 0], passed[:, :, NJ]).then_inc(sums_kept, 1)
                done(tt(posall[:, :, :], pos_ps, region[:, :, :], ALU.add))
                for k in range(2):
                    ins = tt(posk[:, k, :, :], posall[:, :, :], oh[:, k, :, :].rearrange(by_e), ALU.mult)
                done(ins)
                for k in range(2):
                    ins = v.tensor_reduce(posf[:, k, :], posk[:, k, :, :].rearrange("p e j -> p j e"), AX.X, ALU.add)
                done(ins)
                v.tensor_copy(pos[:, :, :], posf[:, :, :]).then_inc(pos_ready, 1)

            def largest_weight(c):
                dve.wait_ge(experts_loaded, 64 * c + 64)
                dve.wait_ge(w2_loaded, 16 * c + 16)
                v.tensor_reduce(wmax[0:C, 2:3], w2n[:, :], **biggest)
                v.tensor_reduce(wmax[:, 0:2], wn[:, :, :, :].rearrange("p t k c -> p t (k c)"), **biggest)\
                    .then_inc(w_max_ready, 1)

            def weight_scales(c):
                done = chained("w", c)
                dve.wait_ge(w_max_all, c + 1)
                scales(wmax_all[:, :], wexp[:, :], wscale[:, :], wpow[:, :], done).then_inc(w_scale_ready, 1)
                dve.wait_ge(w_scale_ready, c + 1)
                inverse = wpow[:, :].bitcast(F32)
                v.tensor_copy(wfactor[:, 0:1], inverse[:, 0:1])
                v.tensor_scalar(wfactor[:, 1:2], wscale[:, 0:1].bitcast(F32), 2.0 ** (1 - 13 - BACK_EXP), None, ALU.mult)
                done(v.scalar_tensor_tensor(out=wprod[:, :], in0=inverse[:, 0:1], scalar=2.0 ** BACK_EXP,
                                            in1=inverse[:, 1:2], op0=ALU.mult, op1=ALU.mult))
                done(v.scalar_tensor_tensor(out=wfactor[:, 2:3], in0=wprod[:, :],
                                            scalar=2.0 ** (2 * BACK_EXP - 1 - 13), in1=inverse[:, 2:3],
                                            op0=ALU.mult, op1=ALU.mult))
                dve.sem_inc(waited, 1)
                v.tensor_copy(wback[:, ds(c, 1), :].rearrange("p o t -> p (o t)"), wfactor[:, :])

            def low_weights(c):
                flat = "p k c -> p (k c)"
                for t in range(2):
                    dve.wait_ge(w_hi_ready, 3 * c + t + 1)
                    v.scalar_tensor_tensor(
                        out=w_lo[:, t, :, :].rearrange(flat), in0=wn[:, t, :, :].rearrange(flat),
                        scalar=wscale[:, t:t + 1].bitcast(F32), in1=w_hi[:, t, :, :].rearrange(flat),
                        op0=ALU.mult, op1=ALU.subtract)
                dve.wait_ge(w_hi_ready, 3 * c + 3)
                v.scalar_tensor_tensor(
                    out=w2_parts[:, 1, :], in0=w2n[:, :], scalar=wscale[0:C, 2:3].bitcast(F32),
                    in1=w2_parts[:, 0, :], op0=ALU.mult, op1=ALU.subtract).then_inc(w_parts_ready, 1)

            def store_weights(c, part):
                dve.wait_ge(w_turned, 4 * c + part + 1)
                dve.sem_inc(waited, 1)
                if part == 2:
                    dst, src = w13_q[:, ds(c, 1), 16:24, :].rearrange("p o q n -> p (o q n)"), w_turn_ps
                else:
                    dst = w2s[:, ds(c, 1), :, :, :].rearrange("p o k a c -> p (o k a c)")
                    src = bk0[:, :].bitcast(F16)[:, 0:CH * 2 * C]
                v.tensor_copy(dst, src).then_inc(w_stored, 1)

            def iteration(a=None, b=None, c=None, d=None):
                count.update(dict.fromkeys(STEPS, 0))
                run(a, channel_statistics)
                run(b, normalise0)
                run(d, centre_logits)
                run(a, channel_variances)
                run(c, variance_c, 2, sq2_ready)
                run(d, picks, 0)
                run(c, normalise2)
                run(b, buckets)
                run(c, low_n2)
                run(a, pair_statistics)
                run(b, bucket_means)
                run(b, store_pooled)
                run(d, picks, 1)
                run(a, row_sums)
                run(d, row_places)
                run(b, key_value_blocks)
                run(c, largest_weight)
                run(b, centre_scores, 0)
                run(b, centre_scores, 1)
                run(c, weight_scales)
                run(a, centre1)
                run(c, low_weights)
                run(c, centre3)
                run(b, centre_scores, 2)
                run(a, variance1)
                run(b, attended, 0)
                run(c, variance_c, 3, sq3_ready)
                run(b, centre_scores, 3)
                run(c, normalise3)
                run(c, low_wtok)
                run(a, normalise1)
                run(b, attended, 1)
                run(c, store_weights, 2)
                run(b, centre2)
                run(c, store_weights, 3)
                groups = dict(a=a, b=b, c=c, d=d, w=c)
                assert all(groups[k] is None or count[k] == STEPS[k] for k in STEPS), count

            pipeline(dve, iteration)

            n = 0

            def step_done(ins):
                nonlocal n
                n += 1
                ins.then_inc(sched_step, 1)
                dve.wait_ge(sched_step, n)

            dve.wait_ge(w_stored, 4 * NG)
            dve.wait_ge(counted, 1)
            step_done(v.tensor_copy(cnt8[:, :], bk7[:, 0:NE]))
            nk = T // MT
            step_done(tt(over[:, :, :], wide(cnt8[:, :], nk), k_rows[:, :].unsqueeze(1).broadcast_to([P, NE, nk]),
                         ALU.is_gt))
            step_done(v.tensor_reduce(tiles[:, :], over[:, :, :], AX.X, ALU.add))
            tt(pad_row[:, :], cnt8[:, :], region[:, :, 0], ALU.add)
            v.tensor_scalar(adjust[:, :], tiles[:, :], -float(MT), float(REG), ALU.mult, ALU.add)
            step_done(v.tensor_tensor_scan(tiles_end[:, :], ones[:, 0:NE], tiles[:, :], 0.0, ALU.mult, ALU.add))
            step_done(tt(past[:, :, :], wide(g_no[:, :], NE), tiles_end[:, :].unsqueeze(1).broadcast_to([P, NS, NE]),
                         ALU.is_ge))
            step_done(v.tensor_reduce(n_past[:, :], past[:, :, :], AX.X, ALU.add))
            v.tensor_scalar(tile_expert_f[:, :], n_past[:, :], float(NE - 1), None, ALU.min)
            step_done(tt(past_a[:, :, :], past[:, :, :], adjust[:, :].unsqueeze(1).broadcast_to([P, NS, NE]),
                         ALU.mult))
            step_done(v.tensor_reduce(a_past[:, :], past_a[:, :, :], AX.X, ALU.add))
            step_done(tt(a_past[:, :], a_past[:, :], g_row[:, :], ALU.add))
            v.tensor_scalar(tile_row[:, :], a_past[:, :], float(NE * REG), None, ALU.min).then_inc(sched_ready, 1)
            dve.wait_ge(sched_ready, 1)
            step_done(v.tensor_copy(packed[:, 0, 0:NS], tile_expert_f[0:1, :]))
            for m in range(1, WINDOW):
                step_done(v.scalar_tensor_tensor(
                    out=packed[:, m % 2, 0:NS], in0=packed[:, (m - 1) % 2, 1:NS + 1],
                    scalar=float(1 << EXPERT_BITS), in1=tile_expert_f[0:1, :], op0=ALU.mult, op1=ALU.add))
            v.tensor_copy(window_experts[:, :], packed[:, (WINDOW - 1) % 2, 0:NS]).then_inc(experts_packed, 1)
            step_done(tt(past[:, :, :], wide(tile_expert_f[:, :], NE),
                         e_no[:, :].unsqueeze(1).broadcast_to([P, NS, NE]), ALU.is_equal))
            for w in range(3):
                back = wback[:, :, w].unsqueeze(1).broadcast_to([P, NS, NE])
                step_done(tt(past_a[:, :, :], past[:, :, :], back, ALU.mult))
                step_done(v.tensor_reduce(tile_back[:, :, w], past_a[:, :, :], AX.X, ALU.add))
            v.tensor_copy(cnt[:, :], ones[:, 0:1]).then_inc(sched_ready, 1)

            def low_units(t, b, q):
                dve.wait_ge(h_hi_ready, 3 * t + q + 1)
                tt(hparts[:, b, 2 * q:2 * q + 2, 1, :], units[q].rearrange("p (k n) -> p k n", k=2),
                   hparts[:, b, 2 * q:2 * q + 2, 0, :], ALU.subtract).then_inc(h_lo_dve, 1)

            def gated(t, b, q):
                factor = tile_back[:, ds(t, 1), 1:2].rearrange("p o n -> p (o n)")
                m = (3 * b + q) % 2
                dve.wait_ge(silu_ready, 3 * t + q + 1)
                dve.wait_ge(h3_ready, 3 * t + q + 1)
                wait(dve, *((h_lo_pool, t), (h_lo_dve, 2 * t - 1), (h_lo_dve, 2 * t))[q])
                v.scalar_tensor_tensor(out=units[q], in0=bk34[:, m, :], scalar=factor, in1=silu[:, m, :],
                                       op0=ALU.mult, op1=ALU.mult).then_inc(h_ready, 1)

            def gate_out(t, b, nth):
                factor = tile_back[:, ds(t, 1), 2:3].rearrange("p o n -> p (o n)")
                y_high = bk56[:, b, 0:4 * C].rearrange("p (h a c) -> p h a c", h=2, a=2)[:, :, 0, :]
                row_route = route[:, ds(t, 1), :, :].rearrange("p o h w -> p (o h) w")
                dve.wait_ge(ylow_ready, t + 1)
                dve.wait_ge(route_ready, t + 1)
                wait(dve, y_scattered[b], 32 * nth)
                dve.sem_inc(waited, 1)
                v.tensor_copy(dest[:, b, :], row_route[:, :, 1])
                v.scalar_tensor_tensor(out=ylow[:, b, :, :], in0=y_high, scalar=factor, in1=ylow[:, b, :, :],
                                       op0=ALU.mult, op1=ALU.add).then_inc(ysum_ready, 1)
                dve.wait_ge(ysum_ready, t + 1)
                tt(yout[:, b, :, :], ylow[:, b, :, :], wide(row_route[:, :, 0], C), ALU.mult)\
                    .then_inc(yout_ready[b], 1)

            def one_tile(t, b, nth):
                first = isinstance(t, int) and t < 1
                if not first:
                    low_units(t - 1, 1 - b, 2)
                gated(t, b, 0)
                if not (isinstance(t, int) and t < 2):
                    gate_out(t - 2, b, nth)
                gated(t, b, 1)
                gated(t, b, 2)
                low_units(t, b, 1)

            def two_tiles(k):
                one_tile(2 * k + 1, 1, k - 1)
                one_tile(2 * k + 2, 0, k)

            one_tile(0, 0, 0)
            first_then_loop(dve, (NT - 1) // 2, two_tiles, first=2, unrolled=UNROLLED)
            low_units(NT - 1, 0, 2)
            gate_out(NT - 2, 1, (NT - 2) // 2)
            gate_out(NT - 1, 0, (NT - 1) // 2)

            def add_results(k):
                for b in range(2):
                    dve.wait_ge(res_loaded[b], 32 * (k + 1))
                    wait(dve, o_turned[b], k)
                    tt(t3[:, b, :, :], res[:, b, 0, :, :], res[:, b, 1, :, :], ALU.add).then_inc(t3_sum, 1)
                    dve.wait_ge(t3_sum, 2 * k + b + 1)
                    tt(t3[:, b, :, :].rearrange("p j c -> p (j c)"), t3[:, b, :, :].rearrange("p j c -> p (j c)"),
                       t2_all[:, ds(2 * k + b, 1), :, :].rearrange("p o j c -> p (o j c)"), ALU.add)\
                        .then_inc(t3_ready, 1)

            first_then_loop(dve, NG // 2, add_results)


DVE_SETUP = 14
STEPS = dict(a=7, b=14, c=3, d=21, w=4)


def wait(engine, semaphore, value):
    if not isinstance(value, int) or value > 0:
        engine.wait_ge(semaphore, value)


def run(group, step, *args):
    if group is not None:
        step(group, *args)


def pipeline(engine, iteration):
    iteration(a=0)
    iteration(a=1, b=0)
    iteration(a=2, b=1, c=0)
    with engine.Fori(0, NG - 3) as i:
        iteration(a=i + 3, b=i + 2, c=i + 1, d=i)
    iteration(b=NG - 1, c=NG - 2, d=NG - 3)
    iteration(c=NG - 1, d=NG - 2)
    iteration(d=NG - 1)


def first_then_loop(engine, n, body, first=1, unrolled=1):
    for k in range(first):
        body(k)
    assert (n - first) % unrolled == 0
    with engine.Fori(0, (n - first) // unrolled) as k:
        carried = ()
        for m in range(first, first + unrolled):
            said = body(k * unrolled + m, *carried)
            carried = () if said is None else (said,)


def kernel(**inputs):
    import numpy as np
    import concourse.bacc as bacc
    from concourse.bass_utils import run_bass_kernel_spmd

    names = ["x", "L0_conv_bias", "L1_attn_rotations", "L1_attn_norm1_g", "L1_attn_norm1_b", "L1_attn_q_w",
             "L1_attn_kv_w", "L1_attn_norm2_g", "L1_attn_norm2_b", "L1_attn_fc1_w", "L1_attn_fc1_b",
             "L1_attn_fc2_w", "L1_attn_fc2_b", "L1_ffn_router_w", "L1_ffn_w1", "L1_ffn_w2", "L1_ffn_w3"]
    nc = bacc.Bacc("TRN2", target_bir_lowering=False, num_devices=1)
    arrays, args = {}, []
    for name in names:
        a = np.ascontiguousarray(inputs[name])
        arrays[f"in_{name}"] = a
        args.append(nc.dram_tensor(f"in_{name}", a.shape, mybir.dt.from_np(a.dtype), kind="ExternalInput").ap())
    out = nc.dram_tensor("out_0", (B, C, HH, WW), F32, kind="ExternalOutput").ap()
    hybrid_block(nc, *args, out)
    r = run_bass_kernel_spmd(nc, [arrays], core_ids=[0])
    return r.results[0]["out_0"]
```
